# Optimizing a Trainium2 kernel written in Bass

```python
import numpy as np
import jax
import jax.numpy as jnp

def _softmax(x, axis=-1):
    return jax.nn.softmax(x, axis=axis)

def _gelu(x):
    return jax.nn.gelu(x, approximate=True)

def _silu(x):
    return jax.nn.silu(x)

def _sigmoid(x):
    return jax.nn.sigmoid(x)

def _layernorm(x, axis=-1, eps=1e-05):
    m = jnp.mean(x, axis=axis, keepdims=True)
    v = jnp.var(x, axis=axis, keepdims=True)
    return (x - m) / jnp.sqrt(v + eps)

def _scatter_add(tgt, idx, src, axis=0):
    return tgt.at[idx].add(src)

def _segment_sum(src, seg, n):
    return jax.ops.segment_sum(src, seg, n)
kernel_name = 'mk_decoder_preln_d2_seqx_r4_d6858f'

def setup_inputs(seed: int=0):
    np.random.seed(seed)
    _w = jnp.asarray

    def _rec_inputs():
        import jax
        import jax.numpy as jnp
        _rk = jax.random.key(seed)
        x = -0.0002928 + 1 * jax.random.normal(jax.random.fold_in(_rk, 1), (2, 1024, 256), jnp.float32)
        _lenS = 1024 - jax.random.randint(jax.random.fold_in(_rk, 7), (2,), 0, max(1, 1024 // 4) + 1, jnp.int32)
        _lenS2 = 64 - jax.random.randint(jax.random.fold_in(_rk, 8), (2,), 0, max(1, 64 // 4) + 1, jnp.int32)
        _ctx_1024P = jax.random.normal(jax.random.fold_in(_rk, 11), (2, 16, 256), jnp.float32)
        _ctx_1024c = jax.random.dirichlet(jax.random.fold_in(_rk, 511), 0.3 * jnp.ones((16,), jnp.float32), (2, 64))
        _ctx_1024t = jnp.einsum('bsk,bkd->bsd', _ctx_1024c, _ctx_1024P)
        _ctx_1024t = _ctx_1024t * jax.lax.rsqrt(jnp.mean(jnp.square(_ctx_1024t)) + 1e-12) * 0.953939
        ctx_1024 = -1.39393e-06 + 0.999914 * (_ctx_1024t + 0.3 * jax.random.normal(jax.random.fold_in(_rk, 611), (2, 64, 256), jnp.float32))
        _validS = jnp.arange(1024)[None, :] < _lenS[:, None]
        _validS2 = jnp.arange(64)[None, :] < _lenS2[:, None]
        _causal = jnp.tril(jnp.ones((1024, 1024), dtype=bool))
        mask_Bx1x1xS2_ff0 = jnp.where(jnp.ones((2, 1, 1, 64), dtype=bool), 0.0, -1000000000.0).astype(jnp.float32)
        return (x, ctx_1024, mask_Bx1x1xS2_ff0)
    x, ctx_1024, mask_Bx1x1xS2_ff0 = _rec_inputs()

    def _L0_attn_setup():
        import jax, jax.numpy as jnp
        import numpy as np
        DM = 256
        E = 512
        NS = 16
        R = 64
        K = 4
        BB, LL = (4, 256)
        EPS = 1e-05

        def rmsnorm(x, w):
            x = x.astype(jnp.float32)
            return x * jax.lax.rsqrt(jnp.mean(x * x, axis=-1, keepdims=True) + EPS) * w

        def causal_conv(x, w, b):
            xp = jnp.pad(x, ((0, 0), (K - 1, 0), (0, 0)))
            L = x.shape[1]
            y = sum((w[:, k] * xp[:, k:k + L, :] for k in range(K)))
            return y + b

        def ssm_scan(dt, Bm, Cm, x, A):

            def step(h, inp):
                dt_t, B_t, C_t, x_t = inp
                dA = jnp.exp(dt_t[..., None] * A)
                h = dA * h + (dt_t * x_t)[..., None] * B_t[:, None, :]
                y = jnp.einsum('ben,bn->be', h, C_t)
                return (h, y)
            h0 = jnp.zeros((dt.shape[0], A.shape[0], A.shape[1]), dt.dtype)
            xs = (dt.transpose(1, 0, 2), Bm.transpose(1, 0, 2), Cm.transpose(1, 0, 2), x.transpose(1, 0, 2))
            _, ys = jax.lax.scan(step, h0, xs)
            return ys.transpose(1, 0, 2)

        def mamba(h, inproj, convw, convb, xproj, dtw, dtb, Alog, Dp, outproj):
            xz = jnp.einsum('bld,ed->ble', h, inproj)
            xc, z = jnp.split(xz, 2, axis=-1)
            xc = jax.nn.silu(causal_conv(xc, convw, convb))
            xdbl = jnp.einsum('ble,fe->blf', xc, xproj)
            dt = jax.nn.softplus(jnp.einsum('blr,er->ble', xdbl[..., :R], dtw) + dtb)
            Bm = xdbl[..., R:R + NS]
            Cm = xdbl[..., R + NS:]
            A = -jnp.exp(Alog)
            y = ssm_scan(dt, Bm, Cm, xc, A) + xc * Dp
            y = y * jax.nn.silu(z)
            return jnp.einsum('ble,de->bld', y, outproj)

        def one_direction(x, norm_w, mixer_params, normf):
            residual = x.astype(jnp.float32)
            hidden = mamba(rmsnorm(residual, norm_w), *mixer_params)
            return rmsnorm(hidden + residual, normf)
        key = jax.random.key(seed)
        ks = iter(jax.random.split(key, 40))

        def w(shape, fan):
            return jax.random.normal(next(ks), shape, jnp.float32) / np.sqrt(fan)
        inp = {'x': jax.random.normal(next(ks), (BB, LL, DM), jnp.float32)}
        for pre in ('fwd', 'bwd'):
            inp[pre + '_norm'] = 1.0 + 0.02 * jax.random.normal(next(ks), (DM,), jnp.float32)
            inp[pre + '_inproj'] = w((2 * E, DM), DM)
            inp[pre + '_convw'] = w((E, K), K)
            inp[pre + '_convb'] = jnp.zeros((E,), jnp.float32)
            inp[pre + '_xproj'] = w((R + 2 * NS, E), E)
            inp[pre + '_dtw'] = w((E, R), R)
            inp[pre + '_dtb'] = jnp.log(jnp.expm1(0.01 * jnp.ones((E,), jnp.float32)))
            inp[pre + '_Alog'] = jnp.log(jnp.broadcast_to(jnp.arange(1, NS + 1, dtype=jnp.float32), (E, NS)))
            inp[pre + '_Dp'] = jnp.ones((E,), jnp.float32)
            inp[pre + '_outproj'] = w((DM, E), E)
        inp['normf'] = 1.0 + 0.02 * jax.random.normal(next(ks), (DM,), jnp.float32)
        return inp
    _L0_attn_all = _L0_attn_setup()
    _L0_attn_in = {k: v for k, v in _L0_attn_all.items() if k in ('fwd_norm', 'fwd_inproj', 'fwd_convw', 'fwd_convb', 'fwd_xproj', 'fwd_dtw', 'fwd_dtb', 'fwd_Alog', 'fwd_Dp', 'fwd_outproj', 'bwd_norm', 'bwd_inproj', 'bwd_convw', 'bwd_convb', 'bwd_xproj', 'bwd_dtw', 'bwd_dtb', 'bwd_Alog', 'bwd_Dp', 'bwd_outproj', 'normf')}
    del _L0_attn_all

    def _L0_xattn_setup():
        import jax, jax.numpy as jnp
        import numpy as np
        EMBED_DIM = 256
        NUM_HEADS = 16
        HEAD_DIM = EMBED_DIM // NUM_HEADS
        key = jax.random.key(seed)
        ks = jax.random.split(key, 7)
        B, S, E = (2, 512, EMBED_DIM)
        scale = 1.0 / np.sqrt(E)
        return {'query': jax.random.normal(ks[0], (B, S, E), dtype=jnp.float32), 'key': jax.random.normal(ks[1], (B, S, E), dtype=jnp.float32), 'value': jax.random.normal(ks[2], (B, S, E), dtype=jnp.float32), 'Wq': jax.random.normal(ks[3], (E, E), dtype=jnp.float32) * scale, 'Wk': jax.random.normal(ks[4], (E, E), dtype=jnp.float32) * scale, 'Wv': jax.random.normal(ks[5], (E, E), dtype=jnp.float32) * scale, 'Wo': jax.random.normal(ks[6], (E, E), dtype=jnp.float32) * scale}
    _L0_xattn_all = _L0_xattn_setup()
    _L0_xattn_in = {k: v for k, v in _L0_xattn_all.items() if k in ('Wq', 'Wk', 'Wv', 'Wo')}
    del _L0_xattn_all

    def _L0_ffn_setup():
        import jax, jax.numpy as jnp
        import numpy as np
        H = 16
        TOP_K = 2
        EPS = 1e-05

        def _layer_norm(x, g, b):
            m = x.mean(-1, keepdims=True)
            v = ((x - m) ** 2).mean(-1, keepdims=True)
            return (x - m) * jax.lax.rsqrt(v + EPS) * g + b

        def _block(x, ln1_g, ln1_b, ln2_g, ln2_b, w_qkv, w_o, w_gate, w1, b1, w2, b2):
            B, S, D = x.shape
            hd = D // H
            h = _layer_norm(x, ln1_g, ln1_b)
            qkv = h @ w_qkv
            q, k, v = jnp.split(qkv, 3, axis=-1)
            q = q.reshape(B, S, H, hd)
            k = k.reshape(B, S, H, hd)
            v = v.reshape(B, S, H, hd)
            scores = jnp.einsum('bqhd,bkhd->bhqk', q, k) * hd ** (-0.5)
            causal = jnp.tril(jnp.ones((S, S), bool))
            scores = jnp.where(causal, scores, jnp.finfo(scores.dtype).min)
            attn = jax.nn.softmax(scores, axis=-1)
            o = jnp.einsum('bhqk,bkhd->bqhd', attn, v).reshape(B, S, D)
            x_resid = x + o @ w_o
            moe_in = _layer_norm(x_resid, ln2_g, ln2_b)
            N = B * S
            xf = moe_in.reshape(N, D)
            probs = jax.nn.softmax(xf @ w_gate, axis=-1)
            top_w, top_i = jax.lax.top_k(probs, TOP_K)
            top_w = top_w / top_w.sum(-1, keepdims=True)
            E = w1.shape[0]
            out = jnp.zeros_like(xf)
            for e in range(E):
                gate_e = jnp.sum(jnp.where(top_i == e, top_w, 0.0), axis=-1)
                he = jax.nn.gelu(xf @ w1[e] + b1[e])
                out = out + gate_e[:, None] * (he @ w2[e] + b2[e])
            return out.reshape(B, S, D) + x_resid
        key = jax.random.key(seed)
        ks = jax.random.split(key, 12)
        B, S, D, F, E = (8, 128, 256, 1024, 8)
        inp = {'x': jax.random.normal(ks[0], (B, S, D), jnp.float32), 'ln1_g': jnp.ones((D,), jnp.float32), 'ln1_b': jnp.zeros((D,), jnp.float32), 'ln2_g': jnp.ones((D,), jnp.float32), 'ln2_b': jnp.zeros((D,), jnp.float32), 'w_qkv': jax.random.normal(ks[1], (D, 3 * D), jnp.float32) * D ** (-0.5), 'w_o': jax.random.normal(ks[2], (D, D), jnp.float32) * D ** (-0.5), 'w_gate': jax.random.normal(ks[3], (D, E), jnp.float32) * D ** (-0.5), 'w1': jax.random.normal(ks[4], (E, D, F), jnp.float32) * D ** (-0.5), 'b1': jnp.zeros((E, F), jnp.float32), 'w2': jax.random.normal(ks[5], (E, F, D), jnp.float32) * F ** (-0.5), 'b2': jnp.zeros((E, D), jnp.float32)}
        return inp
    _L0_ffn_all = _L0_ffn_setup()
    _L0_ffn_in = {k: v for k, v in _L0_ffn_all.items() if k in ('ln1_g', 'ln1_b', 'ln2_g', 'ln2_b', 'w_qkv', 'w_o', 'w_gate', 'w1', 'b1', 'w2', 'b2')}
    del _L0_ffn_all

    def _L1_attn_setup():
        import jax, jax.numpy as jnp
        import numpy as np
        from jax import lax
        D_MODEL = 256
        D_STATE = 16
        D_CONV = 4
        EXPAND = 2
        D_INNER = EXPAND * D_MODEL
        DT_RANK = min(D_MODEL // 16, 64)
        EPS = 1e-05

        def _rmsnorm(x, w):
            var = jnp.mean(x * x, axis=-1, keepdims=True)
            return x * lax.rsqrt(var + EPS) * w

        def _selective_scan(u, delta, A, Bm, Cm, Dv):

            def step(h, inp):
                d_t, b_t, c_t, u_t = inp
                dA = jnp.exp(d_t[..., None] * A)
                dBu = d_t[..., None] * b_t[:, None, :] * u_t[..., None]
                h = dA * h + dBu
                y_t = jnp.einsum('bdn,bn->bd', h, c_t)
                return (h, y_t)
            xs = (jnp.swapaxes(delta, 0, 1), jnp.swapaxes(Bm, 0, 1), jnp.swapaxes(Cm, 0, 1), jnp.swapaxes(u, 0, 1))
            h0 = jnp.zeros((u.shape[0], D_INNER, D_STATE), u.dtype)
            _, ys = lax.scan(step, h0, xs)
            return jnp.swapaxes(ys, 0, 1) + u * Dv
        key = jax.random.key(seed)
        ks = jax.random.split(key, 8)

        def init(k, shape, s=0.02):
            return jax.random.normal(k, shape, jnp.float32) * s
        return {'x': jax.random.normal(ks[0], (8, 512, D_MODEL), jnp.float32), 'norm_w': jnp.ones((D_MODEL,), jnp.float32), 'in_proj_w': init(ks[1], (2 * D_INNER, D_MODEL)), 'conv_w': init(ks[2], (D_INNER, 1, D_CONV), 0.1), 'conv_b': jnp.zeros((D_INNER,), jnp.float32), 'x_proj_w': init(ks[3], (DT_RANK + 2 * D_STATE, D_INNER)), 'dt_proj_w': init(ks[4], (D_INNER, DT_RANK), 0.1), 'dt_proj_b': init(ks[5], (D_INNER,), 0.1), 'A_log': jnp.log(jnp.broadcast_to(jnp.arange(1, D_STATE + 1, dtype=jnp.float32), (D_INNER, D_STATE))), 'D': jnp.ones((D_INNER,), jnp.float32), 'out_proj_w': init(ks[6], (D_MODEL, D_INNER))}
    _L1_attn_all = _L1_attn_setup()
    _L1_attn_in = {k: v for k, v in _L1_attn_all.items() if k in ('norm_w', 'in_proj_w', 'conv_w', 'conv_b', 'x_proj_w', 'dt_proj_w', 'dt_proj_b', 'A_log', 'D', 'out_proj_w')}
    del _L1_attn_all

    def _L1_xattn_setup():
        import jax, jax.numpy as jnp
        import numpy as np
        B, S, D, H = (2, 512, 256, 16)
        HD = D // H
        key = jax.random.key(seed)
        ks = jax.random.split(key, 8)
        sc = 0.02
        return {'q': jax.random.normal(ks[0], (B, S, D), jnp.float32), 'k': jax.random.normal(ks[1], (B, S, D), jnp.float32), 'v': jax.random.normal(ks[2], (B, S, D), jnp.float32), 'padding_mask': jnp.zeros((B, 1, 1, S), jnp.float32), 'Wq': jax.random.normal(ks[3], (D, D), jnp.float32) * sc, 'bq': jnp.zeros((D,), jnp.float32), 'Wk': jax.random.normal(ks[4], (D, D), jnp.float32) * sc, 'bk': jnp.zeros((D,), jnp.float32), 'Wv': jax.random.normal(ks[5], (D, D), jnp.float32) * sc, 'bv': jnp.zeros((D,), jnp.float32), 'Wo': jax.random.normal(ks[6], (D, D), jnp.float32) * sc, 'bo': jnp.zeros((D,), jnp.float32)}
    _L1_xattn_all = _L1_xattn_setup()
    _L1_xattn_in = {k: v for k, v in _L1_xattn_all.items() if k in ('Wq', 'bq', 'Wk', 'bk', 'Wv', 'bv', 'Wo', 'bo')}
    del _L1_xattn_all

    def _L1_ffn_setup():
        import jax, jax.numpy as jnp
        import numpy as np
        B, S, DIM = (4, 1024, 256)
        BASE_COUPLING = 0.1
        NUM_CYCLES = 3

        def _gelu(x):
            return jax.nn.gelu(x, approximate=False)

        def _coupling_net(h, w1, b1, w2, b2, w3, b3, w4, b4):
            h = _gelu(h @ w1 + b1)
            h = _gelu(h @ w2 + b2)
            h = _gelu(h @ w3 + b3)
            return jax.nn.sigmoid(h @ w4 + b4)

        def _global_net(h, w1, b1, w2, b2, w3, b3):
            h = _gelu(h @ w1 + b1)
            h = _gelu(h @ w2 + b2)
            return jax.nn.sigmoid(h @ w3 + b3)

        def _twist(x):
            o_r, o_i, p_r, p_i = jnp.split(x, 4, axis=-1)
            return jnp.concatenate([p_r, -p_i, -o_r, o_i], axis=-1)
        key = jax.random.key(seed)
        ks = jax.random.split(key, 9)
        d = DIM

        def w(k, fan_in, fan_out):
            return jax.random.normal(k, (fan_in, fan_out), dtype=jnp.float32) / np.sqrt(fan_in).astype(np.float32)
        inp = {'x': jax.random.normal(ks[0], (B, S, d), dtype=jnp.float32)}
        cn_dims = [(d, d), (d, d // 2), (d // 2, d // 4), (d // 4, 1)]
        for i, (a, b) in enumerate(cn_dims):
            inp[f'cn_w{i + 1}'] = w(ks[1 + i], a, b)
            inp[f'cn_b{i + 1}'] = jnp.zeros((b,), dtype=jnp.float32)
        gc_dims = [(d, d // 2), (d // 2, d // 4), (d // 4, 1)]
        for i, (a, b) in enumerate(gc_dims):
            inp[f'gc_w{i + 1}'] = w(ks[5 + i], a, b)
            inp[f'gc_b{i + 1}'] = jnp.zeros((b,), dtype=jnp.float32)
        inp['adaptive_range'] = jnp.full((1,), 0.2, dtype=jnp.float32)
        return inp
    _L1_ffn_all = _L1_ffn_setup()
    _L1_ffn_in = {k: v for k, v in _L1_ffn_all.items() if k in ('cn_w1', 'cn_b1', 'cn_w2', 'cn_b2', 'cn_w3', 'cn_b3', 'cn_w4', 'cn_b4', 'gc_w1', 'gc_b1', 'gc_w2', 'gc_b2', 'gc_w3', 'gc_b3', 'adaptive_range')}
    del _L1_ffn_all
    return {'x': x, 'ctx_1024': ctx_1024, 'mask_Bx1x1xS2_ff0': mask_Bx1x1xS2_ff0, 'L0_attn_fwd_norm': _L0_attn_in['fwd_norm'], 'L0_attn_fwd_inproj': _L0_attn_in['fwd_inproj'], 'L0_attn_fwd_convw': _L0_attn_in['fwd_convw'], 'L0_attn_fwd_convb': _L0_attn_in['fwd_convb'], 'L0_attn_fwd_xproj': _L0_attn_in['fwd_xproj'], 'L0_attn_fwd_dtw': _L0_attn_in['fwd_dtw'], 'L0_attn_fwd_dtb': _L0_attn_in['fwd_dtb'], 'L0_attn_fwd_Alog': _L0_attn_in['fwd_Alog'], 'L0_attn_fwd_Dp': _L0_attn_in['fwd_Dp'], 'L0_attn_fwd_outproj': _L0_attn_in['fwd_outproj'], 'L0_attn_bwd_norm': _L0_attn_in['bwd_norm'], 'L0_attn_bwd_inproj': _L0_attn_in['bwd_inproj'], 'L0_attn_bwd_convw': _L0_attn_in['bwd_convw'], 'L0_attn_bwd_convb': _L0_attn_in['bwd_convb'], 'L0_attn_bwd_xproj': _L0_attn_in['bwd_xproj'], 'L0_attn_bwd_dtw': _L0_attn_in['bwd_dtw'], 'L0_attn_bwd_dtb': _L0_attn_in['bwd_dtb'], 'L0_attn_bwd_Alog': _L0_attn_in['bwd_Alog'], 'L0_attn_bwd_Dp': _L0_attn_in['bwd_Dp'], 'L0_attn_bwd_outproj': _L0_attn_in['bwd_outproj'], 'L0_attn_normf': _L0_attn_in['normf'], 'L0_xattn_Wq': _L0_xattn_in['Wq'], 'L0_xattn_Wk': _L0_xattn_in['Wk'], 'L0_xattn_Wv': _L0_xattn_in['Wv'], 'L0_xattn_Wo': _L0_xattn_in['Wo'], 'L0_ffn_ln1_g': _L0_ffn_in['ln1_g'], 'L0_ffn_ln1_b': _L0_ffn_in['ln1_b'], 'L0_ffn_ln2_g': _L0_ffn_in['ln2_g'], 'L0_ffn_ln2_b': _L0_ffn_in['ln2_b'], 'L0_ffn_w_qkv': _L0_ffn_in['w_qkv'], 'L0_ffn_w_o': _L0_ffn_in['w_o'], 'L0_ffn_w_gate': _L0_ffn_in['w_gate'], 'L0_ffn_w1': _L0_ffn_in['w1'], 'L0_ffn_b1': _L0_ffn_in['b1'], 'L0_ffn_w2': _L0_ffn_in['w2'], 'L0_ffn_b2': _L0_ffn_in['b2'], 'L1_attn_norm_w': _L1_attn_in['norm_w'], 'L1_attn_in_proj_w': _L1_attn_in['in_proj_w'], 'L1_attn_conv_w': _L1_attn_in['conv_w'], 'L1_attn_conv_b': _L1_attn_in['conv_b'], 'L1_attn_x_proj_w': _L1_attn_in['x_proj_w'], 'L1_attn_dt_proj_w': _L1_attn_in['dt_proj_w'], 'L1_attn_dt_proj_b': _L1_attn_in['dt_proj_b'], 'L1_attn_A_log': _L1_attn_in['A_log'], 'L1_attn_D': _L1_attn_in['D'], 'L1_attn_out_proj_w': _L1_attn_in['out_proj_w'], 'L1_xattn_Wq': _L1_xattn_in['Wq'], 'L1_xattn_bq': _L1_xattn_in['bq'], 'L1_xattn_Wk': _L1_xattn_in['Wk'], 'L1_xattn_bk': _L1_xattn_in['bk'], 'L1_xattn_Wv': _L1_xattn_in['Wv'], 'L1_xattn_bv': _L1_xattn_in['bv'], 'L1_xattn_Wo': _L1_xattn_in['Wo'], 'L1_xattn_bo': _L1_xattn_in['bo'], 'L1_ffn_cn_w1': _L1_ffn_in['cn_w1'], 'L1_ffn_cn_b1': _L1_ffn_in['cn_b1'], 'L1_ffn_cn_w2': _L1_ffn_in['cn_w2'], 'L1_ffn_cn_b2': _L1_ffn_in['cn_b2'], 'L1_ffn_cn_w3': _L1_ffn_in['cn_w3'], 'L1_ffn_cn_b3': _L1_ffn_in['cn_b3'], 'L1_ffn_cn_w4': _L1_ffn_in['cn_w4'], 'L1_ffn_cn_b4': _L1_ffn_in['cn_b4'], 'L1_ffn_gc_w1': _L1_ffn_in['gc_w1'], 'L1_ffn_gc_b1': _L1_ffn_in['gc_b1'], 'L1_ffn_gc_w2': _L1_ffn_in['gc_w2'], 'L1_ffn_gc_b2': _L1_ffn_in['gc_b2'], 'L1_ffn_gc_w3': _L1_ffn_in['gc_w3'], 'L1_ffn_gc_b3': _L1_ffn_in['gc_b3'], 'L1_ffn_adaptive_range': _L1_ffn_in['adaptive_range']}

def reference(x, ctx_1024, mask_Bx1x1xS2_ff0, L0_attn_fwd_norm, L0_attn_fwd_inproj, L0_attn_fwd_convw, L0_attn_fwd_convb, L0_attn_fwd_xproj, L0_attn_fwd_dtw, L0_attn_fwd_dtb, L0_attn_fwd_Alog, L0_attn_fwd_Dp, L0_attn_fwd_outproj, L0_attn_bwd_norm, L0_attn_bwd_inproj, L0_attn_bwd_convw, L0_attn_bwd_convb, L0_attn_bwd_xproj, L0_attn_bwd_dtw, L0_attn_bwd_dtb, L0_attn_bwd_Alog, L0_attn_bwd_Dp, L0_attn_bwd_outproj, L0_attn_normf, L0_xattn_Wq, L0_xattn_Wk, L0_xattn_Wv, L0_xattn_Wo, L0_ffn_ln1_g, L0_ffn_ln1_b, L0_ffn_ln2_g, L0_ffn_ln2_b, L0_ffn_w_qkv, L0_ffn_w_o, L0_ffn_w_gate, L0_ffn_w1, L0_ffn_b1, L0_ffn_w2, L0_ffn_b2, L1_attn_norm_w, L1_attn_in_proj_w, L1_attn_conv_w, L1_attn_conv_b, L1_attn_x_proj_w, L1_attn_dt_proj_w, L1_attn_dt_proj_b, L1_attn_A_log, L1_attn_D, L1_attn_out_proj_w, L1_xattn_Wq, L1_xattn_bq, L1_xattn_Wk, L1_xattn_bk, L1_xattn_Wv, L1_xattn_bv, L1_xattn_Wo, L1_xattn_bo, L1_ffn_cn_w1, L1_ffn_cn_b1, L1_ffn_cn_w2, L1_ffn_cn_b2, L1_ffn_cn_w3, L1_ffn_cn_b3, L1_ffn_cn_w4, L1_ffn_cn_b4, L1_ffn_gc_w1, L1_ffn_gc_b1, L1_ffn_gc_w2, L1_ffn_gc_b2, L1_ffn_gc_w3, L1_ffn_gc_b3, L1_ffn_adaptive_range):
    import jax
    import jax.numpy as jnp

    def _L0_attn_ref(x, fwd_norm, fwd_inproj, fwd_convw, fwd_convb, fwd_xproj, fwd_dtw, fwd_dtb, fwd_Alog, fwd_Dp, fwd_outproj, bwd_norm, bwd_inproj, bwd_convw, bwd_convb, bwd_xproj, bwd_dtw, bwd_dtb, bwd_Alog, bwd_Dp, bwd_outproj, normf):
        import jax, jax.numpy as jnp
        import numpy as np
        DM = 256
        E = 512
        NS = 16
        R = 64
        K = 4
        BB, LL = (4, 256)
        EPS = 1e-05

        def rmsnorm(x, w):
            x = x.astype(jnp.float32)
            return x * jax.lax.rsqrt(jnp.mean(x * x, axis=-1, keepdims=True) + EPS) * w

        def causal_conv(x, w, b):
            xp = jnp.pad(x, ((0, 0), (K - 1, 0), (0, 0)))
            L = x.shape[1]
            y = sum((w[:, k] * xp[:, k:k + L, :] for k in range(K)))
            return y + b

        def ssm_scan(dt, Bm, Cm, x, A):

            def step(h, inp):
                dt_t, B_t, C_t, x_t = inp
                dA = jnp.exp(dt_t[..., None] * A)
                h = dA * h + (dt_t * x_t)[..., None] * B_t[:, None, :]
                y = jnp.einsum('ben,bn->be', h, C_t)
                return (h, y)
            h0 = jnp.zeros((dt.shape[0], A.shape[0], A.shape[1]), dt.dtype)
            xs = (dt.transpose(1, 0, 2), Bm.transpose(1, 0, 2), Cm.transpose(1, 0, 2), x.transpose(1, 0, 2))
            _, ys = jax.lax.scan(step, h0, xs)
            return ys.transpose(1, 0, 2)

        def mamba(h, inproj, convw, convb, xproj, dtw, dtb, Alog, Dp, outproj):
            xz = jnp.einsum('bld,ed->ble', h, inproj)
            xc, z = jnp.split(xz, 2, axis=-1)
            xc = jax.nn.silu(causal_conv(xc, convw, convb))
            xdbl = jnp.einsum('ble,fe->blf', xc, xproj)
            dt = jax.nn.softplus(jnp.einsum('blr,er->ble', xdbl[..., :R], dtw) + dtb)
            Bm = xdbl[..., R:R + NS]
            Cm = xdbl[..., R + NS:]
            A = -jnp.exp(Alog)
            y = ssm_scan(dt, Bm, Cm, xc, A) + xc * Dp
            y = y * jax.nn.silu(z)
            return jnp.einsum('ble,de->bld', y, outproj)

        def one_direction(x, norm_w, mixer_params, normf):
            residual = x.astype(jnp.float32)
            hidden = mamba(rmsnorm(residual, norm_w), *mixer_params)
            return rmsnorm(hidden + residual, normf)
        fh = one_direction(x, fwd_norm, (fwd_inproj, fwd_convw, fwd_convb, fwd_xproj, fwd_dtw, fwd_dtb, fwd_Alog, fwd_Dp, fwd_outproj), normf)
        bh = one_direction(jnp.flip(x, 1), bwd_norm, (bwd_inproj, bwd_convw, bwd_convb, bwd_xproj, bwd_dtw, bwd_dtb, bwd_Alog, bwd_Dp, bwd_outproj), normf)
        return fh + jnp.flip(bh, 1)

    def _L0_xattn_ref(query, key, value, Wq, Wk, Wv, Wo):
        import jax, jax.numpy as jnp
        import numpy as np
        EMBED_DIM = 256
        NUM_HEADS = 16
        HEAD_DIM = EMBED_DIM // NUM_HEADS
        B, Sq, E = query.shape
        Sk = key.shape[1]
        H, D = (NUM_HEADS, HEAD_DIM)

        def split_heads(x, S):
            return x.reshape(B, S, H, D).transpose(0, 2, 1, 3)
        Q = split_heads(query @ Wq.T, Sq)
        K = split_heads(key @ Wk.T, Sk)
        V = split_heads(value @ Wv.T, Sk)
        scores = jnp.einsum('bhqd,bhkd->bhqk', Q, K) / jnp.sqrt(jnp.float32(D))
        causal = jnp.tril(jnp.ones((Sq, Sk), dtype=bool))
        scores = jnp.where(causal[None, None, :, :], scores, -jnp.inf)
        attn = jax.nn.softmax(scores, axis=-1)
        attn = jnp.nan_to_num(attn, nan=0.0)
        out = jnp.einsum('bhqk,bhkd->bhqd', attn, V)
        out = out.transpose(0, 2, 1, 3).reshape(B, Sq, E)
        return out @ Wo.T

    def _L0_ffn_ref(x, ln1_g, ln1_b, ln2_g, ln2_b, w_qkv, w_o, w_gate, w1, b1, w2, b2):
        import jax, jax.numpy as jnp
        import numpy as np
        H = 16
        TOP_K = 2
        EPS = 1e-05

        def _layer_norm(x, g, b):
            m = x.mean(-1, keepdims=True)
            v = ((x - m) ** 2).mean(-1, keepdims=True)
            return (x - m) * jax.lax.rsqrt(v + EPS) * g + b

        def _block(x, ln1_g, ln1_b, ln2_g, ln2_b, w_qkv, w_o, w_gate, w1, b1, w2, b2):
            B, S, D = x.shape
            hd = D // H
            h = _layer_norm(x, ln1_g, ln1_b)
            qkv = h @ w_qkv
            q, k, v = jnp.split(qkv, 3, axis=-1)
            q = q.reshape(B, S, H, hd)
            k = k.reshape(B, S, H, hd)
            v = v.reshape(B, S, H, hd)
            scores = jnp.einsum('bqhd,bkhd->bhqk', q, k) * hd ** (-0.5)
            causal = jnp.tril(jnp.ones((S, S), bool))
            scores = jnp.where(causal, scores, jnp.finfo(scores.dtype).min)
            attn = jax.nn.softmax(scores, axis=-1)
            o = jnp.einsum('bhqk,bkhd->bqhd', attn, v).reshape(B, S, D)
            x_resid = x + o @ w_o
            moe_in = _layer_norm(x_resid, ln2_g, ln2_b)
            N = B * S
            xf = moe_in.reshape(N, D)
            probs = jax.nn.softmax(xf @ w_gate, axis=-1)
            top_w, top_i = jax.lax.top_k(probs, TOP_K)
            top_w = top_w / top_w.sum(-1, keepdims=True)
            E = w1.shape[0]
            out = jnp.zeros_like(xf)
            for e in range(E):
                gate_e = jnp.sum(jnp.where(top_i == e, top_w, 0.0), axis=-1)
                he = jax.nn.gelu(xf @ w1[e] + b1[e])
                out = out + gate_e[:, None] * (he @ w2[e] + b2[e])
            return out.reshape(B, S, D) + x_resid
        return _block(x, ln1_g, ln1_b, ln2_g, ln2_b, w_qkv, w_o, w_gate, w1, b1, w2, b2)

    def _L1_attn_ref(x, norm_w, in_proj_w, conv_w, conv_b, x_proj_w, dt_proj_w, dt_proj_b, A_log, D, out_proj_w):
        import jax, jax.numpy as jnp
        import numpy as np
        from jax import lax
        D_MODEL = 256
        D_STATE = 16
        D_CONV = 4
        EXPAND = 2
        D_INNER = EXPAND * D_MODEL
        DT_RANK = min(D_MODEL // 16, 64)
        EPS = 1e-05

        def _rmsnorm(x, w):
            var = jnp.mean(x * x, axis=-1, keepdims=True)
            return x * lax.rsqrt(var + EPS) * w

        def _selective_scan(u, delta, A, Bm, Cm, Dv):

            def step(h, inp):
                d_t, b_t, c_t, u_t = inp
                dA = jnp.exp(d_t[..., None] * A)
                dBu = d_t[..., None] * b_t[:, None, :] * u_t[..., None]
                h = dA * h + dBu
                y_t = jnp.einsum('bdn,bn->bd', h, c_t)
                return (h, y_t)
            xs = (jnp.swapaxes(delta, 0, 1), jnp.swapaxes(Bm, 0, 1), jnp.swapaxes(Cm, 0, 1), jnp.swapaxes(u, 0, 1))
            h0 = jnp.zeros((u.shape[0], D_INNER, D_STATE), u.dtype)
            _, ys = lax.scan(step, h0, xs)
            return jnp.swapaxes(ys, 0, 1) + u * Dv
        residual = x
        xn = _rmsnorm(x, norm_w)
        xz = xn @ in_proj_w.T
        x_part, z = jnp.split(xz, 2, axis=-1)
        xc = lax.conv_general_dilated(jnp.swapaxes(x_part, 1, 2), conv_w, window_strides=(1,), padding=((D_CONV - 1, 0),), feature_group_count=D_INNER, dimension_numbers=('NCH', 'OIH', 'NCH'))
        xc = jnp.swapaxes(xc + conv_b[None, :, None], 1, 2)
        u = jax.nn.silu(xc)
        x_dbl = u @ x_proj_w.T
        dt, Bm, Cm = jnp.split(x_dbl, [DT_RANK, DT_RANK + D_STATE], axis=-1)
        delta = jax.nn.softplus(dt @ dt_proj_w.T + dt_proj_b)
        A = -jnp.exp(A_log)
        y = _selective_scan(u, delta, A, Bm, Cm, D)
        y = y * jax.nn.silu(z)
        out = y @ out_proj_w.T
        return out + residual

    def _L1_xattn_ref(q, k, v, padding_mask, Wq, bq, Wk, bk, Wv, bv, Wo, bo):
        import jax, jax.numpy as jnp
        import numpy as np
        B, S, D, H = (2, 512, 256, 16)
        HD = D // H
        b = q.shape[0]
        qh = (q @ Wq + bq).reshape(b, -1, H, HD)
        kh = (k @ Wk + bk).reshape(b, -1, H, HD)
        vh = (v @ Wv + bv).reshape(b, -1, H, HD)
        qk = jnp.einsum('bjhd,bkhd->bhjk', qh, kh) / jnp.sqrt(jnp.float32(HD))
        qk = qk + padding_mask * -1000000000000.0
        attn = jax.nn.softmax(qk, axis=-1)
        qkv = jnp.einsum('bhjk,bkhd->bjhd', attn, vh).reshape(b, -1, D)
        return qkv @ Wo + bo

    def _L1_ffn_ref(x, cn_w1, cn_b1, cn_w2, cn_b2, cn_w3, cn_b3, cn_w4, cn_b4, gc_w1, gc_b1, gc_w2, gc_b2, gc_w3, gc_b3, adaptive_range):
        import jax, jax.numpy as jnp
        import numpy as np
        B, S, DIM = (4, 1024, 256)
        BASE_COUPLING = 0.1
        NUM_CYCLES = 3

        def _gelu(x):
            return jax.nn.gelu(x, approximate=False)

        def _coupling_net(h, w1, b1, w2, b2, w3, b3, w4, b4):
            h = _gelu(h @ w1 + b1)
            h = _gelu(h @ w2 + b2)
            h = _gelu(h @ w3 + b3)
            return jax.nn.sigmoid(h @ w4 + b4)

        def _global_net(h, w1, b1, w2, b2, w3, b3):
            h = _gelu(h @ w1 + b1)
            h = _gelu(h @ w2 + b2)
            return jax.nn.sigmoid(h @ w3 + b3)

        def _twist(x):
            o_r, o_i, p_r, p_i = jnp.split(x, 4, axis=-1)
            return jnp.concatenate([p_r, -p_i, -o_r, o_i], axis=-1)
        global_context = x.mean(axis=1, keepdims=True)
        gf = _global_net(global_context, gc_w1, gc_b1, gc_w2, gc_b2, gc_w3, gc_b3)
        out = x
        for _ in range(NUM_CYCLES):
            tf = _coupling_net(out, cn_w1, cn_b1, cn_w2, cn_b2, cn_w3, cn_b3, cn_w4, cn_b4)
            combined = 0.7 * gf + 0.3 * tf
            coupling = BASE_COUPLING + adaptive_range * (combined - 0.5) * 2.0
            out = out + coupling * _twist(out)
        return out
    x = x + _L0_attn_ref(_layernorm(x, axis=-1), L0_attn_fwd_norm, L0_attn_fwd_inproj, L0_attn_fwd_convw, L0_attn_fwd_convb, L0_attn_fwd_xproj, L0_attn_fwd_dtw, L0_attn_fwd_dtb, L0_attn_fwd_Alog, L0_attn_fwd_Dp, L0_attn_fwd_outproj, L0_attn_bwd_norm, L0_attn_bwd_inproj, L0_attn_bwd_convw, L0_attn_bwd_convb, L0_attn_bwd_xproj, L0_attn_bwd_dtw, L0_attn_bwd_dtb, L0_attn_bwd_Alog, L0_attn_bwd_Dp, L0_attn_bwd_outproj, L0_attn_normf)
    x = x + _L0_xattn_ref(_layernorm(x, axis=-1), ctx_1024, ctx_1024, L0_xattn_Wq, L0_xattn_Wk, L0_xattn_Wv, L0_xattn_Wo)
    x = x + _L0_ffn_ref(_layernorm(x, axis=-1), L0_ffn_ln1_g, L0_ffn_ln1_b, L0_ffn_ln2_g, L0_ffn_ln2_b, L0_ffn_w_qkv, L0_ffn_w_o, L0_ffn_w_gate, L0_ffn_w1, L0_ffn_b1, L0_ffn_w2, L0_ffn_b2)
    x = x + _L1_attn_ref(_layernorm(x, axis=-1), L1_attn_norm_w, L1_attn_in_proj_w, L1_attn_conv_w, L1_attn_conv_b, L1_attn_x_proj_w, L1_attn_dt_proj_w, L1_attn_dt_proj_b, L1_attn_A_log, L1_attn_D, L1_attn_out_proj_w)
    x = x + _L1_xattn_ref(_layernorm(x, axis=-1), ctx_1024, ctx_1024, mask_Bx1x1xS2_ff0, L1_xattn_Wq, L1_xattn_bq, L1_xattn_Wk, L1_xattn_bk, L1_xattn_Wv, L1_xattn_bv, L1_xattn_Wo, L1_xattn_bo)
    x = x + _L1_ffn_ref(_layernorm(x, axis=-1), L1_ffn_cn_w1, L1_ffn_cn_b1, L1_ffn_cn_w2, L1_ffn_cn_b2, L1_ffn_cn_w3, L1_ffn_cn_b3, L1_ffn_cn_w4, L1_ffn_cn_b4, L1_ffn_gc_w1, L1_ffn_gc_b1, L1_ffn_gc_w2, L1_ffn_gc_b2, L1_ffn_gc_w3, L1_ffn_gc_b3, L1_ffn_adaptive_range)
    return x

_drawn_inputs = setup_inputs


def setup_inputs(seed=0):
    import zlib

    import numpy as np

    out = dict(_drawn_inputs(seed))
    spreads = {'L0_attn_fwd_convb': (0.0, 0.1),
     'L0_attn_fwd_dtb': (-4.600166320800781, 0.2),
     'L0_attn_fwd_Dp': (1.0, 0.2),
     'L0_attn_bwd_convb': (0.0, 0.1),
     'L0_attn_bwd_dtb': (-4.600166320800781, 0.2),
     'L0_attn_bwd_Dp': (1.0, 0.2),
     'L0_ffn_ln1_g': (1.0, 0.2),
     'L0_ffn_ln1_b': (0.0, 0.1),
     'L0_ffn_ln2_g': (1.0, 0.2),
     'L0_ffn_ln2_b': (0.0, 0.1),
     'L0_ffn_b1': (0.0, 0.1),
     'L0_ffn_b2': (0.0, 0.1),
     'L1_attn_norm_w': (1.0, 0.2),
     'L1_attn_conv_b': (0.0, 0.1),
     'L1_attn_D': (1.0, 0.2),
     'L1_xattn_bq': (0.0, 0.1),
     'L1_xattn_bk': (0.0, 0.1),
     'L1_xattn_bv': (0.0, 0.1),
     'L1_xattn_bo': (0.0, 0.1),
     'L1_ffn_cn_b1': (0.0, 0.1),
     'L1_ffn_cn_b2': (0.0, 0.1),
     'L1_ffn_cn_b3': (0.0, 0.1),
     'L1_ffn_gc_b1': (0.0, 0.1),
     'L1_ffn_gc_b2': (0.0, 0.1)}
    factors = {}
    for name, (base, spread) in spreads.items():
        noise = np.random.default_rng([zlib.crc32(name.encode()), seed]).standard_normal(out[name].shape)
        drawn = base * np.exp(spread * noise) if base else spread * noise
        out[name] = jnp.asarray(drawn.astype(out[name].dtype))
    for name, factor in factors.items():
        out[name] = (out[name] * factor).astype(out[name].dtype)
    return out
```

```python
from contextlib import ExitStack

import concourse.bass as bass
from concourse import mybir

F32 = mybir.dt.float32
BF16 = mybir.dt.bfloat16
ACT = mybir.ActivationFunctionType
ALU = mybir.AluOpType
AX = mybir.AxisListType

P = 128
B, S, D = 2, 1024, 256
T = B * S
KD = D // P
CH = 512
NCH = T // CH
BCH = S // CH
EI = 512
EB = EI // P
NS = 16
TAPS = 4
XD = 96
BC0 = 64
EPS = 1e-5


class Core:

    def __init__(self, nc, ctx, dram):
        self.nc, self.ctx, self.dram = nc, ctx, dram
        self.n = 0
        self.cleared = []

    def scope(self):
        return Scope(self)


class Scope:

    def __init__(self, core):
        self.core, self.stack = core, ExitStack()
        self.sems, self.ends = [], False

    def __enter__(self):
        self.stack.__enter__()
        self.core.n += 1
        self.tag = f"s{self.core.n}_"
        return self

    def __exit__(self, *what):
        self.stack.__exit__(*what)
        core = self.core
        if self.ends:
            for sem in core.cleared:
                core.nc.release_semaphore(sem)
            core.cleared = []
        for sem in self.sems:
            core.nc.gpsimd.sem_clear(sem)
        core.cleared += self.sems

    def sb(self, name, shape, dt=F32):
        return self.stack.enter_context(self.core.nc.sbuf_tensor(self.tag + name, shape, dt))

    def psum(self, name, shape, dt=F32):
        return self.stack.enter_context(self.core.nc.psum_tensor(self.tag + name, shape, dt))

    def sem(self, name):
        self.sems.append(self.core.nc.alloc_semaphore(self.tag + name))
        return self.sems[-1]

    def block(self):
        self.ends = True
        return self.stack.enter_context(self.core.nc.Block())


def tok(c, n=1):
    return bass.ds(c * CH, n * CH)


def start(core, x, consts):
    nc = core.nc
    with core.scope() as s:
        ident, ones, sel = consts["ident"], consts["ones"], consts["sel"]
        loaded, cleared, made = s.sem("loaded"), s.sem("cleared"), s.sem("made")
        block = s.block()

        @block.sync
        def _(sp):
            sp.dma_start(x[:], core.dram["xT"]).then_inc(loaded, 16)
            for key in ("norms", "head_mask", "pair_mask"):
                sp.dma_start(consts[key][:], core.dram[key]).then_inc(loaded, 16)
            sp.wait_ge(loaded, 4 * 16)

        @block.vector
        def _(dve):
            dve.memset(ones[:], 1.0 / D)
            dve.memset(consts["eps"][:], EPS)
            dve.memset(consts["one"][:], 1.0)
            dve.wait_ge(made, 1)
            dve.tensor_copy(consts["identb"][:], ident[:])

        @block.gpsimd
        def _(pool):
            pool.memset(ident[:], 0.0).then_inc(cleared, 1)
            pool.memset(sel[:], 0.0).then_inc(cleared, 1)
            pool.wait_ge(cleared, 2)
            pool.affine_select(out=ident[:], in_=ident[:], compare_op=ALU.not_equal, fill=1.0,
                               base=0, pattern=[[-1, P]], channel_multiplier=1).then_inc(made, 1)
            for part in range(3):
                pool.wait_ge(made, part + 1)
                v = sel[part * 32:(part + 1) * 32, :, :]
                pool.affine_select(out=v, in_=v, compare_op=ALU.not_equal, fill=1.0, base=0,
                                   pattern=[[-1, 32], [0, P]], channel_multiplier=1).then_inc(made, 1)
            pool.wait_ge(made, 4)


def norm(core, consts, src, dst, center, weight=None, bias=None, add_to=None):
    with core.scope() as s:
        psum = s.psum("stat", [P, 2 * NCH, CH])
        square = s.sb("square", [P, KD, T])
        rstd = s.sb("rstd", [P, T])
        mean_ready, centered, squared = s.sem("mean_ready"), s.sem("centered"), s.sem("squared")
        var_ready, log_ready, rstd_ready = s.sem("var_ready"), s.sem("log_ready"), s.sem("rstd_ready")
        scaled, done = s.sem("scaled"), s.sem("done")
        body = dst if center else src
        block = s.block()

        @block.tensor
        def _(pe):
            if center:
                with pe.Fori(0, NCH) as c:
                    for k in range(KD):
                        mm = pe.matmul(psum[:, c, :], consts["ones"][:], src[:, k, tok(c)],
                                       start=(k == 0), stop=(k == KD - 1))
                    mm.then_inc(mean_ready, 1)
            with pe.Fori(0, NCH) as c:
                pe.wait_ge(squared, c + 1)
                for k in range(KD):
                    mm = pe.matmul(psum[:, c + NCH, :], consts["ones"][:], square[:, k, tok(c)],
                                   start=(k == 0), stop=(k == KD - 1))
                mm.then_inc(var_ready, 1)

        @block.vector
        def _(dve):
            if center:
                with dve.Fori(0, NCH) as c:
                    dve.wait_ge(mean_ready, c + 1)
                    for k in range(KD):
                        last = dve.tensor_tensor(dst[:, k, tok(c)], src[:, k, tok(c)], psum[:, c, :],
                                                 ALU.subtract)
                    last.then_inc(centered, 1)
            with dve.Fori(0, NCH) as c:
                dve.wait_ge(rstd_ready, c + 1)
                for k in range(KD):
                    if weight is None:
                        last = dve.tensor_tensor(dst[:, k, tok(c)], body[:, k, tok(c)],
                                                 rstd[:, tok(c)], ALU.mult)
                    else:
                        last = dve.scalar_tensor_tensor(out=dst[:, k, tok(c)], in0=body[:, k, tok(c)],
                                                        scalar=weight[:, k:k + 1], in1=rstd[:, tok(c)],
                                                        op0=ALU.mult, op1=ALU.mult)
                last.then_inc(scaled, 1)
            if bias is not None:
                dve.wait_ge(scaled, NCH)
                for k in range(KD):
                    last = dve.tensor_scalar(dst[:, k, :], dst[:, k, :], bias[:, k:k + 1], None, ALU.add)
                last.then_inc(done, 1)
            if add_to is not None:
                dve.wait_ge(scaled, NCH)
                last = dve.tensor_tensor(add_to[:], add_to[:], dst[:], ALU.add).then_inc(done, 1)

        @block.scalar
        def _(act):
            with act.Fori(0, NCH) as c:
                if center:
                    act.wait_ge(centered, c + 1)
                act.activation(square[:, :, tok(c)], body[:, :, tok(c)], ACT.Square).then_inc(squared, 1)
            with act.Fori(0, NCH) as c:
                act.wait_ge(var_ready, c + 1)
                act.activation(rstd[:, tok(c)], psum[:, c + NCH, :], ACT.Ln,
                               bias=consts["eps"][:, 0:1]).then_inc(log_ready, 1)
            with act.Fori(0, NCH) as c:
                act.wait_ge(log_ready, c + 1)
                act.activation(rstd[:, tok(c)], rstd[:, tok(c)], ACT.Exp, scale=-0.5).then_inc(rstd_ready, 1)


def mamba(core, consts, name, xn, res, steps, flip, x_out=None):
    dram = core.dram
    with core.scope() as s:
        w_in = s.sb("w_in", [P, KD, 2 * EI])
        w_x = s.sb("w_x", [P, EB, XD])
        w_dt = s.sb("w_dt", [steps, EI])
        w_out = s.sb("w_out", [P, EB, D])
        w_conv = s.sb("w_conv", [P, EB, TAPS])
        cols = s.sb("cols", [P, 3, EB])
        a_log = s.sb("a_log", [P, EB * NS])
        a_neg = s.sb("a_neg", [P, EB * NS])
        gate = s.sb("gate", [P, EB, S])
        u = s.sb("u", [P, EB, S])
        pad = s.sb("pad", [P, EB, S + TAPS - 1])
        dt = pad[:, :, 0:S]
        dx = s.sb("dx", [P, EB, S])
        bc = s.sb("bc", [P, 2 * NS, CH])
        relu = bc[:, 0:8, :].rearrange("p (m c) t -> p m (c t)", m=EB)
        low = bc[0:steps, 8:10, :].rearrange("p c t -> p (c t)")
        parts = s.sb("parts", [96, S], BF16)
        rest = bc[0:32, 10, :]
        mid = bc[0:32, 11, :].bitcast(BF16)[:, 0:CH]
        state = s.sb("state", [P, EB * NS])
        dbu = w_in[:].rearrange("p k (h t) -> p (k h) t", t=CH)
        hc = s.sb("hc", [P, 2, CH])
        ysum = bc[:, 0, :]
        psum = s.psum("psum", [P, 8, CH])

        loaded, a_ready = s.sem("loaded"), s.sem("a_ready")
        one = consts["one"]

        for b in range(B):
            with core.scope() as q:
                x_free, z_free, proj_ready = q.sem("x_free"), q.sem("z_free"), q.sem("proj_ready")
                padded, conv_step, u_ready = q.sem("padded"), q.sem("conv_step"), q.sem("u_ready")
                xd_ready, xd_free, low_ready = q.sem("xd_ready"), q.sem("xd_free"), q.sem("low_ready")
                split_step, dtp_ready, dtp_free = q.sem("split_step"), q.sem("dtp_ready"), q.sem("dtp_free")
                exp_done, soft_done, dt_ready, dx_ready = (q.sem("exp_done"), q.sem("soft_done"),
                                                           q.sem("dt_ready"), q.sem("dx_ready"))
                turn = q.sem("turn")
                stage_ready, bc_ready = q.sem("stage_ready"), q.sem("bc_ready")
                decay_ready, dbu_ready = q.sem("decay_ready"), q.sem("dbu_ready")
                scanned, hc_ready, hc_used = q.sem("scanned"), q.sem("hc_ready"), q.sem("hc_used")
                saved = q.sem("saved")
                y_sum, y_ready = q.sem("y_sum"), q.sem("y_ready")
                out_ready, out_free, stored = q.sem("out_ready"), q.sem("out_free"), q.sem("stored")
                block = q.block()
                c0 = b * BCH

                def flipped(t, k, c):
                    if not flip:
                        return t[:, k, bass.ds((c0 + c) * CH, CH)]
                    return t[:, k, bass.ds((c0 + BCH - 1) * CH - c * CH, CH)][:, ::-1]

                @block.sync
                def _(sp):
                    if b:
                        sp.dma_start(w_in[:], dram[f"{name}_in"]).then_inc(loaded, 16)
                        return
                    for t, key in ((w_in, "in"), (w_x, "x"), (w_dt, "dt"), (w_out, "out"),
                                   (w_conv, "conv"), (cols, "cols"), (a_log, "alog")):
                        sp.dma_start(t[:], dram[f"{name}_{key}"]).then_inc(loaded, 16)

                N_W = (7 + b) * 16

                @block.tensor
                def _(pe):
                    for sem in (hc_used,):
                        pe.sem_inc(sem, 1)
                    pe.wait_ge(loaded, N_W)
                    for c in range(BCH):
                        for m in range(2 * EB):
                            free = x_free if m < EB else z_free
                            pe.wait_ge(free, c * EB + m % EB + 1)
                            for k in range(KD):
                                mm = pe.matmul(psum[:, m, :], w_in[:, k, m * P:(m + 1) * P],
                                               flipped(xn, k, c), start=(k == 0), stop=(k == KD - 1))
                            mm.then_inc(proj_ready, 1)
                    pe.wait_ge(u_ready, EB)
                    with pe.Fori(0, BCH) as c:
                        for k in range(EB):
                            mm = pe.matmul(psum[0:XD, c, :], w_x[:, k, :], u[:, k, tok(c)],
                                           start=(k == 0), stop=(k == EB - 1))
                        mm.then_inc(xd_ready, 1)
                    for c in range(BCH):
                        pe.wait_ge(low_ready, c + 1)
                        for m in range(EB):
                            pe.wait_ge(dtp_free, c * EB + m + 1)
                            pe.matmul(psum[:, 4 + m, :], w_dt[:, m * P:(m + 1) * P], low[:, c * CH:(c + 1) * CH],
                                      start=True, stop=True).then_inc(dtp_ready, 1)
                    pe.wait_ge(dt_ready, BCH * EB)
                    with pe.Fori(0, BCH) as c:
                        pe.wait_ge(split_step, c * 4 + 4)
                        for j in range(2 * NS):
                            pe.wait_ge(bc_ready, 1 + c * 2 * NS + max(j - 1, 0))
                            pe.matmul(psum[:, 6 + j % 2, :], consts["sel"][:, j, :], parts[:, tok(c)],
                                      start=True, stop=True).then_inc(stage_ready, 1)
                        with pe.Fori(0, EB) as e:
                            pe.wait_ge(y_ready, 1 + c * EB + e)
                            for n in range(NS):
                                pe.wait_ge(hc_ready, c * EB * NS + e * NS + n + 1)
                                pe.matmul(psum[:, 4, :], consts["ident"][:], hc[:, n % 2, :],
                                          start=(n == 0), stop=(n == NS - 1)).then_inc(hc_used, 1)
                    with pe.Fori(0, BCH) as c:
                        pe.wait_ge(y_ready, 1 + BCH * EB)
                        for m in range(KD):
                            pe.wait_ge(out_free, c * KD + m + 1)
                            for k in range(EB):
                                mm = pe.matmul(psum[:, 6 + m, :], w_out[:, k, m * P:(m + 1) * P],
                                               dx[:, k, tok(c)], start=(k == 0), stop=(k == EB - 1))
                            mm.then_inc(out_ready, 1)

                @block.vector
                def _(dve):
                    for sem in (y_ready, scanned):
                        dve.sem_inc(sem, 1)
                    dve.sem_inc(x_free, EB)
                    dve.sem_inc(out_free, KD)
                    dve.memset(pad[:, :, 0:TAPS - 1], 0.0).then_inc(padded, 1)
                    dve.memset(state[:], 0.0).then_inc(saved, 1)
                    if b == 0:
                        dve.wait_ge(loaded, N_W)
                        dve.wait_ge(a_ready, 1)
                        dve.tensor_scalar(a_neg[:], a_neg[:], -1.0, None, ALU.mult).then_inc(a_ready, 1)
                    with dve.Fori(0, BCH) as c:
                        for m in range(EB):
                            dve.wait_ge(proj_ready, c * 2 * EB + m + 1)
                            dve.tensor_copy(pad[:, m, bass.ds(c * CH + TAPS - 1, CH)],
                                            psum[:, m, :]).then_inc(x_free, 1)
                    dve.wait_ge(padded, 1)
                    dve.wait_ge(x_free, EB + BCH * EB)
                    for j in range(TAPS):
                        for m in range(EB):
                            if j == 0:
                                dve.tensor_scalar(dx[:, m, :], pad[:, m, 0:S], w_conv[:, m, 0:1], None,
                                                  ALU.mult).then_inc(conv_step, 1)
                            else:
                                dve.wait_ge(conv_step, (j - 1) * EB + m + 1)
                                dve.scalar_tensor_tensor(out=dx[:, m, :], in0=pad[:, m, j:j + S],
                                                         scalar=w_conv[:, m, j:j + 1], in1=dx[:, m, :],
                                                         op0=ALU.mult, op1=ALU.add).then_inc(conv_step, 1)
                    with dve.Fori(0, BCH) as c:
                        dve.wait_ge(xd_ready, c + 1)
                        dve.tensor_copy(low[:, tok(c)], psum[0:steps, c, :]).then_inc(low_ready, 1)
                        v = psum[BC0:XD, c, :]
                        dve.tensor_copy(parts[0:32, tok(c)], v).then_inc(split_step, 1)
                        dve.wait_ge(split_step, c * 4 + 1)
                        dve.tensor_tensor(rest, v, parts[0:32, tok(c)], ALU.subtract)\
                           .then_inc(split_step, 1)
                        dve.wait_ge(split_step, c * 4 + 2)
                        dve.tensor_copy(mid, rest).then_inc(split_step, 1)
                        dve.wait_ge(split_step, c * 4 + 3)
                        dve.tensor_copy(parts[32:64, tok(c)], mid)
                        dve.tensor_tensor(parts[64:96, tok(c)], rest, mid, ALU.subtract)\
                           .then_inc(split_step, 1)
                        dve.wait_ge(split_step, c * 4 + 4)
                    with dve.Fori(0, BCH) as c:
                        for m in range(EB):
                            dve.wait_ge(soft_done, c * EB + m + 1)
                            dve.tensor_tensor(dt[:, m, tok(c)], dt[:, m, tok(c)], relu[:, m, tok(c)],
                                              ALU.add).then_inc(dt_ready, 1)
                            dve.wait_ge(dt_ready, c * EB + m + 1)
                            dve.tensor_tensor(dx[:, m, tok(c)], dt[:, m, tok(c)], u[:, m, tok(c)],
                                              ALU.mult).then_inc(dx_ready, 1)
                    dve.wait_ge(saved, 1)
                    with dve.Fori(0, BCH) as c, dve.Fori(0, EB) as e:
                        i0 = c * (EB * NS) + e * NS

                        def weigh(n):
                            dve.wait_ge(scanned, 1 + i0 + n + 1)
                            dve.wait_ge(bc_ready, 1 + c * (2 * NS) + 2 * n + 2)
                            dve.wait_ge(hc_used, 1 + i0 + max(n - 1, 0))
                            dve.tensor_tensor(hc[:, n % 2, :], psum[:, 2 + n % 2, :], bc[:, 2 * n + 1, :],
                                              ALU.mult).then_inc(hc_ready, 1)
                            dve.tensor_copy(state[:, bass.ds(e * NS + n, 1)],
                                            psum[:, 2 + n % 2, CH - 1:CH]).then_inc(saved, 1)

                        for n in range(NS):
                            dve.wait_ge(decay_ready, i0 + n + 1)
                            dve.wait_ge(dbu_ready, 1 + i0 + n + 1)
                            if n >= 2:
                                dve.wait_ge(saved, i0 + n)
                            dve.tensor_tensor_scan(psum[:, 2 + n % 2, :], psum[:, n % 2, :],
                                                   dbu[:, n % 4, :], state[:, bass.ds(e * NS + n, 1)],
                                                   ALU.mult, ALU.add).then_inc(scanned, 1)
                            if n:
                                weigh(n - 1)
                        weigh(NS - 1)
                        dve.wait_ge(hc_used, 1 + i0 + NS)
                        dve.scalar_tensor_tensor(out=dx[:, e, tok(c)], in0=u[:, e, tok(c)],
                                                 scalar=cols[:, 2, bass.ds(e, 1)], in1=psum[:, 4, :],
                                                 op0=ALU.mult, op1=ALU.add).then_inc(y_sum, 1)
                        dve.wait_ge(y_sum, c * EB + e + 1)
                        dve.wait_ge(saved, i0 + NS + 1)
                        dve.tensor_tensor(dx[:, e, tok(c)], dx[:, e, tok(c)], gate[:, e, tok(c)], ALU.mult)\
                           .then_inc(y_ready, 1)
                    for c in range(BCH):
                        for m in range(KD):
                            dve.wait_ge(out_ready, c * KD + m + 1)
                            if x_out is None:
                                dve.tensor_tensor(flipped(xn, m, c), psum[:, 6 + m, :],
                                                  flipped(res, m, c), ALU.add).then_inc(out_free, 1)
                            else:
                                dve.tensor_tensor(ysum, psum[:, 6 + m, :], flipped(res, m, c),
                                                  ALU.add).then_inc(out_free, 1)
                                dve.wait_ge(out_free, KD + c * KD + m + 1)
                                dve.tensor_tensor(flipped(x_out, m, c), flipped(x_out, m, c), ysum,
                                                  ALU.add).then_inc(stored, 1)
                                dve.wait_ge(stored, c * KD + m + 1)

                @block.scalar
                def _(act):
                    for sem in (bc_ready,):
                        act.sem_inc(sem, 1)
                    act.sem_inc(z_free, EB)
                    act.sem_inc(dtp_free, EB)
                    act.wait_ge(loaded, N_W)
                    if b == 0:
                        act.activation(a_neg[:], a_log[:], ACT.Exp).then_inc(a_ready, 1)
                    with act.Fori(0, BCH) as c:
                        for m in range(EB):
                            act.wait_ge(proj_ready, c * 2 * EB + EB + m + 1)
                            act.activation(gate[:, m, tok(c)], psum[:, EB + m, :], ACT.Silu).then_inc(z_free, 1)
                    for m in range(EB):
                        act.wait_ge(conv_step, (TAPS - 1) * EB + m + 1)
                        act.activation(u[:, m, :], dx[:, m, :], ACT.Silu, bias=cols[:, 0, m:m + 1])\
                           .then_inc(u_ready, 1)
                    with act.Fori(0, BCH) as c:
                        for m in range(EB):
                            act.wait_ge(dtp_ready, c * EB + m + 1)
                            act.activation(dt[:, m, tok(c)], psum[:, 4 + m, :], ACT.Abs,
                                           bias=cols[:, 1, m:m + 1])
                            act.activation(relu[:, m, tok(c)], psum[:, 4 + m, :], ACT.Relu,
                                           bias=cols[:, 1, m:m + 1]).then_inc(dtp_free, 1)
                    act.wait_ge(dtp_free, EB + BCH * EB)
                    act.activation(dt, dt, ACT.Exp, scale=-1.0).then_inc(exp_done, 1)
                    act.wait_ge(exp_done, 1)
                    with act.Fori(0, BCH) as c:
                        for m in range(EB):
                            act.activation(dt[:, m, tok(c)], dt[:, m, tok(c)], ACT.Ln,
                                           bias=one[:, 0:1]).then_inc(soft_done, 1)
                    if b == 0:
                        act.wait_ge(a_ready, 2)
                    act.wait_ge(dt_ready, BCH * EB)
                    with act.Fori(0, BCH) as c:
                        for j in range(2 * NS):
                            used = hc_used if j % 2 else dbu_ready
                            act.wait_ge(used, 1 + c * ((EB - 1) * NS + j // 2 + 1))
                            act.wait_ge(stage_ready, c * 2 * NS + j + 1)
                            act.activation(bc[:, j, :], psum[:, 6 + j % 2, :], ACT.Copy).then_inc(bc_ready, 1)
                        with act.Fori(0, EB) as e:
                            i0 = c * (EB * NS) + e * NS
                            for n in range(NS):
                                act.wait_ge(scanned, 1 + i0 + max(n - 1, 0))
                                act.activation(psum[:, n % 2, :], dt[:, e, tok(c)], ACT.Exp,
                                               scale=a_neg[:, bass.ds(e * NS + n, 1)]).then_inc(decay_ready, 1)

                @block.gpsimd
                def _(pool):
                    for sem in (dbu_ready,):
                        pool.sem_inc(sem, 1)
                    pool.wait_ge(dx_ready, BCH * EB)
                    with pool.Fori(0, BCH) as c, pool.Fori(0, EB) as e:
                        i0 = c * (EB * NS) + e * NS
                        for n in range(NS):
                            pool.wait_ge(bc_ready, 1 + c * (2 * NS) + 2 * n + 1)
                            pool.wait_ge(scanned, 1 + i0 + max(n - 3, 0))
                            pool.sem_inc(turn, 1)
                            pool.tensor_tensor(dbu[:, n % 4, :], dx[:, e, tok(c)], bc[:, 2 * n, :],
                                               ALU.mult).then_inc(dbu_ready, 1)


H = 16
HD = D // H
SK = 64
QT = S // P
HB = P // HD
PAIRS = H // 2


def cross_attention(core, consts, name, h, x, causal):
    dram = core.dram
    with core.scope() as s:
        w = s.sb("w", [P, 4, KD, D])
        bias = s.sb("bias", [P, 3, KD])
        v_bias = s.sb("v_bias", [1, D])
        key_mask = s.sb("key_mask", [1, B, SK])
        ctx = s.sb("ctx", [P, KD, B, 2, SK])
        q = s.sb("q", [P, KD, T])
        o = s.sb("o", [P, KD, T])
        keys = s.sb("keys", [P, KD, B * SK])
        kd = s.sb("kd", [P, B, KD, HB, SK])
        vd = s.sb("vd", [P, B, PAIRS, 2 * HD + 2])
        neg4 = s.sb("neg4", [1, P])
        ones_row = s.sb("ones_row", [1, P])
        qs = s.sb("qs", [P, 2, KD, P])
        nmax = s.sb("nmax", [P, 2, H])
        shifted = s.sb("shifted", [P, 2, H * SK])
        probs = s.sb("probs", [P, 2, H * SK])
        probs_t = s.sb("probs_t", [P, 2, PAIRS, P])
        rden = s.sb("rden", [P, 2, PAIRS, 2])
        on = s.sb("on", [P, 2, D])
        late_f = shifted[:, 0, 0:QT * SK].rearrange("p (t s) -> p t s", t=QT)
        late = s.sb("late", [P, QT, SK], BF16)
        scores = s.psum("scores", [P, 2, 2, CH])
        turned = s.psum("turned", [P, PAIRS, P])
        mixed = s.psum("mixed", [P, CH])
        turned_o = s.psum("turned_o", [P, CH])
        banks = scores[:].rearrange("p u c t -> p (u c) t")

        loaded, made = s.sem("loaded"), s.sem("made")
        q_ready, q_free = s.sem("q_ready"), s.sem("q_free")
        k_ready, k_stored, kd_ready = s.sem("k_ready"), s.sem("k_stored"), s.sem("kd_ready")
        v_ready, vd_ready = s.sem("v_ready"), s.sem("vd_ready")
        qs_ready, scored, maxed, moved = s.sem("qs_ready"), s.sem("scored"), s.sem("maxed"), s.sem("moved")
        probs_ready, turned_ready, pt_ready = s.sem("probs_ready"), s.sem("turned_ready"), s.sem("pt_ready")
        mixed_ready, rden_ready, on_ready = s.sem("mixed_ready"), s.sem("rden_ready"), s.sem("on_ready")
        ot_ready, ot_stored = s.sem("ot_ready"), s.sem("ot_stored")
        out_ready, out_free, turn = s.sem("out_ready"), s.sem("out_free"), s.sem("turn")
        block = s.block()
        NT = B * QT
        N_LOAD = (5 + 2 * B) * 16

        @block.sync
        def _(sp):
            sp.dma_start(w[:], dram[name + "_w"]).then_inc(loaded, 16)
            sp.dma_start(bias[:], dram[name + "_bias"]).then_inc(loaded, 16)
            sp.dma_start(v_bias[:], dram[name + "_v_bias"]).then_inc(loaded, 16)
            sp.dma_start(key_mask[:], dram["key_mask"]).then_inc(loaded, 16)
            sp.dma_start(late_f, dram["late"]).then_inc(loaded, 16)
            for b in range(B):
                for copy in range(2):
                    sp.dma_start(ctx[:, :, b, copy, :], dram["ctxT"][:, :, b, :]).then_inc(loaded, 16)

        @block.tensor
        def _(pe):
            for sem in (scored,):
                pe.sem_inc(sem, 1)
            pe.wait_ge(loaded, N_LOAD)
            for m in range(KD):
                for k in range(KD):
                    mm = pe.matmul(turned[:, m, :], w[:, 1, k, m * P:(m + 1) * P], ctx[:, k, :, 0, :],
                                   start=(k == 0), stop=(k == KD - 1))
            mm.then_inc(k_ready, 1)
            pe.wait_ge(made, 2)
            for b in range(B):
                for k in range(KD):
                    pe.matmul(mixed[:, b * D:(b + 1) * D], ctx[:, k, b, :, :].rearrange("p c s -> p (c s)"),
                              w[:, 2, k, :], start=(k == 0), stop=False)
                mm = pe.matmul(mixed[:, b * D:(b + 1) * D], ones_row[:], v_bias[:], start=False, stop=True)
            mm.then_inc(v_ready, 1)
            with pe.Fori(0, NCH // 2) as c2:
                for j in range(2):
                    for m in range(KD):
                        pe.wait_ge(q_free, c2 * 4 + 2 * j + m + 1)
                        for k in range(KD):
                            mm = pe.matmul(banks[:, 2 * j + m, :], w[:, 0, k, m * P:(m + 1) * P],
                                           h[:, k, bass.ds(c2 * 2 * CH + j * CH, CH)],
                                           start=(k == 0), stop=(k == KD - 1))
                        mm.then_inc(q_ready, 1)
            pe.wait_ge(q_free, 4 + KD * NCH)
            pe.wait_ge(kd_ready, B * KD)
            pe.wait_ge(made, 3)
            pe.wait_ge(vd_ready, B)
            with pe.Fori(0, B) as b, pe.Fori(0, QT // 2) as t2:
                for u in range(2):
                    i = b * QT + t2 * 2 + u
                    pe.wait_ge(qs_ready, i + 1)
                    pe.wait_ge(moved, 1 + i - u)
                    for hb in range(KD):
                        pe.matmul(scores[:, u, hb, :], qs[:, u, hb, :], kd[:, b, hb, :, :],
                                  start=True, stop=False)
                        if causal:
                            mm = pe.matmul(scores[:, u, hb, :], consts["identb"][:],
                                           late[:, t2 * 2 + u, :].unsqueeze(1).to_broadcast([P, HB, SK]),
                                           start=False, stop=True)
                        else:
                            mm = pe.matmul(scores[:, u, hb, :], neg4[:],
                                           key_mask[:, b, :].unsqueeze(1).to_broadcast([1, HB, SK]),
                                           start=False, stop=True)
                    mm.then_inc(scored, 1)
                    pe.wait_ge(probs_ready, i + 1)
                    pe.wait_ge(pt_ready, 1 + i)
                    for j in range(PAIRS):
                        mm = pe.transpose(turned[:, j, :], probs[:, u, j * P:(j + 1) * P], consts["ident"][:])
                    mm.then_inc(turned_ready, 1)
                    pe.wait_ge(pt_ready, 1 + i + 1)
                    pe.wait_ge(on_ready, 1 + i)
                    for j in range(PAIRS):
                        mm = pe.matmul(mixed[:, j * (2 * HD + 2):(j + 1) * (2 * HD + 2)], probs_t[:, u, j, :],
                                       vd[:, b, j, :], start=True, stop=True)
                    mm.then_inc(mixed_ready, 1)
                    pe.wait_ge(on_ready, 1 + i + 1)
                    pe.wait_ge(ot_stored, 1 + i)
                    for k in range(KD):
                        mm = pe.transpose(turned_o[:, k * P:(k + 1) * P], on[:, u, k * P:(k + 1) * P],
                                          consts["ident"][:])
                    mm.then_inc(ot_ready, 1)
            pe.wait_ge(ot_stored, 1 + NT)
            with pe.Fori(0, NCH // 2) as c2:
                for j in range(2):
                    for m in range(KD):
                        pe.wait_ge(out_free, c2 * 4 + 2 * j + m + 1)
                        for k in range(KD):
                            mm = pe.matmul(banks[:, 2 * j + m, :], w[:, 3, k, m * P:(m + 1) * P],
                                           o[:, k, bass.ds(c2 * 2 * CH + j * CH, CH)],
                                           start=(k == 0), stop=(k == KD - 1))
                        mm.then_inc(out_ready, 1)

        @block.vector
        def _(dve):
            for sem in (moved, on_ready):
                dve.sem_inc(sem, 1)
            dve.memset(neg4[:], -4e12).then_inc(made, 1)
            dve.memset(ones_row[:], 1.0).then_inc(made, 1)
            dve.wait_ge(loaded, N_LOAD)
            dve.tensor_copy(late[:], late_f).then_inc(made, 1)
            dve.sem_inc(out_free, 4)
            dve.wait_ge(k_stored, KD)
            for b in range(B):
                for hb in range(KD):
                    dve.tensor_tensor(kd[:, b, hb, :, :],
                                      keys[:, hb, b * SK:(b + 1) * SK].unsqueeze(1).to_broadcast([P, HB, SK]),
                                      consts["head_mask"][:].unsqueeze(2).to_broadcast([P, HB, SK]),
                                      ALU.mult).then_inc(kd_ready, 1)
            dve.wait_ge(v_ready, 1)
            for b in range(B):
                dve.tensor_copy(vd[:, b, :, 2 * HD:2 * HD + 2],
                                consts["pair_mask"][:].unsqueeze(1).to_broadcast([P, PAIRS, 2]))
                for j in range(2):
                    last = dve.tensor_scalar(
                        vd[:, b, :, j * HD:(j + 1) * HD],
                        mixed[:, b * D:(b + 1) * D].rearrange("p (g j e) -> p g j e", j=2, e=HD)[:, :, j, :],
                        consts["pair_mask"][:, j:j + 1], None, ALU.mult)
                last.then_inc(vd_ready, 1)
            with dve.Fori(0, B) as b, dve.Fori(0, QT // 2) as t2:
                for u in range(2):
                    i = b * QT + t2 * 2 + u
                    sc = scores[:, u, :, :].rearrange("p c (h s) -> p (c h) s", s=SK)
                    dve.wait_ge(scored, 1 + i + 1)
                    dve.tensor_reduce(nmax[:, u, :], sc, AX.X, ALU.max, negate=True).then_inc(maxed, 1)
                    dve.wait_ge(maxed, i + 1)
                    dve.tensor_tensor(shifted[:, u, :].rearrange("p (h s) -> p h s", s=SK), sc,
                                      nmax[:, u, :].unsqueeze(2).to_broadcast([P, H, SK]),
                                      ALU.add).then_inc(moved, 1)
                    dve.wait_ge(mixed_ready, i + 1)
                    mx = mixed[:, 0:PAIRS * (2 * HD + 2)].rearrange("p (g e) -> p g e", g=PAIRS)
                    dve.reciprocal(rden[:, u, :, :], mx[:, :, 2 * HD:2 * HD + 2]).then_inc(rden_ready, 1)
                    dve.wait_ge(rden_ready, i + 1)
                    for j in range(2):
                        last = dve.tensor_tensor(
                            on[:, u, :].rearrange("p (g j e) -> p g j e", j=2, e=HD)[:, :, j, :],
                            mx[:, :, j * HD:(j + 1) * HD],
                            rden[:, u, :, j:j + 1].to_broadcast([P, PAIRS, HD]), ALU.mult)
                    last.then_inc(on_ready, 1)
            with dve.Fori(0, NCH // 2) as c2:
                for j in range(2):
                    for m in range(KD):
                        dve.wait_ge(out_ready, c2 * 4 + 2 * j + m + 1)
                        xs = x[:, m, bass.ds(c2 * 2 * CH + j * CH, CH)]
                        dve.scalar_tensor_tensor(out=xs, in0=banks[:, 2 * j + m, :], scalar=bias[:, 2, m:m + 1],
                                                 in1=xs, op0=ALU.add, op1=ALU.add).then_inc(out_free, 1)

        @block.scalar
        def _(act):
            for sem in (pt_ready, ot_stored):
                act.sem_inc(sem, 1)
            act.sem_inc(q_free, 4)
            act.wait_ge(k_ready, 1)
            for m in range(KD):
                act.activation(keys[:, m, :], turned[:, m, :], ACT.Identity, bias=bias[:, 1, m:m + 1])\
                   .then_inc(k_stored, 1)
            with act.Fori(0, NCH // 2) as c2:
                for j in range(2):
                    for m in range(KD):
                        act.wait_ge(q_ready, c2 * 4 + 2 * j + m + 1)
                        act.activation(q[:, m, bass.ds(c2 * 2 * CH + j * CH, CH)], banks[:, 2 * j + m, :],
                                       ACT.Identity, bias=bias[:, 0, m:m + 1]).then_inc(q_free, 1)
            with act.Fori(0, B) as b, act.Fori(0, QT // 2) as t2:
                for u in range(2):
                    i = b * QT + t2 * 2 + u
                    act.wait_ge(moved, 1 + i + 1)
                    act.activation(probs[:, u, :], shifted[:, u, :], ACT.Exp, scale=HD ** -0.5)\
                       .then_inc(probs_ready, 1)
                    act.wait_ge(turned_ready, i + 1)
                    act.activation(probs_t[:, u, :, :], turned[:], ACT.Copy).then_inc(pt_ready, 1)
                    act.wait_ge(ot_ready, i + 1)
                    act.activation(o[:, :, bass.ds(i * P, P)],
                                   turned_o[:, 0:KD * P].rearrange("p (k t) -> p k t", k=KD),
                                   ACT.Copy).then_inc(ot_stored, 1)

        @block.gpsimd
        def _(pool):
            pool.wait_ge(q_free, 4 + KD * NCH)
            with pool.Fori(0, B) as b, pool.Fori(0, QT // 2) as t2:
                for u in range(2):
                    i = b * QT + t2 * 2 + u
                    pool.wait_ge(scored, 1 + i - u)
                    pool.sem_inc(turn, 1)
                    pool.tensor_copy(qs[:, u, :, :], q[:, :, bass.ds(i * P, P)]).then_inc(qs_ready, 1)


NG = 4
GH = H // NG
E = 8
F = 1024
FB = F // P
VW = HD + 1


def self_attention(core, consts, h, res):
    dram = core.dram
    with core.scope() as s:
        w_qk = s.sb("w_qk", [P, 2, KD, NG * P])
        w_v = s.sb("w_v", [P, KD, D])
        w_o = s.sb("w_o", [P, KD, D])
        late = s.sb("late", [P, P])
        lateb = s.sb("lateb", [P, P], BF16)
        qk = s.sb("qk", [P, 2, NG, T])
        v = s.sb("v", [P, B * QT, H, VW])
        staged = s.sb("staged", [P, 2, S])
        nmax = s.sb("nmax", [P, GH * QT])
        probs = s.sb("probs", [P, 2, S])
        probs_t = s.sb("probs_t", [P, 2, S])
        rden = s.sb("rden", [P, GH, QT, 1])
        on = s.sb("on", [P, B * QT, H, HD])
        scores = s.psum("scores", [P, 2, 2 * CH])
        turned = s.psum("turned", [P, 2, CH])
        mixed = s.psum("mixed", [P, 2, CH])
        o = h

        loaded, ready, qk_free, v_ready, v_free = (s.sem("loaded"), s.sem("ready"), s.sem("qk_free"),
                                                   s.sem("v_ready"), s.sem("v_free"))
        staged_ready, scored, maxed, exp_done = (s.sem("staged_ready"), s.sem("scored"), s.sem("maxed"),
                                                 s.sem("exp_done"))
        turned_ready, low_copied, high_copied = s.sem("turned_ready"), s.sem("low_copied"), s.sem("high_copied")
        pv_done, rden_ready, normed = s.sem("pv_done"), s.sem("rden_ready"), s.sem("normed")
        ot_ready, ot_stored, out_ready, out_free = (s.sem("ot_ready"), s.sem("ot_stored"), s.sem("out_ready"),
                                                    s.sem("out_free"))
        made, turn = s.sem("made"), s.sem("turn")
        block = s.block()
        STEPS = GH * QT
        HIGH = GH * QT // 2
        psum8 = [scores[:, 0, 0:CH], scores[:, 0, CH:], scores[:, 1, 0:CH], scores[:, 1, CH:],
                 turned[:, 0, :], turned[:, 1, :]]

        @block.sync
        def _(sp):
            for t, key in ((w_qk, "a0_qk"), (w_v, "a0_v"), (w_o, "a0_o"), (late, "tri")):
                sp.dma_start(t[:], dram[key]).then_inc(loaded, 16)

        def high_before(i):
            return (i // QT) * (QT // 2) + max(i % QT - QT // 2, 0)

        @block.tensor
        def _(pe):
            for sem in (pv_done, turned_ready, scored):
                pe.sem_inc(sem, 1)
            pe.wait_ge(loaded, 4 * 16)
            with pe.Fori(0, NCH) as c:
                for which in range(2):
                    for g in range(NG):
                        pe.wait_ge(qk_free, c * 8 + which * NG + g + 1)
                        for k in range(KD):
                            mm = pe.matmul(psum8[g], w_qk[:, which, k, g * P:(g + 1) * P], h[:, k, tok(c)],
                                           start=(k == 0), stop=(k == KD - 1))
                        mm.then_inc(ready, 1)
            for t in range(B * QT):
                for k in range(KD):
                    mm = pe.matmul(mixed[:, t % 2, 0:D],
                                   h[:, k, t * P:(t + 1) * P], w_v[:, k, :], start=(k == 0), stop=(k == KD - 1))
                mm.then_inc(v_ready, 1)
                if t + 1 < B * QT and t >= 1:
                    pe.wait_ge(v_free, t)
            pe.wait_ge(v_free, B * QT)
            pe.wait_ge(qk_free, 4 + NCH * 8)
            pe.wait_ge(made, 2)
            with pe.Fori(0, B) as b, pe.Fori(0, NG) as g:
                it = b * NG + g

                def score(i):
                    j, qt = i // QT, i % QT
                    pe.wait_ge(exp_done, 1 + it * STEPS + max(i - 1, 0))
                    r = slice(32 * j, 32 * j + HD)
                    for c in range(qt // 4 + 1):
                        n = min((qt + 1) * P - c * CH, CH)
                        mm = pe.matmul(scores[:, i % 2, c * CH:c * CH + n], staged[r, 0, qt * P:(qt + 1) * P],
                                       staged[r, 1, c * CH:c * CH + n], start=True, stop=True)
                    mm = pe.matmul(scores[:, i % 2, qt * P:(qt + 1) * P], consts["identb"][:], lateb[:],
                                   start=False, stop=True, skip_group_check=True)
                    mm.then_inc(scored, 1)

                def turn_weights(i):
                    qt = i % QT
                    pe.wait_ge(exp_done, 1 + it * STEPS + i + 1)
                    pe.wait_ge(low_copied, 1 + it * STEPS + i)
                    for kt in range(qt + 1):
                        if kt == 4:
                            pe.wait_ge(high_copied, 1 + it * HIGH + high_before(i))
                        mm = pe.transpose(turned[:, kt // 4, kt % 4 * P:(kt % 4 + 1) * P],
                                          probs[:, i % 2, kt * P:(kt + 1) * P], consts["ident"][:])
                    mm.then_inc(turned_ready, 1)

                def mix(i):
                    j, qt = i // QT, i % QT
                    pe.wait_ge(low_copied, 1 + it * STEPS + i + 1)
                    if qt >= 4:
                        pe.wait_ge(high_copied, 1 + it * HIGH + high_before(i) + 1)
                    if qt == 0:
                        pe.wait_ge(normed, 1 + it * GH + max(j - 1, 0))
                    for kt in range(qt + 1):
                        mm = pe.matmul(mixed[:, j % 2, qt * VW:(qt + 1) * VW], probs_t[:, i % 2, kt * P:(kt + 1) * P],
                                       v[:, bass.ds(b * QT + kt, 1), bass.ds(g * GH + j, 1), :],
                                       start=(kt == 0), stop=(kt == qt))
                    mm.then_inc(pv_done, 1)

                pe.wait_ge(staged_ready, 2 * it + 2)
                for i in range(STEPS + 2):
                    if i < STEPS:
                        score(i)
                    if 1 <= i <= STEPS:
                        turn_weights(i - 1)
                    if i >= 2:
                        mix(i - 2)
            pe.wait_ge(normed, 1 + B * NG * GH)
            for t in range(B * QT):
                bank = psum8[t // 2 % 4]
                if t % 2 == 0 and t >= 8:
                    pe.wait_ge(ot_stored, t // 2 - 3)
                for k in range(KD):
                    mm = pe.transpose(bank[:, (t % 2 * KD + k) * P:(t % 2 * KD + k + 1) * P],
                                      on[:, t, k * HB:(k + 1) * HB, :].rearrange("p h e -> p (h e)"),
                                      consts["ident"][:])
                mm.then_inc(ot_ready, 1)
            pe.wait_ge(ot_stored, B * QT // 2)
            with pe.Fori(0, NCH // 2) as c2:
                for j in range(2):
                    for m in range(KD):
                        pe.wait_ge(out_free, c2 * 4 + 2 * j + m + 1)
                        for k in range(KD):
                            mm = pe.matmul(psum8[2 * j + m], w_o[:, k, m * P:(m + 1) * P],
                                           o[:, k, bass.ds(c2 * 2 * CH + j * CH, CH)],
                                           start=(k == 0), stop=(k == KD - 1))
                        mm.then_inc(out_ready, 1)

        @block.vector
        def _(dve):
            for sem in (low_copied, normed):
                dve.sem_inc(sem, 1)
            dve.sem_inc(out_free, 4)
            dve.wait_ge(loaded, 4 * 16)
            dve.tensor_copy(lateb[:], late[:]).then_inc(made, 1)
            dve.memset(v[:, :, :, HD:VW], 1.0).then_inc(made, 1)
            for t in range(B * QT):
                dve.wait_ge(v_ready, t + 1)
                dve.tensor_copy(v[:, t, :, 0:HD], mixed[:, t % 2, 0:D].rearrange("p (h e) -> p h e", h=H))\
                   .then_inc(v_free, 1)
            with dve.Fori(0, B) as b, dve.Fori(0, NG) as g:
                it = b * NG + g

                def norm_head(j):
                    m = mixed[:, j % 2, 0:QT * VW].rearrange("p (t e) -> p t e", e=VW)
                    dve.wait_ge(pv_done, 1 + it * STEPS + (j + 1) * QT)
                    dve.reciprocal(rden[:, j, :, :], m[:, :, HD:VW]).then_inc(rden_ready, 1)
                    dve.wait_ge(rden_ready, it * GH + j + 1)
                    dve.tensor_tensor(on[:, bass.ds(b * QT, QT), g * GH + j, :],
                                      m[:, :, 0:HD], rden[:, j, :, :].to_broadcast([P, QT, HD]),
                                      ALU.mult).then_inc(normed, 1)

                for i in range(STEPS + 3):
                    if i < STEPS:
                        dve.wait_ge(scored, 1 + it * STEPS + i + 1)
                        dve.tensor_reduce(nmax[:, i:i + 1], scores[:, i % 2, 0:(i % QT + 1) * P], AX.X, ALU.max,
                                          negate=True).then_inc(maxed, 1)
                    if 1 <= i <= STEPS:
                        k = i - 1
                        n = min(k % QT + 1, 4) * P
                        dve.wait_ge(turned_ready, 1 + it * STEPS + k + 1)
                        dve.wait_ge(pv_done, 1 + it * STEPS + max(k - 1, 0))
                        dve.tensor_copy(probs_t[:, k % 2, 0:n], turned[:, 0, 0:n]).then_inc(low_copied, 1)
                    if i >= 3 and (i - 3) % QT == QT - 1:
                        norm_head((i - 3) // QT)
            with dve.Fori(0, NCH // 2) as c2:
                for j in range(2):
                    for m in range(KD):
                        dve.wait_ge(out_ready, c2 * 4 + 2 * j + m + 1)
                        r = res[:, m, bass.ds(c2 * 2 * CH + j * CH, CH)]
                        dve.tensor_tensor(r, psum8[2 * j + m], r, ALU.add).then_inc(out_free, 1)

        @block.scalar
        def _(act):
            for sem in (exp_done, high_copied):
                act.sem_inc(sem, 1)
            act.sem_inc(qk_free, 4)
            with act.Fori(0, NCH) as c:
                for which in range(2):
                    for g in range(NG):
                        act.wait_ge(ready, c * 8 + which * NG + g + 1)
                        act.activation(qk[:, which, g, tok(c)], psum8[g], ACT.Copy,
                                       scale=1.0 if which else HD ** -0.5).then_inc(qk_free, 1)
            with act.Fori(0, B) as b, act.Fori(0, NG) as g:
                it = b * NG + g
                act.wait_ge(qk_free, 4 + NCH * 8)
                act.wait_ge(scored, 1 + it * STEPS)
                for which in range(2):
                    act.activation(staged[:, which, :], qk[:, which, g, bass.ds(b * S, S)], ACT.Copy)\
                       .then_inc(staged_ready, 1)
                for i in range(STEPS + 1):
                    if i < STEPS:
                        n = (i % QT + 1) * P
                        act.wait_ge(maxed, it * STEPS + i + 1)
                        act.wait_ge(turned_ready, 1 + it * STEPS + max(i - 1, 0))
                        act.activation(probs[:, i % 2, 0:n], scores[:, i % 2, 0:n], ACT.Exp,
                                       bias=nmax[:, i:i + 1]).then_inc(exp_done, 1)
                    if i >= 1 and (i - 1) % QT >= 4:
                        k = i - 1
                        n = (k % QT - 3) * P
                        act.wait_ge(turned_ready, 1 + it * STEPS + k + 1)
                        act.wait_ge(pv_done, 1 + it * STEPS + max(k - 1, 0))
                        act.activation(probs_t[:, k % 2, CH:CH + n], turned[:, 1, 0:n], ACT.Copy)\
                           .then_inc(high_copied, 1)
            for t2 in range(B * QT // 2):
                act.wait_ge(ot_ready, 2 * t2 + 2)
                act.activation(o[:, :, t2 * 2 * P:(t2 + 1) * 2 * P].rearrange("p k (t c) -> p t k c", t=2),
                               psum8[t2 % 4].rearrange("p (t k c) -> p t k c", t=2, k=KD),
                               ACT.Copy).then_inc(ot_stored, 1)


def gates(core, consts, h, gate_t):
    dram = core.dram
    with core.scope() as s:
        NT = B * QT
        w = s.sb("w", [P, KD, E])
        small = s.sb("small", [P, 8, NT, E])
        shifted, prob, rank, cmp, kept, gate, col = (small[:, n] for n in range(7))
        nmax, total, inv, top, top_inv = (col[:, :, n:n + 1] for n in range(5))
        logits = s.psum("logits", [P, CH])
        flat = s.psum("flat", [E, NCH, CH])
        loaded, ready, step, exp_done, flat_ready = (s.sem("loaded"), s.sem("ready"), s.sem("step"),
                                                     s.sem("exp_done"), s.sem("flat_ready"))
        block = s.block()
        lg = logits[:, 0:NT * E].rearrange("p (t e) -> p t e", e=E)

        @block.sync
        def _(sp):
            sp.dma_start(w[:], dram["moe_gate"]).then_inc(loaded, 16)

        @block.tensor
        def _(pe):
            pe.wait_ge(loaded, 16)
            for t in range(NT):
                for k in range(KD):
                    mm = pe.matmul(lg[:, t, :], h[:, k, t * P:(t + 1) * P], w[:, k, :],
                                   start=(k == 0), stop=(k == KD - 1))
            mm.then_inc(ready, 1)
            pe.wait_ge(ready, 2)
            for t in range(NT):
                mm = pe.transpose(flat[:, t // 4, t % 4 * P:(t % 4 + 1) * P], gate[:, t, :], consts["ident"][:])
            mm.then_inc(flat_ready, 1)

        @block.vector
        def _(dve):
            count = [0]

            def link(ins):
                count[0] += 1
                ins.then_inc(step, 1)
                dve.wait_ge(step, count[0])

            def wide(v):
                return v.to_broadcast([P, NT, E])

            dve.wait_ge(ready, 1)
            link(dve.tensor_reduce(nmax, lg, AX.X, ALU.max, negate=True))
            link(dve.tensor_tensor(shifted, lg, wide(nmax), ALU.add))
            dve.wait_ge(exp_done, 1)
            link(dve.tensor_reduce(total, prob, AX.X, ALU.add))
            link(dve.reciprocal(inv, total))
            link(dve.tensor_tensor(prob, prob, wide(inv), ALU.mult))
            link(dve.memset(rank, 0.0))
            for j in range(E):
                for lo, hi, op in ((0, j, ALU.is_gt), (j + 1, E, ALU.is_ge)):
                    if lo < hi:
                        link(dve.tensor_tensor(cmp[:, :, lo:hi], prob[:, :, j:j + 1].to_broadcast([P, NT, hi - lo]),
                                               prob[:, :, lo:hi], op))
                        link(dve.tensor_tensor(rank[:, :, lo:hi], rank[:, :, lo:hi], cmp[:, :, lo:hi], ALU.add))
            link(dve.scalar_tensor_tensor(out=kept, in0=rank, scalar=1.5, in1=prob, op0=ALU.is_lt, op1=ALU.mult))
            link(dve.tensor_reduce(top, kept, AX.X, ALU.add))
            link(dve.reciprocal(top_inv, top))
            dve.tensor_tensor(gate, kept, wide(top_inv), ALU.mult).then_inc(ready, 1)
            dve.wait_ge(flat_ready, 1)
            dve.tensor_copy(gate_t[:], flat[:].rearrange("e c t -> e (c t)"))

        @block.scalar
        def _(act):
            act.wait_ge(step, 2)
            act.activation(prob, shifted, ACT.Exp).then_inc(exp_done, 1)


def experts(core, consts, h, gate_t, res, x):
    dram = core.dram
    with core.scope() as s:
        w1 = s.sb("w1", [P, 2, KD, F])
        w2 = s.sb("w2", [P, 2, FB, D])
        pick = s.sb("pick", [E, 2, P])
        b1 = s.sb("b1", [P, 2, FB])
        b2 = s.sb("b2", [P, 2, KD])
        hidden = s.sb("hidden", [P, 2, FB, CH])
        gate = s.sb("gate", [P, 2, CH])
        weighed = s.sb("weighed", [P, 2, KD, CH])
        up = s.psum("up", [P, 3, CH])
        down = s.psum("down", [P, 2, KD, CH])
        pg = s.psum("pg", [P, CH])
        done = s.sem("done")
        loaded = [s.sem("loaded0"), s.sem("loaded1")]
        up_ready, hidden_ready = s.sem("up_ready"), s.sem("hidden_ready")
        pg_ready, gate_ready = s.sem("pg_ready"), s.sem("gate_ready")
        down_ready, weighed_ready, added = s.sem("down_ready"), s.sem("weighed_ready"), s.sem("added")
        block = s.block()
        EXPERT = ((w1, "moe_w1"), (w2, "moe_w2"), (pick, "moe_pick"), (b1, "moe_b1"), (b2, "moe_b2"))
        N_LOAD = len(EXPERT) * 16
        STEPS = 2 * NCH

        @block.sync
        def _(sp):
            with sp.Fori(0, E // 2) as e2:
                for u in range(2):
                    sp.wait_ge(added, 1 + e2 * STEPS)
                    for t, key in EXPERT:
                        sp.dma_start(t[:, u], dram[key][e2 * 2 + u]).then_inc(loaded[u], 16)

        @block.tensor
        def _(pe):
            for sem in (down_ready,):
                pe.sem_inc(sem, 1)
            with pe.Fori(0, E // 2) as e2:
                g0 = e2 * STEPS

                def first(i):
                    u, c = i // NCH, i % NCH
                    if c == 0:
                        pe.wait_ge(loaded[u], (e2 + 1) * N_LOAD)
                    pe.wait_ge(gate_ready, 1 + g0 + i)
                    pe.matmul(pg[:], pick[:, u, :], gate_t[:, c * CH:(c + 1) * CH], start=True, stop=True)\
                      .then_inc(pg_ready, 1)
                    for f in range(FB):
                        n = i * FB + f
                        pe.wait_ge(hidden_ready, 1 + g0 * FB + max(n - 2, 0))
                        for k in range(KD):
                            mm = pe.matmul(up[:, n % 3, :], w1[:, u, k, f * P:(f + 1) * P], h[:, k, c * CH:(c + 1) * CH],
                                           start=(k == 0), stop=(k == KD - 1))
                        mm.then_inc(up_ready, 1)

                def second(i):
                    u = i // NCH
                    pe.wait_ge(hidden_ready, 1 + (g0 + i + 1) * FB)
                    pe.wait_ge(weighed_ready, 1 + g0 + max(i - 1, 0))
                    for m in range(KD):
                        for f in range(FB):
                            mm = pe.matmul(down[:, i % 2, m, :], w2[:, u, f, m * P:(m + 1) * P],
                                           hidden[:, i % 2, f, :], start=(f == 0), stop=(f == FB - 1))
                    mm.then_inc(down_ready, 1)

                for i in range(STEPS + 1):
                    if i < STEPS:
                        first(i)
                    if i:
                        second(i - 1)

        @block.scalar
        def _(act):
            for sem in (gate_ready, hidden_ready):
                act.sem_inc(sem, 1)
            with act.Fori(0, E // 2) as e2:
                g0 = e2 * STEPS
                for i in range(STEPS):
                    act.wait_ge(pg_ready, g0 + i + 1)
                    act.wait_ge(weighed_ready, 1 + g0 + max(i - 1, 0))
                    act.activation(gate[:, i % 2, :], pg[:], ACT.Copy).then_inc(gate_ready, 1)
                    for f in range(FB):
                        n = i * FB + f
                        act.wait_ge(up_ready, g0 * FB + n + 1)
                        if f == 0:
                            act.wait_ge(down_ready, 1 + g0 + max(i - 1, 0))
                        act.activation(hidden[:, i % 2, f, :], up[:, n % 3, :], ACT.Gelu_apprx_tanh,
                                       bias=b1[:, i // NCH, f:f + 1]).then_inc(hidden_ready, 1)

        @block.vector
        def _(dve):
            for sem in (added, weighed_ready):
                dve.sem_inc(sem, 1)
            with dve.Fori(0, E // 2) as e2:
                g0 = e2 * STEPS
                for i in range(STEPS):
                    c = i % NCH
                    dve.wait_ge(gate_ready, 1 + g0 + i + 1)
                    dve.wait_ge(down_ready, 1 + g0 + i + 1)
                    for m in range(KD):
                        last = dve.scalar_tensor_tensor(out=weighed[:, i % 2, m, :], in0=down[:, i % 2, m, :],
                                                        scalar=b2[:, i // NCH, m:m + 1],
                                                        in1=gate[:, i % 2, :], op0=ALU.add, op1=ALU.mult)
                    last.then_inc(weighed_ready, 1)
                    dve.wait_ge(weighed_ready, 1 + g0 + i + 1)
                    r = res[:, :, c * CH:(c + 1) * CH]
                    dve.tensor_tensor(r, r, weighed[:, i % 2, :, :], ALU.add).then_inc(added, 1)
            dve.wait_ge(added, 1 + E * NCH)
            dve.tensor_tensor(x[:], x[:], res[:], ALU.add).then_inc(done, 1)


def coupling(core, consts, r, x):
    dram = core.dram
    CYCLES = 3
    with core.scope() as s:
        w1 = s.sb("w1", [P, KD, D])
        w2 = s.sb("w2", [P, KD, P])
        w3 = s.sb("w3", [P, 64])
        w4 = s.sb("w4", [64, 2])
        b12 = s.sb("b12", [P, 3])
        b3 = s.sb("b3", [64, 1])
        g1 = s.sb("g1", [P, KD, P])
        g2 = s.sb("g2", [P, 64])
        gb = s.sb("gb", [P, 2])
        one_each = s.sb("one_each", [P, 4])
        w4b = s.sb("w4b", [64, 2, P])
        mean = s.sb("mean", [P, KD, B])
        gh1 = s.sb("gh1", [P, B])
        gh2 = s.sb("gh2", [64, B])
        gf = s.sb("gf", [P, B])
        k = s.sb("k", [P, 4])
        h1 = s.sb("h1", [P, KD, T])
        h2 = s.sb("h2", [P, T])
        h3 = s.sb("h3", [64, T])
        tf = s.sb("tf", [P, T])
        twist = s.sb("twist", [P, 2, KD, CH])
        psum = s.psum("psum", [P, 8, CH])
        loaded, made, step = s.sem("loaded"), s.sem("made"), s.sem("step")
        g_ready, g_done = s.sem("g_ready"), s.sem("g_done")
        m1, m2, m3, m4 = (s.sem(f"layer{n}_ready") for n in range(1, 5))
        a1, a2, a3, a4 = (s.sem(f"layer{n}_stored") for n in range(1, 5))
        coupled, twisted, moved, done = s.sem("coupled"), s.sem("twisted"), s.sem("moved"), s.sem("done")
        block = s.block()
        LOADS = ((w1, "c_w1"), (w2, "c_w2"), (w3, "c_w3"), (w4, "c_w4"), (b12, "c_b12"), (b3, "c_b3"),
                 (g1, "g_w1"), (g2, "g_w2"), (gb, "g_b"), (one_each, "c_each"))

        @block.sync
        def _(sp):
            for t, key in LOADS:
                sp.dma_start(t[:], dram[key]).then_inc(loaded, 16)

        @block.tensor
        def _(pe):
            pe.wait_ge(loaded, 16 * len(LOADS))
            pe.wait_ge(step, 1)
            for q in range(KD):
                mm = pe.matmul(psum[:, 4, 0:B], g1[:, q, :], mean[:, q, :], start=(q == 0), stop=(q == KD - 1))
            mm.then_inc(g_ready, 1)
            pe.wait_ge(g_done, 1)
            pe.matmul(psum[0:64, 5, 0:B], g2[:], gh1[:], start=True, stop=True).then_inc(g_ready, 1)
            pe.wait_ge(g_done, 2)
            pe.wait_ge(made, 1)
            pe.matmul(psum[:, 6, 0:B], w4b[:, 0, :], gh2[:], start=True, stop=True).then_inc(g_ready, 1)
            pe.wait_ge(g_done, 3)
            for y in range(CYCLES):
                n0 = y * NCH
                for c in range(NCH):
                    if y:
                        pe.wait_ge(moved, n0 - NCH + c + 1)
                    for m in range(KD):
                        if c >= 2 or y:
                            pe.wait_ge(a1, (n0 + c - 2) * KD + m + 1)
                        for q in range(KD):
                            mm = pe.matmul(psum[:, 2 * (c % 2) + m, :], w1[:, q, m * P:(m + 1) * P],
                                           r[:, q, c * CH:(c + 1) * CH], start=(q == 0), stop=(q == KD - 1))
                        mm.then_inc(m1, 1)
                for c in range(NCH):
                    pe.wait_ge(a1, (n0 + c + 1) * KD)
                    if c >= 2 or y:
                        pe.wait_ge(a2, n0 + c - 1)
                    for q in range(KD):
                        mm = pe.matmul(psum[:, 4 + c % 2, :], w2[:, q, :], h1[:, q, c * CH:(c + 1) * CH],
                                       start=(q == 0), stop=(q == KD - 1))
                    mm.then_inc(m2, 1)
                for c in range(NCH):
                    pe.wait_ge(a2, n0 + c + 1)
                    if c or y:
                        pe.wait_ge(a3, n0 + c)
                    pe.matmul(psum[0:64, 6, :], w3[:], h2[:, c * CH:(c + 1) * CH], start=True, stop=True)\
                      .then_inc(m3, 1)
                for c in range(NCH):
                    pe.wait_ge(a3, n0 + c + 1)
                    if c or y:
                        pe.wait_ge(a4, n0 + c)
                    pe.matmul(psum[:, 7, :], w4b[:, 1, :], h3[:, c * CH:(c + 1) * CH], start=True, stop=True)\
                      .then_inc(m4, 1)

        @block.scalar
        def _(act):
            act.wait_ge(loaded, 16 * len(LOADS))
            act.wait_ge(g_ready, 1)
            act.activation(gh1[:], psum[:, 4, 0:B], ACT.Gelu, bias=gb[:, 0:1], scale=1.0 / S).then_inc(g_done, 1)
            act.wait_ge(g_ready, 2)
            act.activation(gh2[:], psum[0:64, 5, 0:B], ACT.Gelu, bias=gb[0:64, 1:2]).then_inc(g_done, 1)
            act.wait_ge(g_ready, 3)
            act.activation(gf[:], psum[:, 6, 0:B], ACT.Sigmoid, bias=one_each[:, 1:2]).then_inc(g_done, 1)
            for y in range(CYCLES):
                n0 = y * NCH
                for c in range(NCH):
                    for m in range(KD):
                        act.wait_ge(m1, (n0 + c) * KD + m + 1)
                        act.activation(h1[:, m, c * CH:(c + 1) * CH], psum[:, 2 * (c % 2) + m, :], ACT.Gelu,
                                       bias=b12[:, m:m + 1]).then_inc(a1, 1)
                for c in range(NCH):
                    act.wait_ge(m2, n0 + c + 1)
                    act.activation(h2[:, c * CH:(c + 1) * CH], psum[:, 4 + c % 2, :], ACT.Gelu,
                                   bias=b12[:, 2:3]).then_inc(a2, 1)
                for c in range(NCH):
                    act.wait_ge(m3, n0 + c + 1)
                    act.activation(h3[:, c * CH:(c + 1) * CH], psum[0:64, 6, :], ACT.Gelu,
                                   bias=b3[:, 0:1]).then_inc(a3, 1)
                for c in range(NCH):
                    act.wait_ge(m4, n0 + c + 1)
                    if y:
                        act.wait_ge(coupled, n0 - NCH + c + 1)
                        act.wait_ge(moved, n0 - NCH + c + 1)
                    act.activation(tf[:, c * CH:(c + 1) * CH], psum[:, 7, :], ACT.Sigmoid,
                                   bias=one_each[:, 0:1]).then_inc(a4, 1)

        @block.vector
        def _(dve):
            count = [1]

            def link(ins):
                count[0] += 1
                ins.then_inc(step, 1)
                dve.wait_ge(step, count[0])

            dve.tensor_reduce(mean[:], r[:].rearrange("p k (b t) -> p k b t", b=B), AX.X, ALU.add).then_inc(step, 1)
            dve.wait_ge(loaded, 16 * len(LOADS))
            dve.tensor_copy(w4b[:], w4[:].unsqueeze(2).to_broadcast([64, 2, P])).then_inc(made, 1)
            dve.wait_ge(g_done, 3)
            rng, sign = one_each[:, 2:3], one_each[:, 3:4]
            link(dve.tensor_scalar(k[:, 0:1], rng, 0.6, sign, ALU.mult, ALU.mult))
            link(dve.tensor_scalar(k[:, 1:3], gf[:], 0.7, -0.5, ALU.mult, ALU.add))
            link(dve.tensor_scalar(k[:, 1:3], k[:, 1:3], rng, 2.0, ALU.mult, ALU.mult))
            link(dve.tensor_scalar(k[:, 1:3], k[:, 1:3], 0.1, sign, ALU.add, ALU.mult))
            for y in range(CYCLES):
                for c in range(NCH):
                    n = y * NCH + c
                    t = tf[:, c * CH:(c + 1) * CH]
                    rc = r[:, :, c * CH:(c + 1) * CH]
                    dve.wait_ge(a4, n + 1)
                    b = c // BCH
                    dve.tensor_scalar(t, t, k[:, 0:1], k[:, 1 + b:2 + b], ALU.mult, ALU.add).then_inc(coupled, 1)
                    dve.wait_ge(coupled, n + 1)
                    dve.tensor_tensor(twist[:, c % 2, :, :], rc, t.unsqueeze(1).to_broadcast([P, KD, CH]),
                                      ALU.mult).then_inc(twisted, 1)
                    dve.wait_ge(twisted, n + 1)
                    dve.tensor_tensor(rc[:, 0, :], rc[:, 0, :], twist[:, c % 2, 1, :], ALU.add)
                    dve.tensor_tensor(rc[:, 1, :], rc[:, 1, :], twist[:, c % 2, 0, :], ALU.subtract).then_inc(moved, 1)
                    dve.wait_ge(moved, n + 1)
            dve.tensor_tensor(x[:], x[:], r[:], ALU.add).then_inc(done, 1)


def cols(a, n):
    return a.reshape(n, P).T


def rows(a):
    return a.reshape(-1, P, a.shape[-1]).transpose(1, 0, 2)


def mamba_arrays(name, inproj, xproj, dtw, outproj, convw, convb, dtb, skip, alog, rank):
    import numpy as np
    x = np.zeros((XD, EI), np.float32)
    x[0:rank] = xproj[0:rank]
    x[BC0:XD] = xproj[rank:].reshape(2, NS, EI).transpose(1, 0, 2).reshape(2 * NS, EI)
    return {
        f"{name}_in": rows(inproj.T), f"{name}_x": rows(x.T), f"{name}_dt": dtw.T,
        f"{name}_out": rows(outproj.T),
        f"{name}_conv": convw.reshape(EB, P, TAPS).transpose(1, 0, 2),
        f"{name}_cols": np.stack([cols(v, EB) for v in (convb, dtb, skip)], 1),
        f"{name}_alog": alog.reshape(EB, P, NS).transpose(1, 0, 2).reshape(P, EB * NS),
    }


def xattn_arrays(name, i, p, transposed, biased):
    import numpy as np
    w = [i[p + k].T if transposed else i[p + k] for k in ("Wq", "Wk", "Wv", "Wo")]
    none = np.zeros(D, np.float32)
    bq, bk, bv, bo = (i[p + k] if biased else none for k in ("bq", "bk", "bv", "bo"))
    return {name + "_w": np.stack([rows(m) for m in w], 1), name + "_bias": np.stack([cols(v, KD) for v in (bq, bk, bo)], 1),
            name + "_v_bias": bv[None]}


def layout(i):
    a = {"xT": rows(i["x"].reshape(T, D).T)}
    for d in ("fwd", "bwd"):
        p = f"L0_attn_{d}_"
        a |= mamba_arrays(d, i[p + "inproj"], i[p + "xproj"], i[p + "dtw"], i[p + "outproj"], i[p + "convw"],
                          i[p + "convb"], i[p + "dtb"], i[p + "Dp"], i[p + "Alog"], 64)
    p = "L1_attn_"
    a |= mamba_arrays("m1", i[p + "in_proj_w"], i[p + "x_proj_w"], i[p + "dt_proj_w"], i[p + "out_proj_w"],
                      i[p + "conv_w"], i[p + "conv_b"], i[p + "dt_proj_b"], i[p + "D"], i[p + "A_log"], 16)
    import numpy as np
    a |= xattn_arrays("x0", i, "L0_xattn_", True, False)
    a |= xattn_arrays("x1", i, "L1_xattn_", False, True)
    a["ctxT"] = rows(i["ctx_1024"].reshape(B * SK, D).T).reshape(P, KD, B, SK)
    a["key_mask"] = i["mask_Bx1x1xS2_ff0"].reshape(1, B, SK)
    f = "L0_ffn_"
    qkv = i[f + "w_qkv"].reshape(D, 3, H, HD)
    padded = np.zeros((D, 2, H, 2 * HD), np.float32)
    padded[..., 0:HD] = qkv[:, 0:2]
    a["a0_qk"] = padded.reshape(KD, P, 2, NG * P).transpose(1, 2, 0, 3)
    a["a0_v"] = rows(qkv[:, 2].reshape(D, D))
    a["a0_o"] = rows(i[f + "w_o"])
    a["tri"] = np.where(np.arange(P)[None] > np.arange(P)[:, None], np.float32(-1e30), np.float32(0))
    a["lns"] = np.stack([cols(i[f + n], KD) for n in ("ln1_g", "ln1_b", "ln2_g", "ln2_b")], 1)
    a["moe_gate"] = rows(i[f + "w_gate"])
    a["moe_w1"] = np.stack([rows(w) for w in i[f + "w1"]])
    a["moe_w2"] = np.stack([rows(w) for w in i[f + "w2"]])
    a["moe_pick"] = np.broadcast_to(np.eye(E, dtype=np.float32)[:, :, None], (E, E, P))
    a["moe_b1"] = i[f + "b1"].reshape(E, FB, P).transpose(0, 2, 1)
    a["moe_b2"] = i[f + "b2"].reshape(E, KD, P).transpose(0, 2, 1)
    g = "L1_ffn_"
    a["c_w1"], a["c_w2"], a["c_w3"] = rows(i[g + "cn_w1"]), rows(i[g + "cn_w2"]), i[g + "cn_w3"]
    a["c_w4"] = np.concatenate([i[g + "gc_w3"], i[g + "cn_w4"]], 1)
    a["c_b12"] = np.concatenate([cols(i[g + "cn_b1"], KD), cols(i[g + "cn_b2"], 1)], 1)
    a["c_b3"] = i[g + "cn_b3"][:, None]
    a["g_w1"], a["g_w2"] = rows(i[g + "gc_w1"]), i[g + "gc_w2"]
    gb = np.zeros((P, 2), np.float32)
    gb[:, 0], gb[0:64, 1] = i[g + "gc_b1"], i[g + "gc_b2"]
    a["g_b"] = gb
    each = np.empty((P, 4), np.float32)
    each[:, 0], each[:, 1], each[:, 2] = i[g + "cn_b4"], i[g + "gc_b3"], i[g + "adaptive_range"]
    each[:, 3] = np.where(np.arange(P) < P // 2, 1, -1)
    a["c_each"] = each
    part = np.arange(P)
    a["head_mask"] = (part[:, None] // HD == np.arange(HB)).astype(np.float32)
    a["pair_mask"] = (part[:, None] // SK == np.arange(2)).astype(np.float32)
    query = part[:, None, None] + P * np.arange(QT)[None, :, None]
    a["late"] = np.where(np.arange(SK)[None, None, :] > query, np.float32(-1e30), np.float32(0))
    a["norms"] = np.stack([cols(i[k], KD) for k in
                           ("L0_attn_fwd_norm", "L0_attn_bwd_norm", "L0_attn_normf", "L1_attn_norm_w")], 1)
    return a


def program(nc, dram, out, stages=range(6)):
    with ExitStack() as ctx:
        core = Core(nc, ctx, dram)

        def sb(name, shape, dt=F32):
            return ctx.enter_context(nc.sbuf_tensor(name, shape, dt))

        x = sb("x", [P, KD, T])
        consts = {"ident": sb("ident", [P, P]), "ones": sb("ones", [P, P]), "sel": sb("sel", [96, 32, P], BF16),
                  "eps": sb("eps", [P, 1]), "one": sb("one", [P, 1]), "norms": sb("norms", [P, 4, KD]), "identb": sb("identb", [P, P], BF16),
                  "head_mask": sb("head_mask", [P, HB]),
                  "pair_mask": sb("pair_mask", [P, 2])}
        norms = consts["norms"]
        start(core, x, consts)
        if 0 in stages:
            with core.scope() as s:
                res = s.sb("res", [P, KD, T])
                xn = s.sb("xn", [P, KD, T])
                norm(core, consts, x, res, True)
                for n, (name, flip) in enumerate((("fwd", False), ("bwd", True))):
                    norm(core, consts, res, xn, False, weight=norms[:, n, :])
                    mamba(core, consts, name, xn, res, 64, flip)
                    norm(core, consts, xn, xn, False, weight=norms[:, 2, :], add_to=x)
        if 1 in stages:
            with core.scope() as s:
                h = s.sb("h", [P, KD, T])
                norm(core, consts, x, h, True)
                cross_attention(core, consts, "x0", h, x, True)
        if 2 in stages:
            with core.scope() as s:
                lns = s.sb("lns", [P, 4, KD])
                res = s.sb("res", [P, KD, T])
                h = s.sb("h", [P, KD, T])
                gate_t = s.sb("gate_t", [E, T])
                load(core, lns, "lns")
                norm(core, consts, x, res, True)
                norm(core, consts, res, h, True, weight=lns[:, 0, :], bias=lns[:, 1, :])
                self_attention(core, consts, h, res)
                norm(core, consts, res, h, True, weight=lns[:, 2, :], bias=lns[:, 3, :])
                gates(core, consts, h, gate_t)
                experts(core, consts, h, gate_t, res, x)
        if 3 in stages:
            with core.scope() as s:
                res = s.sb("res", [P, KD, T])
                xn = s.sb("xn", [P, KD, T])
                norm(core, consts, x, res, True)
                norm(core, consts, res, xn, False, weight=norms[:, 3, :])
                mamba(core, consts, "m1", xn, res, 16, False, x_out=x)
        if 4 in stages:
            with core.scope() as s:
                h = s.sb("h", [P, KD, T])
                norm(core, consts, x, h, True)
                cross_attention(core, consts, "x1", h, x, False)
        if 5 in stages:
            with core.scope() as s:
                h = s.sb("h", [P, KD, T])
                norm(core, consts, x, h, True)
                coupling(core, consts, h, x)
        finish(core, x, out)


def load(core, tile, key):
    with core.scope() as s:
        loaded = s.sem("loaded")
        block = s.block()

        @block.sync
        def _(sp):
            sp.dma_start(tile[:], core.dram[key]).then_inc(loaded, 16)
            sp.wait_ge(loaded, 16)


def finish(core, x, out):
    with core.scope() as s:
        stored = s.sem("stored")
        block = s.block()

        @block.sync
        def _(sp):
            sp.dma_start(out, x[:]).then_inc(stored, 16)
            sp.wait_ge(stored, 16)


def kernel(**inputs):
    import numpy as np
    import concourse.bacc as bacc
    from concourse.bass_utils import run_bass_kernel_spmd

    nc = bacc.Bacc("TRN2", target_bir_lowering=False, num_devices=1)
    arrays = {k: np.ascontiguousarray(v) for k, v in layout({k: np.asarray(v) for k, v in inputs.items()}).items()}
    dram = {k: nc.dram_tensor(f"in_{k}", v.shape, mybir.dt.from_np(v.dtype), kind="ExternalInput").ap()
            for k, v in arrays.items()}
    out = nc.dram_tensor("out", (P, KD, T), F32, kind="ExternalOutput").ap()
    program(nc, dram, out)
    r = run_bass_kernel_spmd(nc, [{f"in_{k}": v for k, v in arrays.items()}], core_ids=[0])
    y = r.results[0]["out"]
    return np.ascontiguousarray(y.transpose(1, 0, 2).reshape(D, T).T).reshape(B, S, D)
```

```python
from contextlib import ExitStack

import concourse.bass as bass
from concourse import mybir

F32 = mybir.dt.float32
BF16 = mybir.dt.bfloat16
ACT = mybir.ActivationFunctionType
ALU = mybir.AluOpType
AX = mybir.AxisListType

P = 128
B, S, D = 2, 1024, 256
T = B * S
KD = D // P
CH = 512
NCH = T // CH
BCH = S // CH
EI = 512
EB = EI // P
NS = 16
STAGE_AHEAD = 6
AHEAD = 1
TAPS = 4
XD = 96
BC0 = 64
EPS = 1e-5


class Core:

    def __init__(self, nc, ctx, dram):
        self.nc, self.ctx, self.dram = nc, ctx, dram
        self.n = 0
        self.cleared = []

    def scope(self):
        return Scope(self)


class Scope:

    def __init__(self, core):
        self.core, self.stack = core, ExitStack()
        self.sems, self.ends = [], False

    def __enter__(self):
        self.stack.__enter__()
        self.core.n += 1
        self.tag = f"s{self.core.n}_"
        return self

    def __exit__(self, *what):
        self.stack.__exit__(*what)
        core = self.core
        if self.ends:
            for sem in core.cleared:
                core.nc.release_semaphore(sem)
            core.cleared = []
        for sem in self.sems:
            core.nc.gpsimd.sem_clear(sem)
        core.cleared += self.sems

    def sb(self, name, shape, dt=F32):
        return self.stack.enter_context(self.core.nc.sbuf_tensor(self.tag + name, shape, dt))

    def psum(self, name, shape, dt=F32):
        return self.stack.enter_context(self.core.nc.psum_tensor(self.tag + name, shape, dt))

    def sem(self, name):
        self.sems.append(self.core.nc.alloc_semaphore(self.tag + name))
        return self.sems[-1]

    def block(self):
        self.ends = True
        return self.stack.enter_context(self.core.nc.Block())


def tok(c, n=1):
    return bass.ds(c * CH, n * CH)


def start(core, x, consts):
    nc = core.nc
    with core.scope() as s:
        ident, ones, sel = consts["ident"], consts["ones"], consts["sel"]
        loaded, cleared, made = s.sem("loaded"), s.sem("cleared"), s.sem("made")
        block = s.block()

        @block.sync
        def _(sp):
            sp.dma_start(x[:], core.dram["xT"]).then_inc(loaded, 16)
            for key in ("norms", "head_mask", "pair_mask"):
                sp.dma_start(consts[key][:], core.dram[key]).then_inc(loaded, 16)
            sp.wait_ge(loaded, 4 * 16)

        @block.vector
        def _(dve):
            dve.memset(ones[:], 1.0 / D)
            dve.memset(consts["eps"][:], EPS)
            dve.memset(consts["one"][:], 1.0)
            dve.wait_ge(made, 1)
            dve.tensor_copy(consts["identb"][:], ident[:])

        @block.gpsimd
        def _(pool):
            pool.memset(ident[:], 0.0).then_inc(cleared, 1)
            pool.memset(sel[:], 0.0).then_inc(cleared, 1)
            pool.wait_ge(cleared, 2)
            pool.affine_select(out=ident[:], in_=ident[:], compare_op=ALU.not_equal, fill=1.0,
                               base=0, pattern=[[-1, P]], channel_multiplier=1).then_inc(made, 1)
            for part in range(3):
                pool.wait_ge(made, part + 1)
                v = sel[part * 32:(part + 1) * 32, :, :]
                pool.affine_select(out=v, in_=v, compare_op=ALU.not_equal, fill=1.0, base=0,
                                   pattern=[[-1, 32], [0, P]], channel_multiplier=1).then_inc(made, 1)
            pool.wait_ge(made, 4)


def norm(core, consts, src, dst, center, weight=None, bias=None, add_to=None, prefetch=()):
    with core.scope() as s:
        psum = s.psum("stat", [P, 2 * NCH, CH])
        square = s.sb("square", [P, KD, T])
        rstd = s.sb("rstd", [P, T])
        mean_ready, centered, squared = s.sem("mean_ready"), s.sem("centered"), s.sem("squared")
        var_ready, log_ready, rstd_ready = s.sem("var_ready"), s.sem("log_ready"), s.sem("rstd_ready")
        scaled, done = s.sem("scaled"), s.sem("done")
        body = dst if center else src
        block = s.block()

        @block.sync
        def _(sp):
            for tile, array, sem in prefetch:
                sp.dma_start(tile, array).then_inc(sem, 16)

        @block.tensor
        def _(pe):
            if center:
                with pe.Fori(0, NCH) as c:
                    for k in range(KD):
                        mm = pe.matmul(psum[:, c, :], consts["ones"][:], src[:, k, tok(c)],
                                       start=(k == 0), stop=(k == KD - 1))
                    mm.then_inc(mean_ready, 1)
            with pe.Fori(0, NCH) as c:
                pe.wait_ge(squared, c + 1)
                for k in range(KD):
                    mm = pe.matmul(psum[:, c + NCH, :], consts["ones"][:], square[:, k, tok(c)],
                                   start=(k == 0), stop=(k == KD - 1))
                mm.then_inc(var_ready, 1)

        @block.vector
        def _(dve):
            if center:
                with dve.Fori(0, NCH) as c:
                    dve.wait_ge(mean_ready, c + 1)
                    for k in range(KD):
                        last = dve.tensor_tensor(dst[:, k, tok(c)], src[:, k, tok(c)], psum[:, c, :],
                                                 ALU.subtract)
                    last.then_inc(centered, 1)
            with dve.Fori(0, NCH) as c:
                dve.wait_ge(rstd_ready, c + 1)
                for k in range(KD):
                    if weight is None:
                        last = dve.tensor_tensor(dst[:, k, tok(c)], body[:, k, tok(c)],
                                                 rstd[:, tok(c)], ALU.mult)
                    else:
                        last = dve.scalar_tensor_tensor(out=dst[:, k, tok(c)], in0=body[:, k, tok(c)],
                                                        scalar=weight[:, k:k + 1], in1=rstd[:, tok(c)],
                                                        op0=ALU.mult, op1=ALU.mult)
                last.then_inc(scaled, 1)
            if bias is not None:
                dve.wait_ge(scaled, NCH)
                for k in range(KD):
                    last = dve.tensor_scalar(dst[:, k, :], dst[:, k, :], bias[:, k:k + 1], None, ALU.add)
                last.then_inc(done, 1)
            if add_to is not None:
                dve.wait_ge(scaled, NCH)
                last = dve.tensor_tensor(add_to[:], add_to[:], dst[:], ALU.add).then_inc(done, 1)

        @block.scalar
        def _(act):
            with act.Fori(0, NCH) as c:
                if center:
                    act.wait_ge(centered, c + 1)
                act.activation(square[:, :, tok(c)], body[:, :, tok(c)], ACT.Square).then_inc(squared, 1)
            with act.Fori(0, NCH) as c:
                act.wait_ge(var_ready, c + 1)
                act.activation(rstd[:, tok(c)], psum[:, c + NCH, :], ACT.Ln,
                               bias=consts["eps"][:, 0:1]).then_inc(log_ready, 1)
            with act.Fori(0, NCH) as c:
                act.wait_ge(log_ready, c + 1)
                act.activation(rstd[:, tok(c)], rstd[:, tok(c)], ACT.Exp, scale=-0.5).then_inc(rstd_ready, 1)


def mamba(core, consts, name, xn, res, norm_weight, steps, flip, x_out=None):
    dram = core.dram
    with core.scope() as s:
        w_in = s.sb("w_in", [P, KD, 2 * EI])
        w_x = s.sb("w_x", [P, EB, XD])
        w_dt = s.sb("w_dt", [steps, EI])
        w_out = s.sb("w_out", [P, EB, D])
        w_conv = s.sb("w_conv", [P, EB, TAPS])
        cols = s.sb("cols", [P, 3, EB])
        a_log = s.sb("a_log", [P, EB * NS])
        loaded, a_ready = s.sem("loaded"), s.sem("a_ready")
        norm(core, consts, res, xn, False, weight=norm_weight,
             prefetch=[(t[:], dram[f"{name}_{key}"], loaded)
                       for t, key in ((w_in, "in"), (w_x, "x"), (w_dt, "dt"), (w_out, "out"),
                                      (w_conv, "conv"), (cols, "cols"), (a_log, "alog"))])
        a_neg = s.sb("a_neg", [P, EB * NS])
        gate = s.sb("gate", [P, EB, S])
        u = s.sb("u", [P, EB, S])
        pad = s.sb("pad", [P, EB, S + TAPS - 1])
        dt = pad[:, :, 0:S]
        dx = s.sb("dx", [P, EB, S])
        bc = s.sb("bc", [P, 2 * NS, CH])
        relu = bc[:, 0:8, :].rearrange("p (m c) t -> p m (c t)", m=EB)
        low = bc[0:steps, 8:10, :].rearrange("p c t -> p (c t)")
        parts = s.sb("parts", [96, S], BF16)
        rest = bc[0:32, 10, :]
        mid = bc[0:32, 11, :].bitcast(BF16)[:, 0:CH]
        state = s.sb("state", [P, EB * NS])
        dbu = w_in[:].rearrange("p k (h t) -> p (k h) t", t=CH)
        hc = s.sb("hc", [P, 2, CH])
        ysum = bc[:, 0, :]
        psum = s.psum("psum", [P, 8, CH])
        one = consts["one"]

        for b in range(B):
            with core.scope() as q:
                x_free, z_free, x_ready, z_ready = (q.sem("x_free"), q.sem("z_free"), q.sem("x_ready"),
                                                    q.sem("z_ready"))
                padded, conv_step, u_ready = q.sem("padded"), q.sem("conv_step"), q.sem("u_ready")
                xd_ready, xd_free, low_ready = q.sem("xd_ready"), q.sem("xd_free"), q.sem("low_ready")
                split_step, dtp_ready, dtp_free = q.sem("split_step"), q.sem("dtp_ready"), q.sem("dtp_free")
                exp_done, soft_done, dt_ready, dx_ready = (q.sem("exp_done"), q.sem("soft_done"),
                                                           q.sem("dt_ready"), q.sem("dx_ready"))
                turn, act_turn = q.sem("turn"), q.sem("act_turn")
                stage_ready, bc_ready = q.sem("stage_ready"), q.sem("bc_ready")
                decay_ready, dbu_ready = q.sem("decay_ready"), q.sem("dbu_ready")
                scanned, hc_ready, hc_used = q.sem("scanned"), q.sem("hc_ready"), q.sem("hc_used")
                saved = q.sem("saved")
                y_sum, y_ready = q.sem("y_sum"), q.sem("y_ready")
                out_ready, out_free, stored = q.sem("out_ready"), q.sem("out_free"), q.sem("stored")
                block = q.block()
                c0 = b * BCH

                def flipped(t, k, c):
                    if not flip:
                        return t[:, k, bass.ds((c0 + c) * CH, CH)]
                    return t[:, k, bass.ds((c0 + BCH - 1) * CH - c * CH, CH)][:, ::-1]

                @block.sync
                def _(sp):
                    if b + 1 < B:
                        sp.wait_ge(scanned, 1 + BCH * EB * NS)
                        sp.dma_start(w_in[:], dram[f"{name}_in"]).then_inc(loaded, 16)

                N_W = (7 + b) * 16

                @block.tensor
                def _(pe):
                    for sem in (hc_used,):
                        pe.sem_inc(sem, 1)
                    pe.wait_ge(loaded, N_W)
                    for c, m in [(c, m) for half in range(2) for c in range(BCH)
                                 for m in range(half * EB, (half + 1) * EB)]:
                        free, done = (x_free, x_ready) if m < EB else (z_free, z_ready)
                        pe.wait_ge(free, c * EB + m % EB + 1)
                        for k in range(KD):
                            mm = pe.matmul(psum[:, m, :], w_in[:, k, m * P:(m + 1) * P],
                                           flipped(xn, k, c), start=(k == 0), stop=(k == KD - 1))
                        mm.then_inc(done, 1)
                    with pe.Fori(0, BCH) as c:
                        for k in range(EB):
                            pe.wait_ge(u_ready, k + 1)
                            mm = pe.matmul(psum[0:XD, c, :], w_x[:, k, :], u[:, k, tok(c)],
                                           start=(k == 0), stop=(k == EB - 1))
                        mm.then_inc(xd_ready, 1)
                    for c in range(BCH):
                        pe.wait_ge(low_ready, c + 1)
                        for m in range(EB):
                            pe.wait_ge(dtp_free, c * EB + m + 1)
                            pe.matmul(psum[:, 4 + m, :], w_dt[:, m * P:(m + 1) * P], low[:, c * CH:(c + 1) * CH],
                                      start=True, stop=True).then_inc(dtp_ready, 1)
                    pe.wait_ge(dt_ready, BCH * EB)
                    with pe.Fori(0, BCH) as c:
                        pe.wait_ge(split_step, c * 4 + 4)

                        def stage(j):
                            pe.wait_ge(bc_ready, 1 + c * 2 * NS + max(j - 1, 0))
                            pe.matmul(psum[:, 6 + j % 2, :], consts["sel"][:, j, :], parts[:, tok(c)],
                                      start=True, stop=True).then_inc(stage_ready, 1)

                        for j in range(2 * STAGE_AHEAD):
                            stage(j)
                        for e in range(EB):
                            pe.wait_ge(y_ready, 1 + c * EB + max(e - 1, 0))
                            for n in range(NS):
                                if e == 0 and n + STAGE_AHEAD < NS:
                                    stage(2 * (n + STAGE_AHEAD))
                                    stage(2 * (n + STAGE_AHEAD) + 1)
                                pe.wait_ge(hc_ready, 4 + c * EB * NS + e * NS + n + 1)
                                pe.matmul(psum[:, 4 + e % 2, :], consts["ident"][:], hc[:, n % 2, :],
                                          start=(n == 0), stop=(n == NS - 1)).then_inc(hc_used, 1)
                    with pe.Fori(0, BCH) as c:
                        pe.wait_ge(y_ready, 1 + BCH * EB)
                        for m in range(KD):
                            pe.wait_ge(out_free, c * KD + m + 1)
                            for k in range(EB):
                                mm = pe.matmul(psum[:, 6 + m, :], w_out[:, k, m * P:(m + 1) * P],
                                               dx[:, k, tok(c)], start=(k == 0), stop=(k == EB - 1))
                            mm.then_inc(out_ready, 1)

                @block.vector
                def _(dve):
                    for sem in (y_ready, scanned):
                        dve.sem_inc(sem, 1)
                    dve.sem_inc(hc_ready, 4)
                    dve.sem_inc(x_free, EB)
                    dve.sem_inc(out_free, KD)
                    dve.memset(pad[:, :, 0:TAPS - 1], 0.0).then_inc(padded, 1)
                    dve.memset(state[:], 0.0).then_inc(saved, 1)
                    if b == 0:
                        dve.wait_ge(loaded, N_W)
                        dve.wait_ge(a_ready, 1)
                        dve.tensor_scalar(a_neg[:], a_neg[:], -1.0, None, ALU.mult).then_inc(a_ready, 1)

                    def keep_x(c, m):
                        dve.wait_ge(x_ready, c * EB + m + 1)
                        dve.tensor_copy(pad[:, m, c * CH + TAPS - 1:(c + 1) * CH + TAPS - 1],
                                        psum[:, m, :]).then_inc(x_free, 1)

                    for c in range(BCH - 1):
                        for m in range(EB):
                            keep_x(c, m)
                    dve.wait_ge(padded, 1)
                    for m in range(EB):
                        keep_x(BCH - 1, m)
                        dve.wait_ge(x_free, EB + (BCH - 1) * EB + m + 1)
                        for j in range(TAPS):
                            if j == 0:
                                dve.tensor_scalar(dx[:, m, :], pad[:, m, 0:S], w_conv[:, m, 0:1], None,
                                                  ALU.mult).then_inc(conv_step, 1)
                            else:
                                dve.wait_ge(conv_step, m * TAPS + j)
                                dve.scalar_tensor_tensor(out=dx[:, m, :], in0=pad[:, m, j:j + S],
                                                         scalar=w_conv[:, m, j:j + 1], in1=dx[:, m, :],
                                                         op0=ALU.mult, op1=ALU.add).then_inc(conv_step, 1)
                    with dve.Fori(0, BCH) as c:
                        dve.wait_ge(xd_ready, c + 1)
                        dve.tensor_copy(low[:, tok(c)], psum[0:steps, c, :]).then_inc(low_ready, 1)
                        v = psum[BC0:XD, c, :]
                        dve.tensor_copy(parts[0:32, tok(c)], v).then_inc(split_step, 1)
                        dve.wait_ge(split_step, c * 4 + 1)
                        dve.tensor_tensor(rest, v, parts[0:32, tok(c)], ALU.subtract)\
                           .then_inc(split_step, 1)
                        dve.wait_ge(split_step, c * 4 + 2)
                        dve.tensor_copy(mid, rest).then_inc(split_step, 1)
                        dve.wait_ge(split_step, c * 4 + 3)
                        dve.tensor_copy(parts[32:64, tok(c)], mid)
                        dve.tensor_tensor(parts[64:96, tok(c)], rest, mid, ALU.subtract)\
                           .then_inc(split_step, 1)
                        dve.wait_ge(split_step, c * 4 + 4)
                    with dve.Fori(0, BCH) as c:
                        for m in range(EB):
                            dve.wait_ge(soft_done, c * EB + m + 1)
                            dve.tensor_tensor(dt[:, m, tok(c)], dt[:, m, tok(c)], relu[:, m, tok(c)],
                                              ALU.add).then_inc(dt_ready, 1)
                            dve.wait_ge(dt_ready, c * EB + m + 1)
                            dve.tensor_tensor(dx[:, m, tok(c)], dt[:, m, tok(c)], u[:, m, tok(c)],
                                              ALU.mult).then_inc(dx_ready, 1)
                    dve.wait_ge(saved, 1)
                    with dve.Fori(0, BCH) as c:
                        c_first = c * (EB * NS)

                        def weigh(e, n):
                            i = c_first + e * NS + n
                            dve.wait_ge(scanned, 1 + i + 1)
                            dve.wait_ge(saved, 1 + i + 1)
                            dve.wait_ge(bc_ready, 1 + c * (2 * NS) + 2 * n + 2)
                            dve.wait_ge(hc_used, 1 + c_first + max(e * NS + n - 1, 0))
                            dve.tensor_tensor(hc[:, n % 2, :], psum[:, n % 4, :], bc[:, 2 * n + 1, :],
                                              ALU.mult).then_inc(hc_ready, 1)

                        def finish_block(e):
                            dve.wait_ge(hc_used, 1 + c_first + (e + 1) * NS)
                            dve.scalar_tensor_tensor(out=dx[:, e, tok(c)], in0=u[:, e, tok(c)],
                                                     scalar=cols[:, 2, e:e + 1], in1=psum[:, 4 + e % 2, :],
                                                     op0=ALU.mult, op1=ALU.add).then_inc(y_sum, 1)
                            dve.wait_ge(y_sum, c * EB + e + 1)
                            dve.tensor_tensor(dx[:, e, tok(c)], dx[:, e, tok(c)], gate[:, e, tok(c)], ALU.mult)\
                               .then_inc(y_ready, 1)

                        for e in range(EB):
                            for n in range(NS):
                                i = c_first + e * NS + n
                                dve.wait_ge(decay_ready, i + 1)
                                dve.wait_ge(dbu_ready, 1 + i + 1)
                                dve.tensor_tensor_scan(psum[:, n % 4, :], psum[:, n % 4, :],
                                                       dbu[:, n % 4, :], state[:, e * NS + n:e * NS + n + 1],
                                                       ALU.mult, ALU.add).then_inc(scanned, 1)
                                if n or e:
                                    weigh(e if n else e - 1, (n - 1) % NS)
                                if n == 3 and e:
                                    finish_block(e - 1)
                        weigh(EB - 1, NS - 1)
                        finish_block(EB - 1)
                        dve.wait_ge(saved, c_first + EB * NS + 1)
                    for c in range(BCH):
                        for m in range(KD):
                            dve.wait_ge(out_ready, c * KD + m + 1)
                            if x_out is None:
                                dve.tensor_tensor(flipped(xn, m, c), psum[:, 6 + m, :],
                                                  flipped(res, m, c), ALU.add).then_inc(out_free, 1)
                            else:
                                dve.tensor_tensor(ysum, psum[:, 6 + m, :], flipped(res, m, c),
                                                  ALU.add).then_inc(out_free, 1)
                                dve.wait_ge(out_free, KD + c * KD + m + 1)
                                dve.tensor_tensor(flipped(x_out, m, c), flipped(x_out, m, c), ysum,
                                                  ALU.add).then_inc(stored, 1)
                                dve.wait_ge(stored, c * KD + m + 1)

                @block.scalar
                def _(act):
                    for sem in (bc_ready,):
                        act.sem_inc(sem, 1)
                    act.sem_inc(z_free, EB)
                    act.sem_inc(dtp_free, EB)
                    act.wait_ge(loaded, N_W)
                    if b == 0:
                        act.activation(a_neg[:], a_log[:], ACT.Exp).then_inc(a_ready, 1)
                    with act.Fori(0, BCH) as c:
                        for m in range(EB):
                            act.wait_ge(z_ready, c * EB + m + 1)
                            act.activation(gate[:, m, tok(c)], psum[:, EB + m, :], ACT.Silu).then_inc(z_free, 1)
                    for m in range(EB):
                        act.wait_ge(conv_step, (m + 1) * TAPS)
                        act.activation(u[:, m, :], dx[:, m, :], ACT.Silu, bias=cols[:, 0, m:m + 1])\
                           .then_inc(u_ready, 1)
                    with act.Fori(0, BCH) as c:
                        for m in range(EB):
                            act.wait_ge(dtp_ready, c * EB + m + 1)
                            act.activation(dt[:, m, tok(c)], psum[:, 4 + m, :], ACT.Abs,
                                           bias=cols[:, 1, m:m + 1])
                            act.activation(relu[:, m, tok(c)], psum[:, 4 + m, :], ACT.Relu,
                                           bias=cols[:, 1, m:m + 1]).then_inc(dtp_free, 1)
                    act.wait_ge(dtp_free, EB + BCH * EB)
                    act.activation(dt, dt, ACT.Exp, scale=-1.0).then_inc(exp_done, 1)
                    act.wait_ge(exp_done, 1)
                    with act.Fori(0, BCH) as c:
                        for m in range(EB):
                            act.activation(dt[:, m, tok(c)], dt[:, m, tok(c)], ACT.Ln,
                                           bias=one[:, 0:1]).then_inc(soft_done, 1)
                    if b == 0:
                        act.wait_ge(a_ready, 2)
                    act.wait_ge(dt_ready, BCH * EB)
                    with act.Fori(0, BCH) as c:

                        def keep_state(i, bank):
                            act.wait_ge(scanned, 1 + c * (EB * NS) + i + 1)
                            act.sem_inc(act_turn, 1)
                            act.activation(state[:, bass.ds(i, 1)], psum[:, bank, CH - 1:CH], ACT.Copy)\
                               .then_inc(saved, 1)

                        def decay(e, n):
                            i0 = c * (EB * NS) + e * NS
                            act.wait_ge(hc_ready, i0 + n + 1)
                            act.sem_inc(act_turn, 1)
                            act.activation(psum[:, n % 4, :], dt[:, e, tok(c)], ACT.Exp,
                                           scale=a_neg[:, bass.ds(e * NS + n, 1)]).then_inc(decay_ready, 1)

                        def keep_rows(n):
                            for j in (2 * n, 2 * n + 1):
                                used = hc_used if j % 2 else dbu_ready
                                act.wait_ge(used, 1 + c * ((EB - 1) * NS + n + 1))
                                act.wait_ge(stage_ready, c * 2 * NS + j + 1)
                                act.activation(bc[:, j, :], psum[:, 6 + j % 2, :], ACT.Copy).then_inc(bc_ready, 1)

                        for n in range(AHEAD):
                            keep_rows(n)
                        for n in range(NS):
                            if n >= 3:
                                keep_state(n - 3, (n - 3) % 4)
                            if n + AHEAD < NS:
                                keep_rows(n + AHEAD)
                            decay(0, n)
                        with act.Fori(0, EB - 1) as e1:
                            for n in range(NS):
                                keep_state(e1 * NS + (NS + n - 3), (n - 3) % 4)
                                decay(e1 + 1, n)
                        for n in range(NS - 3, NS):
                            keep_state((EB - 1) * NS + n, n % 4)

                @block.gpsimd
                def _(pool):
                    for sem in (dbu_ready,):
                        pool.sem_inc(sem, 1)
                    pool.wait_ge(dx_ready, BCH * EB)
                    with pool.Fori(0, BCH) as c, pool.Fori(0, EB) as e:
                        i0 = c * (EB * NS) + e * NS
                        for n in range(NS):
                            pool.wait_ge(bc_ready, 1 + c * (2 * NS) + 2 * n + 1)
                            pool.wait_ge(scanned, 1 + i0 + max(n - 3, 0))
                            pool.sem_inc(turn, 1)
                            pool.tensor_tensor(dbu[:, n % 4, :], dx[:, e, tok(c)], bc[:, 2 * n, :],
                                               ALU.mult).then_inc(dbu_ready, 1)


H = 16
HD = D // H
SK = 64
QT = S // P
HB = P // HD
PAIRS = H // 2


def cross_attention(core, consts, name, h, x, causal):
    dram = core.dram
    with core.scope() as s:
        w = s.sb("w", [P, 4, KD, D])
        bias = s.sb("bias", [P, 3, KD])
        v_bias = s.sb("v_bias", [1, D])
        key_mask = s.sb("key_mask", [1, B, SK])
        ctx = s.sb("ctx", [P, KD, B, 2, SK])
        shifted = s.sb("shifted", [P, 2, H * SK])
        late_f = shifted[:, 0, 0:QT * SK].rearrange("p (t s) -> p t s", t=QT)
        loaded = s.sem("loaded")
        norm(core, consts, x, h, True,
             prefetch=[(w[:], dram[name + "_w"], loaded), (bias[:], dram[name + "_bias"], loaded),
                       (v_bias[:], dram[name + "_v_bias"], loaded), (key_mask[:], dram["key_mask"], loaded),
                       (late_f, dram["late"], loaded)]
             + [(ctx[:, :, b, copy, :], dram["ctxT"][:, :, b, :], loaded) for b in range(B) for copy in range(2)])
        q = s.sb("q", [P, KD, T])
        o = s.sb("o", [P, KD, T])
        keys = s.sb("keys", [P, KD, B * SK])
        kd = s.sb("kd", [P, B, KD, HB, SK])
        vd = s.sb("vd", [P, B, PAIRS, 2 * HD + 2])
        neg4 = s.sb("neg4", [1, P])
        ones_row = s.sb("ones_row", [1, P])
        qs = s.sb("qs", [P, 2, KD, P])
        nmax = s.sb("nmax", [P, 2, H])
        probs = s.sb("probs", [P, 2, H * SK])
        probs_t = s.sb("probs_t", [P, 2, PAIRS, P])
        rden = s.sb("rden", [P, 2, PAIRS, 2])
        on = s.sb("on", [P, 2, D])
        late = s.sb("late", [P, QT, SK], BF16)
        scores = s.psum("scores", [P, 2, 2, CH])
        turned = s.psum("turned", [P, PAIRS, P])
        mixed = s.psum("mixed", [P, CH])
        turned_o = s.psum("turned_o", [P, CH])
        banks = scores[:].rearrange("p u c t -> p (u c) t")

        made = s.sem("made")
        q_ready, q_free = s.sem("q_ready"), s.sem("q_free")
        k_ready, k_stored, kd_ready = s.sem("k_ready"), s.sem("k_stored"), s.sem("kd_ready")
        v_ready, vd_ready = s.sem("v_ready"), s.sem("vd_ready")
        qs_ready, scored, maxed, moved = s.sem("qs_ready"), s.sem("scored"), s.sem("maxed"), s.sem("moved")
        probs_ready, turned_ready, pt_ready = s.sem("probs_ready"), s.sem("turned_ready"), s.sem("pt_ready")
        mixed_ready, rden_ready, on_ready = s.sem("mixed_ready"), s.sem("rden_ready"), s.sem("on_ready")
        ot_ready, ot_stored = s.sem("ot_ready"), s.sem("ot_stored")
        out_ready, out_free, turn, gap = s.sem("out_ready"), s.sem("out_free"), s.sem("turn"), s.sem("gap")
        block = s.block()
        NT = B * QT
        N_LOAD = (5 + 2 * B) * 16

        @block.tensor
        def _(pe):
            for sem in (scored,):
                pe.sem_inc(sem, 1)
            pe.wait_ge(loaded, N_LOAD)
            for m in range(KD):
                for k in range(KD):
                    mm = pe.matmul(turned[:, m, :], w[:, 1, k, m * P:(m + 1) * P], ctx[:, k, :, 0, :],
                                   start=(k == 0), stop=(k == KD - 1))
            mm.then_inc(k_ready, 1)
            pe.wait_ge(made, 2)
            for b in range(B):
                for k in range(KD):
                    pe.matmul(mixed[:, b * D:(b + 1) * D], ctx[:, k, b, :, :].rearrange("p c s -> p (c s)"),
                              w[:, 2, k, :], start=(k == 0), stop=False)
                mm = pe.matmul(mixed[:, b * D:(b + 1) * D], ones_row[:], v_bias[:], start=False, stop=True)
            mm.then_inc(v_ready, 1)
            with pe.Fori(0, NCH // 2) as c2:
                for j in range(2):
                    for m in range(KD):
                        pe.wait_ge(q_free, c2 * 4 + 2 * j + m + 1)
                        for k in range(KD):
                            mm = pe.matmul(banks[:, 2 * j + m, :], w[:, 0, k, m * P:(m + 1) * P],
                                           h[:, k, bass.ds(c2 * 2 * CH + j * CH, CH)],
                                           start=(k == 0), stop=(k == KD - 1))
                        mm.then_inc(q_ready, 1)
            pe.wait_ge(q_free, 4 + KD * NCH)
            pe.wait_ge(kd_ready, B * KD)
            pe.wait_ge(made, 3)
            pe.wait_ge(vd_ready, B)
            with pe.Fori(0, B) as b:

                def score(i):
                    u = i % 2
                    pe.wait_ge(qs_ready, b * QT + i + 1)
                    pe.wait_ge(moved, 1 + b * QT + max(i - 1, 0))
                    for hb in range(KD):
                        pe.matmul(scores[:, u, hb, :], qs[:, u, hb, :], kd[:, b, hb, :, :],
                                  start=True, stop=False)
                        if causal:
                            mm = pe.matmul(scores[:, u, hb, :], consts["identb"][:],
                                           late[:, i, :].unsqueeze(1).to_broadcast([P, HB, SK]),
                                           start=False, stop=True)
                        else:
                            mm = pe.matmul(scores[:, u, hb, :], neg4[:],
                                           key_mask[:, b, :].unsqueeze(1).to_broadcast([1, HB, SK]),
                                           start=False, stop=True)
                    mm.then_inc(scored, 1)

                def mix(i):
                    pe.wait_ge(pt_ready, 1 + b * QT + i + 1)
                    pe.wait_ge(on_ready, 1 + b * QT + i)
                    for j in range(PAIRS):
                        mm = pe.matmul(mixed[:, j * (2 * HD + 2):(j + 1) * (2 * HD + 2)],
                                       probs_t[:, i % 2, j, :], vd[:, b, j, :], start=True, stop=True)
                    mm.then_inc(mixed_ready, 1)

                def turn_weights(i):
                    pe.wait_ge(probs_ready, b * QT + i + 1)
                    pe.wait_ge(pt_ready, 1 + b * QT + i)
                    pe.sem_inc(gap, 1)
                    for j in range(PAIRS):
                        mm = pe.transpose(turned[:, j, :], probs[:, i % 2, j * P:(j + 1) * P], consts["ident"][:])
                    mm.then_inc(turned_ready, 1)

                def turn_out(i):
                    pe.wait_ge(on_ready, 1 + b * QT + i + 1)
                    pe.wait_ge(ot_stored, 1 + b * QT + i)
                    pe.sem_inc(gap, 1)
                    for k in range(KD):
                        mm = pe.transpose(turned_o[:, k * P:(k + 1) * P], on[:, i % 2, k * P:(k + 1) * P],
                                          consts["ident"][:])
                    mm.then_inc(ot_ready, 1)

                for i in range(QT + 2):
                    if i < QT:
                        score(i)
                    if i >= 2:
                        mix(i - 2)
                    if 1 <= i <= QT:
                        turn_weights(i - 1)
                    if i >= 2:
                        turn_out(i - 2)
            pe.wait_ge(ot_stored, 1 + NT)
            with pe.Fori(0, NCH // 2) as c2:
                for j in range(2):
                    for m in range(KD):
                        pe.wait_ge(out_free, c2 * 4 + 2 * j + m + 1)
                        for k in range(KD):
                            mm = pe.matmul(banks[:, 2 * j + m, :], w[:, 3, k, m * P:(m + 1) * P],
                                           o[:, k, bass.ds(c2 * 2 * CH + j * CH, CH)],
                                           start=(k == 0), stop=(k == KD - 1))
                        mm.then_inc(out_ready, 1)

        @block.vector
        def _(dve):
            for sem in (moved, on_ready):
                dve.sem_inc(sem, 1)
            dve.memset(neg4[:], -4e12).then_inc(made, 1)
            dve.memset(ones_row[:], 1.0).then_inc(made, 1)
            dve.wait_ge(loaded, N_LOAD)
            dve.tensor_copy(late[:], late_f).then_inc(made, 1)
            dve.sem_inc(out_free, 4)
            dve.wait_ge(k_stored, KD)
            for b in range(B):
                for hb in range(KD):
                    dve.tensor_tensor(kd[:, b, hb, :, :],
                                      keys[:, hb, b * SK:(b + 1) * SK].unsqueeze(1).to_broadcast([P, HB, SK]),
                                      consts["head_mask"][:].unsqueeze(2).to_broadcast([P, HB, SK]),
                                      ALU.mult).then_inc(kd_ready, 1)
            dve.wait_ge(v_ready, 1)
            for b in range(B):
                dve.tensor_copy(vd[:, b, :, 2 * HD:2 * HD + 2],
                                consts["pair_mask"][:].unsqueeze(1).to_broadcast([P, PAIRS, 2]))
                for j in range(2):
                    last = dve.tensor_scalar(
                        vd[:, b, :, j * HD:(j + 1) * HD],
                        mixed[:, b * D:(b + 1) * D].rearrange("p (g j e) -> p g j e", j=2, e=HD)[:, :, j, :],
                        consts["pair_mask"][:, j:j + 1], None, ALU.mult)
                last.then_inc(vd_ready, 1)
            with dve.Fori(0, B) as b:

                def shift(i):
                    u = i % 2
                    sc = scores[:, u, :, :].rearrange("p c (h s) -> p (c h) s", s=SK)
                    dve.wait_ge(scored, 1 + b * QT + i + 1)
                    dve.tensor_reduce(nmax[:, u, :], sc, AX.X, ALU.max, negate=True).then_inc(maxed, 1)
                    dve.wait_ge(maxed, b * QT + i + 1)
                    dve.tensor_tensor(shifted[:, u, :].rearrange("p (h s) -> p h s", s=SK), sc,
                                      nmax[:, u, :].unsqueeze(2).to_broadcast([P, H, SK]),
                                      ALU.add).then_inc(moved, 1)

                def divide(i):
                    u = i % 2
                    dve.wait_ge(mixed_ready, b * QT + i + 1)
                    mx = mixed[:, 0:PAIRS * (2 * HD + 2)].rearrange("p (g e) -> p g e", g=PAIRS)
                    dve.reciprocal(rden[:, u, :, :], mx[:, :, 2 * HD:2 * HD + 2]).then_inc(rden_ready, 1)
                    dve.wait_ge(rden_ready, b * QT + i + 1)
                    for j in range(2):
                        last = dve.tensor_tensor(
                            on[:, u, :].rearrange("p (g j e) -> p g j e", j=2, e=HD)[:, :, j, :],
                            mx[:, :, j * HD:(j + 1) * HD],
                            rden[:, u, :, j:j + 1].to_broadcast([P, PAIRS, HD]), ALU.mult)
                    last.then_inc(on_ready, 1)

                for i in range(QT + 2):
                    if i < QT:
                        shift(i)
                    if i >= 2:
                        divide(i - 2)
            with dve.Fori(0, NCH // 2) as c2:
                for j in range(2):
                    for m in range(KD):
                        dve.wait_ge(out_ready, c2 * 4 + 2 * j + m + 1)
                        xs = x[:, m, bass.ds(c2 * 2 * CH + j * CH, CH)]
                        dve.scalar_tensor_tensor(out=xs, in0=banks[:, 2 * j + m, :], scalar=bias[:, 2, m:m + 1],
                                                 in1=xs, op0=ALU.add, op1=ALU.add).then_inc(out_free, 1)

        @block.scalar
        def _(act):
            for sem in (pt_ready, ot_stored):
                act.sem_inc(sem, 1)
            act.sem_inc(q_free, 4)
            act.wait_ge(k_ready, 1)
            for m in range(KD):
                act.activation(keys[:, m, :], turned[:, m, :], ACT.Identity, bias=bias[:, 1, m:m + 1])\
                   .then_inc(k_stored, 1)
            with act.Fori(0, NCH // 2) as c2:
                for j in range(2):
                    for m in range(KD):
                        act.wait_ge(q_ready, c2 * 4 + 2 * j + m + 1)
                        act.activation(q[:, m, bass.ds(c2 * 2 * CH + j * CH, CH)], banks[:, 2 * j + m, :],
                                       ACT.Identity, bias=bias[:, 0, m:m + 1]).then_inc(q_free, 1)
            with act.Fori(0, B) as b:
                for i in range(QT + 2):
                    if i < QT:
                        act.wait_ge(moved, 1 + b * QT + i + 1)
                        act.activation(probs[:, i % 2, :], shifted[:, i % 2, :], ACT.Exp, scale=HD ** -0.5)\
                           .then_inc(probs_ready, 1)
                    if 1 <= i <= QT:
                        act.wait_ge(turned_ready, b * QT + i)
                        act.activation(probs_t[:, (i - 1) % 2, :, :], turned[:], ACT.Copy).then_inc(pt_ready, 1)
                    if i >= 2:
                        act.wait_ge(ot_ready, b * QT + i - 1)
                        act.activation(o[:, :, bass.ds(b * S + (i - 2) * P, P)],
                                       turned_o[:, 0:KD * P].rearrange("p (k t) -> p k t", k=KD),
                                       ACT.Copy).then_inc(ot_stored, 1)

        @block.gpsimd
        def _(pool):
            pool.wait_ge(q_free, 4 + KD * NCH)
            with pool.Fori(0, B) as b:
                for i in range(QT):
                    pool.wait_ge(scored, 1 + b * QT + max(i - 1, 0))
                    pool.sem_inc(turn, 1)
                    pool.tensor_copy(qs[:, i % 2, :, :], q[:, :, bass.ds(b * S + i * P, P)]).then_inc(qs_ready, 1)


HH = 4
PARTS = 3
QPARTS, KPARTS = (0, 0, 0, 1, 1, 2), (0, 1, 2, 0, 1, 0)
STACK = len(QPARTS) * HD
VW = HD + 1
E = 8
F = 1024
FB = F // P


def self_attention(core, consts, h, res, lns):
    dram = core.dram
    with core.scope() as s:
        w_qk = s.sb("w_qk", [P, KD, 2 * D])
        w_v = s.sb("w_v", [P, KD, D])
        w_o = s.sb("w_o", [P, KD, D])
        late = s.sb("late", [P, 2, P])
        loaded = s.sem("loaded")
        norm(core, consts, res, h, True, weight=lns[:, 0, :], bias=lns[:, 1, :],
             prefetch=[(t[:], dram[key], loaded)
                       for t, key in ((w_qk, "a0_qk"), (w_v, "a0_v"), (w_o, "a0_o"), (late, "tri"))])
        lateb = s.sb("lateb", [P, 2, P], BF16)
        parts = s.sb("parts", [P, 2, PARTS, 4, CH], BF16)
        rest = s.sb("rest", [P, 2, CH])
        v = s.sb("v", [P, B * QT, H, VW])
        vs = s.sb("vs", [P, B * QT, HH, VW])
        stack = s.sb("stack", [STACK + PARTS, HH, 2, T], BF16)
        umax = s.sb("umax", [P, 2, 12])
        row = s.sb("row", [QT, 2, PARTS, P], BF16)
        row_rest = s.sb("row_rest", [QT, P])
        probs = s.sb("probs", [P, 4, CH])
        ot = s.sb("ot", [VW, 2, S])
        rden = s.sb("rden", [P, 2, QT, 1])
        on = s.sb("on", [P, B * QT, H, HD])
        banks = s.psum("banks", [P, 8, CH])
        o = h

        ready, split, split2, split3 = (s.sem("ready"), s.sem("split"), s.sem("split2"),
                                                s.sem("split3"))
        parts_stored = [s.sem("parts_stored0"), s.sem("parts_stored1")]
        v_ready, v_free, made = (s.sem("v_ready"), s.sem("v_free"),
                                               s.sem("made"))
        stack_ready = [s.sem(f"stack_ready{j}") for j in range(HH)]
        stack_used, vs_ready, row_split = s.sem("stack_used"), s.sem("vs_ready"), s.sem("row_split")
        max_ready, max_read, unit_max, maxed = (s.sem("max_ready"), s.sem("max_read"), s.sem("unit_max"),
                                                s.sem("maxed"))
        turned, row_ready = s.sem("turned"), s.sem("row_ready")
        row_stored = [s.sem("row_stored0"), s.sem("row_stored1")]
        scored, exp_done, pv_done, ot_copied = s.sem("scored"), s.sem("exp_done"), s.sem("pv_done"), s.sem("ot_copied")
        o_ready, rden_ready, normed = s.sem("o_ready"), s.sem("rden_ready"), s.sem("normed")
        ot_ready, ot_stored, out_ready, out_free = (s.sem("ot_ready"), s.sem("ot_stored"), s.sem("out_ready"),
                                                    s.sem("out_free"))
        gap, sp_gap, pool_gap = s.sem("gap"), s.sem("sp_gap"), s.sem("pool_gap")
        qk_d = core.nc.dram_tensor("qk_parts", (2, PARTS, H, HD, T), BF16, kind="Internal").ap()
        block = s.block()
        MAX_UNITS = [(t, 0) for t in range(QT)] + [(t, 1) for t in range(4, QT)]
        UNITS = [(t, 0) for t in range(4)] + [(t, 1) for t in range(QT)]
        NU = len(UNITS)
        NN = HH * B
        NTURN = H // HH
        STORES = 2 * PARTS * KD * 16

        @block.sync
        def _(sp):
            for c in range(NCH):
                sp.wait_ge(split3, 4 * c + 5)
                for which in range(2):
                    for part in range(PARTS):
                        for k in range(KD):
                            sp.dma_start(
                                qk_d[which, part, k * HB:(k + 1) * HB, :, c * CH:(c + 1) * CH]
                                .rearrange("h e t -> (h e) t"),
                                parts[:, c % 2, part, which * KD + k, :]).then_inc(parts_stored[c % 2], 16)
            for stored in parts_stored:
                sp.wait_ge(stored, NCH // 2 * STORES)
            sp.wait_ge(made, 3)

            def load_stack(g, j):
                sp.wait_ge(stack_used, g * HH + j + 1)
                for which, order in ((0, QPARTS), (1, KPARTS)):
                    for r, part in enumerate(order):
                        sp.dma_start(stack[r * HD:(r + 1) * HD, j % HH, which, :],
                                     qk_d[which, part, bass.ds(g * HH + j, 1), :, :]
                                     .rearrange("h e t -> (h e) t")).then_inc(stack_ready[j % HH], 16)

            def store_rows(g, j):
                for b in range(B):
                    n = j * B + b
                    sp.wait_ge(row_ready, 1 + g * NN + n + 1)
                    sp.sem_inc(sp_gap, 1)
                    for part in range(PARTS):
                        sp.dma_start(stack[STACK + part:STACK + part + 1, j, 0, b * S:(b + 1) * S],
                                     row[:, n % 2, part, :]).then_inc(row_stored[n % 2], 16)

            load_stack(0, 0)
            with sp.Fori(0, NTURN - 1) as g:
                for j in range(HH):
                    load_stack(g, j + 1)
                    store_rows(g, j)
            for j in range(HH):
                if j + 1 < HH:
                    load_stack(NTURN - 1, j + 1)
                store_rows(NTURN - 1, j)

        @block.tensor
        def _(pe):
            for sem in (max_ready, scored, turned, pv_done, o_ready):
                pe.sem_inc(sem, 1)
            pe.sem_inc(stack_used, HH)
            pe.wait_ge(loaded, 4 * 16)
            for c in range(NCH):
                for m in range(4):
                    pe.wait_ge(split2, c * 4 + m + 1)
                    for k in range(KD):
                        mm = pe.matmul(banks[:, m, :], w_qk[:, k, m * P:(m + 1) * P], h[:, k, tok(c)],
                                       start=(k == 0), stop=(k == KD - 1))
                    mm.then_inc(ready, 1)
            for t in range(B * QT):
                if t >= 4:
                    pe.wait_ge(v_free, t - 3)
                for k in range(KD):
                    mm = pe.matmul(banks[:, 4 + t % 4, 0:D], h[:, k, t * P:(t + 1) * P], w_v[:, k, :],
                                   start=(k == 0), stop=(k == KD - 1))
                mm.then_inc(v_ready, 1)
            pe.wait_ge(v_free, B * QT)
            pe.wait_ge(split2, 4 + NCH * 4)
            pe.wait_ge(made, 3)


            def turn_of_heads(g, last):
                def max_unit(n, u):
                    j, b = n // B % HH, n % B
                    t, half = MAX_UNITS[u]
                    if u == 0 and b == 0:
                        pe.wait_ge(stack_ready[j], (g + n // NN + 1) * (12 * 16))
                    pe.wait_ge(max_read, g * (NN * NU) + n * NU + u)
                    w = min((t + 1) * P - half * CH, CH)
                    bank = banks[:, u % 2, :]
                    mm = pe.matmul(bank[:, 0:w], stack[0:STACK, j, 0, b * S + t * P:b * S + (t + 1) * P],
                                   stack[0:STACK, j, 1, b * S + half * CH:b * S + half * CH + w],
                                   start=True, stop=True)
                    if t // 4 == half:
                        mm = pe.matmul(bank[:, w - P:w], consts["identb"][:], lateb[:, 0, :], start=False,
                                       stop=True, skip_group_check=True)
                    mm.then_inc(max_ready, 1)

                def turn_max(n):
                    pe.wait_ge(maxed, g * NN + n + 1)
                    pe.wait_ge(row_ready, 1 + g * NN + n)
                    pe.sem_inc(gap, 1)
                    pe.transpose(banks[0:QT, 7, 0:P], umax[:, n % 2, 0:QT], consts["ident"][:])\
                      .then_inc(turned, 1)

                def weight_unit(n, u):
                    j, b = n // B, n % B
                    t, half = UNITS[u]
                    if u == 0:
                        pe.wait_ge(row_stored[n % 2], (g * (NN // 2) + n // 2 + 1) * (PARTS * 16))
                    pe.wait_ge(exp_done, g * (NN * NU) + n * NU + u)
                    q0 = max(t * P, half * CH)
                    w = (half + 1) * CH - q0
                    bank = banks[:, 2 + u % 2, :]
                    mm = pe.matmul(bank[:, 0:w], stack[:, j, 1, b * S + t * P:b * S + (t + 1) * P],
                                   stack[:, j, 0, b * S + q0:b * S + q0 + w], start=True, stop=True)
                    if t // 4 == half:
                        mm = pe.matmul(bank[:, 0:P], consts["identb"][:], lateb[:, 1, :], start=False, stop=True,
                                       skip_group_check=True)
                    mm.then_inc(scored, 1)

                def mix_unit(n, u):
                    j, b = n // B, n % B
                    t, half = UNITS[u]
                    if u == 0:
                        pe.wait_ge(ot_copied, 1 + g * (2 * NN) + 2 * n)
                        if n == 0:
                            pe.wait_ge(vs_ready, g + 1)
                    pe.wait_ge(exp_done, 1 + g * (NN * NU) + n * NU + u + 1)
                    q0 = max(t * P, half * CH)
                    w = (half + 1) * CH - q0
                    pe.matmul(banks[0:VW, 4 + half, CH - w:CH], vs[:, b * QT + t, j, :], probs[:, u % 4, 0:w],
                              start=(t == 0), stop=(t == 4 * half + 3)).then_inc(pv_done, 1)

                def turn_out(n):
                    pe.wait_ge(ot_copied, 1 + g * (2 * NN) + 2 * n + 2)
                    pe.wait_ge(normed, 1 + g * NN + n)
                    pe.sem_inc(gap, 1)
                    for t in range(QT):
                        mm = pe.transpose(banks[:, 6, t * VW:(t + 1) * VW], ot[:, n % 2, t * P:(t + 1) * P],
                                          consts["ident"][0:VW, 0:VW])
                    mm.then_inc(o_ready, 1)

                if g is None:
                    g = 0
                    for n in range(2):
                        for u in range(NU):
                            max_unit(n, u)
                        turn_max(n)
                    return
                for n in range(NN):
                    ahead = n + 2 < NN or not last
                    for u in range(NU):
                        weight_unit(n, u)
                        if ahead:
                            max_unit(n + 2, u)
                        if u == 2 and n:
                            turn_out(n - 1)
                        if u:
                            mix_unit(n, u - 1)
                    mix_unit(n, NU - 1)
                    if n % B == B - 1:
                        pe.wait_ge(pv_done, 1 + g * (NN * NU) + (n + 1) * NU)
                        pe.sem_inc(stack_used, 1)
                    if ahead:
                        turn_max(n + 2)
                turn_out(NN - 1)

            turn_of_heads(None, False)
            with pe.Fori(0, NTURN - 1) as g:
                turn_of_heads(g, False)
            turn_of_heads(NTURN - 1, True)
            pe.wait_ge(normed, 1 + NTURN * NN)
            for t in range(B * QT):
                bank = banks[:, t // 2 % 4, :]
                if t % 2 == 0 and t >= 8:
                    pe.wait_ge(ot_stored, t // 2 - 3)
                for k in range(KD):
                    mm = pe.transpose(bank[:, (t % 2 * KD + k) * P:(t % 2 * KD + k + 1) * P],
                                      on[:, t, k * HB:(k + 1) * HB, :].rearrange("p h e -> p (h e)"),
                                      consts["ident"][:])
                mm.then_inc(ot_ready, 1)
            pe.wait_ge(ot_stored, B * QT // 2)
            with pe.Fori(0, NCH // 2) as c2:
                for j in range(2):
                    for m in range(KD):
                        pe.wait_ge(out_free, c2 * 4 + 2 * j + m + 1)
                        for k in range(KD):
                            mm = pe.matmul(banks[:, 2 * j + m, :], w_o[:, k, m * P:(m + 1) * P],
                                           o[:, k, bass.ds(c2 * 2 * CH + j * CH, CH)],
                                           start=(k == 0), stop=(k == KD - 1))
                        mm.then_inc(out_ready, 1)

        @block.vector
        def _(dve):
            for sem in (max_read, row_ready, normed):
                dve.sem_inc(sem, 1)
            dve.sem_inc(split2, 4)
            dve.sem_inc(out_free, 4)
            dve.memset(v[:, :, :, HD:VW], 1.0).then_inc(made, 1)
            dve.memset(stack[STACK:STACK + PARTS, :, 1, :], 1.0).then_inc(made, 1)
            dve.wait_ge(loaded, 4 * 16)
            dve.tensor_copy(lateb[:], late[:]).then_inc(made, 1)
            for c in range(NCH):
                for m in range(4):
                    scale = HD ** -0.5 if m < KD else 1.0
                    dve.wait_ge(split, c * 4 + m + 1)
                    dve.wait_ge(split3, c * 4 + max(m - 1, 0) + 1)
                    dve.scalar_tensor_tensor(out=rest[:, m % 2, :], in0=banks[:, m, :], scalar=scale,
                                             in1=parts[:, c % 2, 0, m, :], op0=ALU.mult, op1=ALU.subtract)\
                       .then_inc(split2, 1)
                    dve.wait_ge(split2, c * 4 + m + 5)
                    dve.tensor_copy(parts[:, c % 2, 1, m, :], rest[:, m % 2, :]).then_inc(unit_max, 1)
            for t in range(B * QT):
                dve.wait_ge(v_ready, t + 1)
                dve.tensor_copy(v[:, t, :, 0:HD], banks[:, 4 + t % 4, 0:D].rearrange("p (h e) -> p h e", h=H))\
                   .then_inc(v_free, 1)

            def turn_of_heads(g, last):
                def maxima(n, u):
                    t, half = MAX_UNITS[u]
                    w = min((t + 1) * P - half * CH, CH)
                    if u == 0:
                        dve.wait_ge(turned, g * NN + max(n, 1))
                    dve.wait_ge(max_ready, 1 + g * (NN * NU) + n * NU + u + 1)
                    dve.tensor_reduce(umax[:, n % 2, u:u + 1], banks[:, u % 2, 0:w], AX.X, ALU.max)\
                       .then_inc(max_read, 1)

                def finish_max(n):
                    dve.wait_ge(max_read, 1 + g * (NN * NU) + (n + 1) * NU)
                    dve.tensor_tensor(umax[:, n % 2, 4:8], umax[:, n % 2, 4:8], umax[:, n % 2, 8:12], ALU.max)\
                       .then_inc(maxed, 1)

                def store_row(n):
                    dve.wait_ge(turned, 1 + g * NN + n + 1)
                    if n >= 2:
                        dve.wait_ge(row_stored[n % 2], (g * (NN // 2) + n // 2) * (PARTS * 16))
                    low = banks[0:QT, 7, 0:P]
                    dve.tensor_scalar(row[:, n % 2, 0, :], low, -1.0, None, ALU.mult).then_inc(row_split, 1)
                    dve.wait_ge(row_split, (g * NN + n) * 3 + 1)
                    dve.scalar_tensor_tensor(out=row_rest[:], in0=low, scalar=-1.0, in1=row[:, n % 2, 0, :],
                                             op0=ALU.mult, op1=ALU.subtract).then_inc(row_split, 1)
                    dve.wait_ge(row_split, (g * NN + n) * 3 + 2)
                    dve.tensor_copy(row[:, n % 2, 1, :], row_rest[:]).then_inc(row_split, 1)
                    dve.wait_ge(row_split, (g * NN + n) * 3 + 3)
                    dve.tensor_tensor(row[:, n % 2, 2, :], row_rest[:], row[:, n % 2, 1, :], ALU.subtract)\
                       .then_inc(row_ready, 1)

                def norm_head(n):
                    j, b = n // B, n % B
                    m = banks[:, 6, 0:QT * VW].rearrange("p (t e) -> p t e", e=VW)
                    dve.wait_ge(o_ready, 1 + g * NN + n + 1)
                    dve.reciprocal(rden[:, n % 2, :, :], m[:, :, HD:VW]).then_inc(rden_ready, 1)
                    dve.wait_ge(rden_ready, g * NN + n + 1)
                    dve.tensor_tensor(on[:, b * QT:(b + 1) * QT, g * HH + j, :], m[:, :, 0:HD],
                                      rden[:, n % 2, :, :].to_broadcast([P, QT, HD]), ALU.mult).then_inc(normed, 1)

                if g is None:
                    g = 0
                    for n in range(2):
                        for u in range(NU):
                            maxima(n, u)
                        finish_max(n)
                        store_row(n)
                    return
                for n in range(NN):
                    if n + 2 < NN or not last:
                        for u in range(NU):
                            maxima(n + 2, u)
                            if u == 4 and n:
                                norm_head(n - 1)
                        finish_max(n + 2)
                        store_row(n + 2)
                    else:
                        norm_head(n - 1)
                norm_head(NN - 1)

            turn_of_heads(None, False)
            with dve.Fori(0, NTURN - 1) as g:
                turn_of_heads(g, False)
            turn_of_heads(NTURN - 1, True)
            with dve.Fori(0, NCH // 2) as c2:
                for j in range(2):
                    for m in range(KD):
                        dve.wait_ge(out_ready, c2 * 4 + 2 * j + m + 1)
                        r = res[:, m, bass.ds(c2 * 2 * CH + j * CH, CH)]
                        dve.tensor_tensor(r, banks[:, 2 * j + m, :], r, ALU.add).then_inc(out_free, 1)

        @block.scalar
        def _(act):
            for sem in (exp_done, ot_copied):
                act.sem_inc(sem, 1)
            for c in range(NCH):
                if c >= 2:
                    act.wait_ge(parts_stored[c % 2], c // 2 * STORES)
                for m in range(4):
                    act.wait_ge(ready, c * 4 + m + 1)
                    act.activation(parts[:, c % 2, 0, m, :], banks[:, m, :], ACT.Copy,
                                   scale=HD ** -0.5 if m < KD else 1.0).then_inc(split, 1)
            with act.Fori(0, NTURN) as g:

                def copy_out(n):
                    for half in range(2):
                        act.wait_ge(pv_done, 1 + g * (NN * NU) + n * NU + (4 if half == 0 else NU))
                        if n >= 2:
                            act.wait_ge(o_ready, 1 + g * NN + n - 1)
                        act.activation(ot[:, n % 2, half * CH:(half + 1) * CH], banks[0:VW, 4 + half, :], ACT.Copy)\
                           .then_inc(ot_copied, 1)

                for n in range(NN):
                    for u in range(NU):
                        t, half = UNITS[u]
                        w = (half + 1) * CH - max(t * P, half * CH)
                        act.wait_ge(scored, 1 + g * (NN * NU) + n * NU + u + 1)
                        act.wait_ge(pv_done, 1 + g * (NN * NU) + max(n * NU + u - 3, 0))
                        act.activation(probs[:, u % 4, 0:w], banks[:, 2 + u % 2, 0:w], ACT.Exp)\
                           .then_inc(exp_done, 1)
                        if u == 0 and n:
                            copy_out(n - 1)
                copy_out(NN - 1)
            for t2 in range(B * QT // 2):
                act.wait_ge(ot_ready, 2 * t2 + 2)
                act.activation(o[:, :, t2 * 2 * P:(t2 + 1) * 2 * P].rearrange("p k (t c) -> p t k c", t=2),
                               banks[:, t2 % 4, :].rearrange("p (t k c) -> p t k c", t=2, k=KD),
                               ACT.Copy).then_inc(ot_stored, 1)

        @block.gpsimd
        def _(pool):
            pool.sem_inc(split3, 1)
            for c in range(NCH):
                for m in range(4):
                    pool.wait_ge(unit_max, c * 4 + m + 1)
                    pool.tensor_tensor(parts[:, c % 2, 2, m, :], rest[:, m % 2, :], parts[:, c % 2, 1, m, :], ALU.subtract)\
                        .then_inc(split3, 1)
            pool.wait_ge(v_free, B * QT)
            with pool.Fori(0, NTURN) as g:
                pool.wait_ge(pv_done, 1 + g * (NN * NU))
                pool.sem_inc(pool_gap, 1)
                pool.tensor_copy(vs[:], v[:, :, bass.ds(g * HH, HH), :]).then_inc(vs_ready, 1)


def gates(core, consts, h, gate_t, prefetch):
    dram = core.dram
    with core.scope() as s:
        NT = B * QT
        w = s.sb("w", [P, KD, E])
        small = s.sb("small", [P, 8, NT, E])
        shifted, prob, rank, cmp, kept, gate, col = (small[:, n] for n in range(7))
        nmax, total, inv, top, top_inv = (col[:, :, n:n + 1] for n in range(5))
        logits = s.psum("logits", [P, CH])
        flat = s.psum("flat", [E, NCH, CH])
        loaded, ready, step, exp_done, flat_ready = (s.sem("loaded"), s.sem("ready"), s.sem("step"),
                                                     s.sem("exp_done"), s.sem("flat_ready"))
        block = s.block()
        lg = logits[:, 0:NT * E].rearrange("p (t e) -> p t e", e=E)

        @block.sync
        def _(sp):
            sp.dma_start(w[:], dram["moe_gate"]).then_inc(loaded, 16)
            for tile, array, sem in prefetch:
                sp.dma_start(tile, array).then_inc(sem, 16)

        @block.tensor
        def _(pe):
            pe.wait_ge(loaded, 16)
            for t in range(NT):
                for k in range(KD):
                    mm = pe.matmul(lg[:, t, :], h[:, k, t * P:(t + 1) * P], w[:, k, :],
                                   start=(k == 0), stop=(k == KD - 1))
            mm.then_inc(ready, 1)
            pe.wait_ge(ready, 2)
            for t in range(NT):
                mm = pe.transpose(flat[:, t // 4, t % 4 * P:(t % 4 + 1) * P], gate[:, t, :], consts["ident"][:])
            mm.then_inc(flat_ready, 1)

        @block.vector
        def _(dve):
            count = [0]

            def link(ins):
                count[0] += 1
                ins.then_inc(step, 1)
                dve.wait_ge(step, count[0])

            def wide(v):
                return v.to_broadcast([P, NT, E])

            dve.wait_ge(ready, 1)
            link(dve.tensor_reduce(nmax, lg, AX.X, ALU.max, negate=True))
            link(dve.tensor_tensor(shifted, lg, wide(nmax), ALU.add))
            dve.wait_ge(exp_done, 1)
            link(dve.tensor_reduce(total, prob, AX.X, ALU.add))
            link(dve.reciprocal(inv, total))
            link(dve.tensor_tensor(prob, prob, wide(inv), ALU.mult))
            link(dve.memset(rank, 0.0))
            for j in range(E):
                for lo, hi, op in ((0, j, ALU.is_gt), (j + 1, E, ALU.is_ge)):
                    if lo < hi:
                        link(dve.tensor_tensor(cmp[:, :, lo:hi], prob[:, :, j:j + 1].to_broadcast([P, NT, hi - lo]),
                                               prob[:, :, lo:hi], op))
                        link(dve.tensor_tensor(rank[:, :, lo:hi], rank[:, :, lo:hi], cmp[:, :, lo:hi], ALU.add))
            link(dve.scalar_tensor_tensor(out=kept, in0=rank, scalar=1.5, in1=prob, op0=ALU.is_lt, op1=ALU.mult))
            link(dve.tensor_reduce(top, kept, AX.X, ALU.add))
            link(dve.reciprocal(top_inv, top))
            dve.tensor_tensor(gate, kept, wide(top_inv), ALU.mult).then_inc(ready, 1)
            dve.wait_ge(flat_ready, 1)
            dve.tensor_copy(gate_t[:], flat[:].rearrange("e c t -> e (c t)"))

        @block.scalar
        def _(act):
            act.wait_ge(step, 2)
            act.activation(prob, shifted, ACT.Exp).then_inc(exp_done, 1)


def experts(core, consts, h, gate_t, res, x):
    dram = core.dram
    with core.scope() as s:
        w1 = s.sb("w1", [P, 2, KD, F])
        w2 = s.sb("w2", [P, 2, FB, D])
        pick = s.sb("pick", [E, 2, P])
        b1 = s.sb("b1", [P, 2, FB])
        b2 = s.sb("b2", [P, 2, KD])
        loaded = [s.sem("loaded0"), s.sem("loaded1")]
        EXPERT = ((w1, "moe_w1"), (w2, "moe_w2"), (pick, "moe_pick"), (b1, "moe_b1"), (b2, "moe_b2"))
        N_LOAD = len(EXPERT) * 16
        gates(core, consts, h, gate_t,
              [(t[:, u], dram[key][u], loaded[u]) for u in range(2) for t, key in EXPERT])
        hidden = s.sb("hidden", [P, 2, FB, CH])
        gate = s.sb("gate", [P, 2, CH])
        weighed = s.sb("weighed", [P, 2, KD, CH])
        up = s.psum("up", [P, 3, CH])
        down = s.psum("down", [P, 2, KD, CH])
        pg = s.psum("pg", [P, CH])
        done = s.sem("done")
        up_ready, hidden_ready = s.sem("up_ready"), s.sem("hidden_ready")
        pg_ready, gate_ready = s.sem("pg_ready"), s.sem("gate_ready")
        down_ready, weighed_ready, added = s.sem("down_ready"), s.sem("weighed_ready"), s.sem("added")
        block = s.block()
        STEPS = 2 * NCH

        @block.sync
        def _(sp):
            with sp.Fori(0, E // 2 - 1) as e2:
                for u in range(2):
                    sp.wait_ge(added, 1 + (u + 1) * NCH + e2 * STEPS)
                    for t, key in EXPERT:
                        sp.dma_start(t[:, u], dram[key][e2 * 2 + u + 2]).then_inc(loaded[u], 16)

        @block.tensor
        def _(pe):
            for sem in (down_ready,):
                pe.sem_inc(sem, 1)
            with pe.Fori(0, E // 2) as e2:
                g0 = e2 * STEPS

                def first(i):
                    u, c = i // NCH, i % NCH
                    if c == 0:
                        pe.wait_ge(loaded[u], (e2 + 1) * N_LOAD)
                    pe.wait_ge(gate_ready, 1 + g0 + i)
                    pe.matmul(pg[:], pick[:, u, :], gate_t[:, c * CH:(c + 1) * CH], start=True, stop=True)\
                      .then_inc(pg_ready, 1)
                    for f in range(FB):
                        n = i * FB + f
                        pe.wait_ge(hidden_ready, 1 + g0 * FB + max(n - 2, 0))
                        for k in range(KD):
                            mm = pe.matmul(up[:, n % 3, :], w1[:, u, k, f * P:(f + 1) * P], h[:, k, c * CH:(c + 1) * CH],
                                           start=(k == 0), stop=(k == KD - 1))
                        mm.then_inc(up_ready, 1)

                def second(i):
                    u = i // NCH
                    pe.wait_ge(hidden_ready, 1 + (g0 + i + 1) * FB)
                    pe.wait_ge(weighed_ready, 1 + g0 + max(i - 1, 0))
                    for m in range(KD):
                        for f in range(FB):
                            mm = pe.matmul(down[:, i % 2, m, :], w2[:, u, f, m * P:(m + 1) * P],
                                           hidden[:, i % 2, f, :], start=(f == 0), stop=(f == FB - 1))
                    mm.then_inc(down_ready, 1)

                for i in range(STEPS + 1):
                    if i < STEPS:
                        first(i)
                    if i:
                        second(i - 1)

        @block.scalar
        def _(act):
            for sem in (gate_ready, hidden_ready):
                act.sem_inc(sem, 1)
            with act.Fori(0, E // 2) as e2:
                g0 = e2 * STEPS
                for i in range(STEPS):
                    act.wait_ge(pg_ready, g0 + i + 1)
                    act.wait_ge(weighed_ready, 1 + g0 + max(i - 1, 0))
                    act.activation(gate[:, i % 2, :], pg[:], ACT.Copy).then_inc(gate_ready, 1)
                    for f in range(FB):
                        n = i * FB + f
                        act.wait_ge(up_ready, g0 * FB + n + 1)
                        if f == 0:
                            act.wait_ge(down_ready, 1 + g0 + max(i - 1, 0))
                        act.activation(hidden[:, i % 2, f, :], up[:, n % 3, :], ACT.Gelu_apprx_tanh,
                                       bias=b1[:, i // NCH, f:f + 1]).then_inc(hidden_ready, 1)

        @block.vector
        def _(dve):
            for sem in (added, weighed_ready):
                dve.sem_inc(sem, 1)
            with dve.Fori(0, E // 2) as e2:
                g0 = e2 * STEPS
                for i in range(STEPS):
                    c = i % NCH
                    dve.wait_ge(gate_ready, 1 + g0 + i + 1)
                    dve.wait_ge(down_ready, 1 + g0 + i + 1)
                    for m in range(KD):
                        last = dve.scalar_tensor_tensor(out=weighed[:, i % 2, m, :], in0=down[:, i % 2, m, :],
                                                        scalar=b2[:, i // NCH, m:m + 1],
                                                        in1=gate[:, i % 2, :], op0=ALU.add, op1=ALU.mult)
                    last.then_inc(weighed_ready, 1)
                    dve.wait_ge(weighed_ready, 1 + g0 + i + 1)
                    r = res[:, :, c * CH:(c + 1) * CH]
                    dve.tensor_tensor(r, r, weighed[:, i % 2, :, :], ALU.add).then_inc(added, 1)
            dve.wait_ge(added, 1 + E * NCH)
            dve.tensor_tensor(x[:], x[:], res[:], ALU.add).then_inc(done, 1)


def coupling(core, consts, r, x):
    dram = core.dram
    CYCLES = 3
    with core.scope() as s:
        w1 = s.sb("w1", [P, KD, D])
        w2 = s.sb("w2", [P, KD, P])
        w3 = s.sb("w3", [P, 64])
        w4 = s.sb("w4", [64, 2])
        b12 = s.sb("b12", [P, 3])
        b3 = s.sb("b3", [64, 1])
        g1 = s.sb("g1", [P, KD, P])
        g2 = s.sb("g2", [P, 64])
        gb = s.sb("gb", [P, 2])
        one_each = s.sb("one_each", [P, 4])
        w4b = s.sb("w4b", [64, 2, P])
        mean = s.sb("mean", [P, KD, B])
        gh1 = s.sb("gh1", [P, B])
        gh2 = s.sb("gh2", [64, B])
        gf = s.sb("gf", [P, B])
        k = s.sb("k", [P, 4])
        h1 = s.sb("h1", [P, KD, T])
        h2 = s.sb("h2", [P, T])
        h3 = s.sb("h3", [64, T])
        tf = s.sb("tf", [P, T])
        twist = s.sb("twist", [P, 2, KD, CH])
        psum = s.psum("psum", [P, 8, CH])
        loaded, made, step = s.sem("loaded"), s.sem("made"), s.sem("step")
        g_ready, g_done = s.sem("g_ready"), s.sem("g_done")
        m1, m2, m3, m4 = (s.sem(f"layer{n}_ready") for n in range(1, 5))
        a1, a2, a3, a4 = (s.sem(f"layer{n}_stored") for n in range(1, 5))
        coupled, twisted, moved, done = s.sem("coupled"), s.sem("twisted"), s.sem("moved"), s.sem("done")
        block = s.block()
        LOADS = ((w1, "c_w1"), (w2, "c_w2"), (w3, "c_w3"), (w4, "c_w4"), (b12, "c_b12"), (b3, "c_b3"),
                 (g1, "g_w1"), (g2, "g_w2"), (gb, "g_b"), (one_each, "c_each"))

        @block.sync
        def _(sp):
            for t, key in LOADS:
                sp.dma_start(t[:], dram[key]).then_inc(loaded, 16)

        @block.tensor
        def _(pe):
            pe.wait_ge(loaded, 16 * len(LOADS))
            pe.wait_ge(step, 1)
            for q in range(KD):
                mm = pe.matmul(psum[:, 4, 0:B], g1[:, q, :], mean[:, q, :], start=(q == 0), stop=(q == KD - 1))
            mm.then_inc(g_ready, 1)
            pe.wait_ge(g_done, 1)
            pe.matmul(psum[0:64, 5, 0:B], g2[:], gh1[:], start=True, stop=True).then_inc(g_ready, 1)
            pe.wait_ge(g_done, 2)
            pe.wait_ge(made, 1)
            pe.matmul(psum[:, 6, 0:B], w4b[:, 0, :], gh2[:], start=True, stop=True).then_inc(g_ready, 1)
            pe.wait_ge(g_done, 3)
            for y in range(CYCLES):
                n0 = y * NCH
                for c in range(NCH):
                    if y:
                        pe.wait_ge(moved, n0 - NCH + c + 1)
                    for m in range(KD):
                        if c >= 2 or y:
                            pe.wait_ge(a1, (n0 + c - 2) * KD + m + 1)
                        for q in range(KD):
                            mm = pe.matmul(psum[:, 2 * (c % 2) + m, :], w1[:, q, m * P:(m + 1) * P],
                                           r[:, q, c * CH:(c + 1) * CH], start=(q == 0), stop=(q == KD - 1))
                        mm.then_inc(m1, 1)
                for c in range(NCH):
                    pe.wait_ge(a1, (n0 + c + 1) * KD)
                    if c >= 2 or y:
                        pe.wait_ge(a2, n0 + c - 1)
                    for q in range(KD):
                        mm = pe.matmul(psum[:, 4 + c % 2, :], w2[:, q, :], h1[:, q, c * CH:(c + 1) * CH],
                                       start=(q == 0), stop=(q == KD - 1))
                    mm.then_inc(m2, 1)
                for c in range(NCH):
                    pe.wait_ge(a2, n0 + c + 1)
                    if c or y:
                        pe.wait_ge(a3, n0 + c)
                    pe.matmul(psum[0:64, 6, :], w3[:], h2[:, c * CH:(c + 1) * CH], start=True, stop=True)\
                      .then_inc(m3, 1)
                for c in range(NCH):
                    pe.wait_ge(a3, n0 + c + 1)
                    if c or y:
                        pe.wait_ge(a4, n0 + c)
                    pe.matmul(psum[:, 7, :], w4b[:, 1, :], h3[:, c * CH:(c + 1) * CH], start=True, stop=True)\
                      .then_inc(m4, 1)

        @block.scalar
        def _(act):
            act.wait_ge(loaded, 16 * len(LOADS))
            act.wait_ge(g_ready, 1)
            act.activation(gh1[:], psum[:, 4, 0:B], ACT.Gelu, bias=gb[:, 0:1], scale=1.0 / S).then_inc(g_done, 1)
            act.wait_ge(g_ready, 2)
            act.activation(gh2[:], psum[0:64, 5, 0:B], ACT.Gelu, bias=gb[0:64, 1:2]).then_inc(g_done, 1)
            act.wait_ge(g_ready, 3)
            act.activation(gf[:], psum[:, 6, 0:B], ACT.Sigmoid, bias=one_each[:, 1:2]).then_inc(g_done, 1)
            for y in range(CYCLES):
                n0 = y * NCH
                for c in range(NCH):
                    for m in range(KD):
                        act.wait_ge(m1, (n0 + c) * KD + m + 1)
                        act.activation(h1[:, m, c * CH:(c + 1) * CH], psum[:, 2 * (c % 2) + m, :], ACT.Gelu,
                                       bias=b12[:, m:m + 1]).then_inc(a1, 1)
                for c in range(NCH):
                    act.wait_ge(m2, n0 + c + 1)
                    act.activation(h2[:, c * CH:(c + 1) * CH], psum[:, 4 + c % 2, :], ACT.Gelu,
                                   bias=b12[:, 2:3]).then_inc(a2, 1)
                for c in range(NCH):
                    act.wait_ge(m3, n0 + c + 1)
                    act.activation(h3[:, c * CH:(c + 1) * CH], psum[0:64, 6, :], ACT.Gelu,
                                   bias=b3[:, 0:1]).then_inc(a3, 1)
                for c in range(NCH):
                    act.wait_ge(m4, n0 + c + 1)
                    if y:
                        act.wait_ge(coupled, n0 - NCH + c + 1)
                        act.wait_ge(moved, n0 - NCH + c + 1)
                    act.activation(tf[:, c * CH:(c + 1) * CH], psum[:, 7, :], ACT.Sigmoid,
                                   bias=one_each[:, 0:1]).then_inc(a4, 1)

        @block.vector
        def _(dve):
            count = [1]

            def link(ins):
                count[0] += 1
                ins.then_inc(step, 1)
                dve.wait_ge(step, count[0])

            dve.tensor_reduce(mean[:], r[:].rearrange("p k (b t) -> p k b t", b=B), AX.X, ALU.add).then_inc(step, 1)
            dve.wait_ge(loaded, 16 * len(LOADS))
            dve.tensor_copy(w4b[:], w4[:].unsqueeze(2).to_broadcast([64, 2, P])).then_inc(made, 1)
            dve.wait_ge(g_done, 3)
            rng, sign = one_each[:, 2:3], one_each[:, 3:4]
            link(dve.tensor_scalar(k[:, 0:1], rng, 0.6, sign, ALU.mult, ALU.mult))
            link(dve.tensor_scalar(k[:, 1:3], gf[:], 0.7, -0.5, ALU.mult, ALU.add))
            link(dve.tensor_scalar(k[:, 1:3], k[:, 1:3], rng, 2.0, ALU.mult, ALU.mult))
            link(dve.tensor_scalar(k[:, 1:3], k[:, 1:3], 0.1, sign, ALU.add, ALU.mult))
            for y in range(CYCLES):
                for c in range(NCH):
                    n = y * NCH + c
                    t = tf[:, c * CH:(c + 1) * CH]
                    rc = r[:, :, c * CH:(c + 1) * CH]
                    dve.wait_ge(a4, n + 1)
                    b = c // BCH
                    dve.tensor_scalar(t, t, k[:, 0:1], k[:, 1 + b:2 + b], ALU.mult, ALU.add).then_inc(coupled, 1)
                    dve.wait_ge(coupled, n + 1)
                    dve.tensor_tensor(twist[:, c % 2, :, :], rc, t.unsqueeze(1).to_broadcast([P, KD, CH]),
                                      ALU.mult).then_inc(twisted, 1)
                    dve.wait_ge(twisted, n + 1)
                    dve.tensor_tensor(rc[:, 0, :], rc[:, 0, :], twist[:, c % 2, 1, :], ALU.add)
                    dve.tensor_tensor(rc[:, 1, :], rc[:, 1, :], twist[:, c % 2, 0, :], ALU.subtract).then_inc(moved, 1)
                    dve.wait_ge(moved, n + 1)
            dve.tensor_tensor(x[:], x[:], r[:], ALU.add).then_inc(done, 1)


def cols(a, n):
    return a.reshape(n, P).T


def rows(a):
    return a.reshape(-1, P, a.shape[-1]).transpose(1, 0, 2)


def mamba_arrays(name, inproj, xproj, dtw, outproj, convw, convb, dtb, skip, alog, rank):
    import numpy as np
    x = np.zeros((XD, EI), np.float32)
    x[0:rank] = xproj[0:rank]
    x[BC0:XD] = xproj[rank:].reshape(2, NS, EI).transpose(1, 0, 2).reshape(2 * NS, EI)
    return {
        f"{name}_in": rows(inproj.T), f"{name}_x": rows(x.T), f"{name}_dt": dtw.T,
        f"{name}_out": rows(outproj.T),
        f"{name}_conv": convw.reshape(EB, P, TAPS).transpose(1, 0, 2),
        f"{name}_cols": np.stack([cols(v, EB) for v in (convb, dtb, skip)], 1),
        f"{name}_alog": alog.reshape(EB, P, NS).transpose(1, 0, 2).reshape(P, EB * NS),
    }


def xattn_arrays(name, i, p, transposed, biased):
    import numpy as np
    w = [i[p + k].T if transposed else i[p + k] for k in ("Wq", "Wk", "Wv", "Wo")]
    none = np.zeros(D, np.float32)
    bq, bk, bv, bo = (i[p + k] if biased else none for k in ("bq", "bk", "bv", "bo"))
    return {name + "_w": np.stack([rows(m) for m in w], 1), name + "_bias": np.stack([cols(v, KD) for v in (bq, bk, bo)], 1),
            name + "_v_bias": bv[None]}


def layout(i):
    a = {"xT": rows(i["x"].reshape(T, D).T)}
    for d in ("fwd", "bwd"):
        p = f"L0_attn_{d}_"
        a |= mamba_arrays(d, i[p + "inproj"], i[p + "xproj"], i[p + "dtw"], i[p + "outproj"], i[p + "convw"],
                          i[p + "convb"], i[p + "dtb"], i[p + "Dp"], i[p + "Alog"], 64)
    p = "L1_attn_"
    a |= mamba_arrays("m1", i[p + "in_proj_w"], i[p + "x_proj_w"], i[p + "dt_proj_w"], i[p + "out_proj_w"],
                      i[p + "conv_w"], i[p + "conv_b"], i[p + "dt_proj_b"], i[p + "D"], i[p + "A_log"], 16)
    import numpy as np
    a |= xattn_arrays("x0", i, "L0_xattn_", True, False)
    a |= xattn_arrays("x1", i, "L1_xattn_", False, True)
    a["ctxT"] = rows(i["ctx_1024"].reshape(B * SK, D).T).reshape(P, KD, B, SK)
    a["key_mask"] = i["mask_Bx1x1xS2_ff0"].reshape(1, B, SK)
    f = "L0_ffn_"
    qkv = i[f + "w_qkv"].reshape(D, 3, H, HD)
    a["a0_qk"] = rows(qkv[:, 0:2].reshape(D, 2 * D))
    a["a0_v"] = rows(qkv[:, 2].reshape(D, D))
    a["a0_o"] = rows(i[f + "w_o"])
    tri = np.where(np.arange(P)[None] > np.arange(P)[:, None], np.float32(-1e30), np.float32(0))
    a["tri"] = np.stack([tri, tri.T], 1)
    a["lns"] = np.stack([cols(i[f + n], KD) for n in ("ln1_g", "ln1_b", "ln2_g", "ln2_b")], 1)
    a["moe_gate"] = rows(i[f + "w_gate"])
    a["moe_w1"] = np.stack([rows(w) for w in i[f + "w1"]])
    a["moe_w2"] = np.stack([rows(w) for w in i[f + "w2"]])
    a["moe_pick"] = np.broadcast_to(np.eye(E, dtype=np.float32)[:, :, None], (E, E, P))
    a["moe_b1"] = i[f + "b1"].reshape(E, FB, P).transpose(0, 2, 1)
    a["moe_b2"] = i[f + "b2"].reshape(E, KD, P).transpose(0, 2, 1)
    g = "L1_ffn_"
    a["c_w1"], a["c_w2"], a["c_w3"] = rows(i[g + "cn_w1"]), rows(i[g + "cn_w2"]), i[g + "cn_w3"]
    a["c_w4"] = np.concatenate([i[g + "gc_w3"], i[g + "cn_w4"]], 1)
    a["c_b12"] = np.concatenate([cols(i[g + "cn_b1"], KD), cols(i[g + "cn_b2"], 1)], 1)
    a["c_b3"] = i[g + "cn_b3"][:, None]
    a["g_w1"], a["g_w2"] = rows(i[g + "gc_w1"]), i[g + "gc_w2"]
    gb = np.zeros((P, 2), np.float32)
    gb[:, 0], gb[0:64, 1] = i[g + "gc_b1"], i[g + "gc_b2"]
    a["g_b"] = gb
    each = np.empty((P, 4), np.float32)
    each[:, 0], each[:, 1], each[:, 2] = i[g + "cn_b4"], i[g + "gc_b3"], i[g + "adaptive_range"]
    each[:, 3] = np.where(np.arange(P) < P // 2, 1, -1)
    a["c_each"] = each
    part = np.arange(P)
    a["head_mask"] = (part[:, None] // HD == np.arange(HB)).astype(np.float32)
    a["pair_mask"] = (part[:, None] // SK == np.arange(2)).astype(np.float32)
    query = part[:, None, None] + P * np.arange(QT)[None, :, None]
    a["late"] = np.where(np.arange(SK)[None, None, :] > query, np.float32(-1e30), np.float32(0))
    a["norms"] = np.stack([cols(i[k], KD) for k in
                           ("L0_attn_fwd_norm", "L0_attn_bwd_norm", "L0_attn_normf", "L1_attn_norm_w")], 1)
    return a


def program(nc, dram, out, stages=range(6)):
    with ExitStack() as ctx:
        core = Core(nc, ctx, dram)

        def sb(name, shape, dt=F32):
            return ctx.enter_context(nc.sbuf_tensor(name, shape, dt))

        x = sb("x", [P, KD, T])
        consts = {"ident": sb("ident", [P, P]), "ones": sb("ones", [P, P]), "sel": sb("sel", [96, 32, P], BF16),
                  "eps": sb("eps", [P, 1]), "one": sb("one", [P, 1]), "norms": sb("norms", [P, 4, KD]), "identb": sb("identb", [P, P], BF16),
                  "head_mask": sb("head_mask", [P, HB]),
                  "pair_mask": sb("pair_mask", [P, 2])}
        norms = consts["norms"]
        start(core, x, consts)
        if 0 in stages:
            with core.scope() as s:
                res = s.sb("res", [P, KD, T])
                xn = s.sb("xn", [P, KD, T])
                norm(core, consts, x, res, True)
                for n, (name, flip) in enumerate((("fwd", False), ("bwd", True))):
                    mamba(core, consts, name, xn, res, norms[:, n, :], 64, flip)
                    norm(core, consts, xn, xn, False, weight=norms[:, 2, :], add_to=x)
        if 1 in stages:
            with core.scope() as s:
                h = s.sb("h", [P, KD, T])
                cross_attention(core, consts, "x0", h, x, True)
        if 2 in stages:
            with core.scope() as s:
                lns = s.sb("lns", [P, 4, KD])
                res = s.sb("res", [P, KD, T])
                h = s.sb("h", [P, KD, T])
                gate_t = s.sb("gate_t", [E, T])
                load(core, lns, "lns")
                norm(core, consts, x, res, True)
                self_attention(core, consts, h, res, lns)
                norm(core, consts, res, h, True, weight=lns[:, 2, :], bias=lns[:, 3, :])
                experts(core, consts, h, gate_t, res, x)
        if 3 in stages:
            with core.scope() as s:
                res = s.sb("res", [P, KD, T])
                xn = s.sb("xn", [P, KD, T])
                norm(core, consts, x, res, True)
                mamba(core, consts, "m1", xn, res, norms[:, 3, :], 16, False, x_out=x)
        if 4 in stages:
            with core.scope() as s:
                h = s.sb("h", [P, KD, T])
                cross_attention(core, consts, "x1", h, x, False)
        if 5 in stages:
            with core.scope() as s:
                h = s.sb("h", [P, KD, T])
                norm(core, consts, x, h, True)
                coupling(core, consts, h, x)
        finish(core, x, out)


def load(core, tile, key):
    with core.scope() as s:
        loaded = s.sem("loaded")
        block = s.block()

        @block.sync
        def _(sp):
            sp.dma_start(tile[:], core.dram[key]).then_inc(loaded, 16)
            sp.wait_ge(loaded, 16)


def finish(core, x, out):
    with core.scope() as s:
        stored = s.sem("stored")
        block = s.block()

        @block.sync
        def _(sp):
            sp.dma_start(out, x[:]).then_inc(stored, 16)
            sp.wait_ge(stored, 16)


def kernel(**inputs):
    import numpy as np
    import concourse.bacc as bacc
    from concourse.bass_utils import run_bass_kernel_spmd

    nc = bacc.Bacc("TRN2", target_bir_lowering=False, num_devices=1)
    arrays = {k: np.ascontiguousarray(v) for k, v in layout({k: np.asarray(v) for k, v in inputs.items()}).items()}
    dram = {k: nc.dram_tensor(f"in_{k}", v.shape, mybir.dt.from_np(v.dtype), kind="ExternalInput").ap()
            for k, v in arrays.items()}
    out = nc.dram_tensor("out", (P, KD, T), F32, kind="ExternalOutput").ap()
    program(nc, dram, out)
    r = run_bass_kernel_spmd(nc, [{f"in_{k}": v for k, v in arrays.items()}], core_ids=[0])
    y = r.results[0]["out"]
    return np.ascontiguousarray(y.transpose(1, 0, 2).reshape(D, T).T).reshape(B, S, D)
```
